# Optimizing a Trainium2 kernel written in Bass

```python
import numpy as np
import jax
import jax.numpy as jnp

def _softmax(x, axis=-1):
    return jax.nn.softmax(x, axis=axis)

def _gelu(x):
    return jax.nn.gelu(x, approximate=True)

def _silu(x):
    return jax.nn.silu(x)

def _sigmoid(x):
    return jax.nn.sigmoid(x)

def _layernorm(x, axis=-1, eps=1e-05):
    m = jnp.mean(x, axis=axis, keepdims=True)
    v = jnp.var(x, axis=axis, keepdims=True)
    return (x - m) / jnp.sqrt(v + eps)

def _scatter_add(tgt, idx, src, axis=0):
    return tgt.at[idx].add(src)

def _segment_sum(src, seg, n):
    return jax.ops.segment_sum(src, seg, n)
kernel_name = 'mk_conv_preact_d4_conv_nhwc128_r4_9e9ab4'

def setup_inputs(seed: int=0):
    np.random.seed(seed)
    _w = jnp.asarray

    def _rec_inputs():
        import jax
        import jax.numpy as jnp
        _gk = jax.random.key(seed)
        x = 7.22e-05 + 1 * jax.random.normal(jax.random.fold_in(_gk, 1), (4, 32, 32, 32), jnp.float32)
        return x
    x = _rec_inputs()

    def _L0_conv_setup():
        import jax, jax.numpy as jnp
        import numpy as np
        B, CIN, COUT, H, W = (4, 32, 32, 32, 32)
        K, G, PAD = (3, 4, 1)
        CG = CIN // G

        def _deform_conv(x, offset, w):
            off = offset.reshape(B, G, K * K, 2, H, W)
            ky, kx = np.meshgrid(np.arange(K), np.arange(K), indexing='ij')
            ky = jnp.asarray(ky.reshape(-1), jnp.float32)
            kx = jnp.asarray(kx.reshape(-1), jnp.float32)
            py = off[:, :, :, 0] + (ky - PAD).reshape(1, 1, K * K, 1, 1) + jnp.arange(H, dtype=jnp.float32).reshape(1, 1, 1, H, 1)
            px = off[:, :, :, 1] + (kx - PAD).reshape(1, 1, K * K, 1, 1) + jnp.arange(W, dtype=jnp.float32).reshape(1, 1, 1, 1, W)
            y0 = jnp.floor(py)
            x0 = jnp.floor(px)
            wy1 = py - y0
            wx1 = px - x0
            wy0 = 1.0 - wy1
            wx0 = 1.0 - wx1
            y0i = y0.astype(jnp.int32)
            x0i = x0.astype(jnp.int32)
            xg = x.reshape(B, G, CG, H * W)

            def gather(yi, xi):
                valid = (yi >= 0) & (yi < H) & (xi >= 0) & (xi < W)
                idx = (jnp.clip(yi, 0, H - 1) * W + jnp.clip(xi, 0, W - 1)).reshape(B, G, 1, K * K * H * W)
                v = jnp.take_along_axis(xg, idx, axis=3).reshape(B, G, CG, K * K, H, W)
                return v * valid[:, :, None].astype(x.dtype)
            val = gather(y0i, x0i) * (wy0 * wx0)[:, :, None]
            val = val + gather(y0i, x0i + 1) * (wy0 * wx1)[:, :, None]
            val = val + gather(y0i + 1, x0i) * (wy1 * wx0)[:, :, None]
            val = val + gather(y0i + 1, x0i + 1) * (wy1 * wx1)[:, :, None]
            wg = w.reshape(COUT, G, CG, K * K)
            return jnp.einsum('bgckhw,ogck->bohw', val, wg)
        key = jax.random.key(seed)
        k1, k2, k3, k4 = jax.random.split(key, 4)
        x = jax.random.normal(k1, (B, CIN, H, W), jnp.float32)
        w_off = jax.random.normal(k2, (G * K * K * 2, CIN), jnp.float32) * 0.01
        b_off = jax.random.normal(k3, (G * K * K * 2,), jnp.float32) * 0.1
        w_def = jax.random.normal(k4, (COUT, CIN, K, K), jnp.float32) * (1.0 / np.sqrt(CIN * K * K))
        return {'x': x, 'w_off': w_off, 'b_off': b_off, 'w_def': w_def}
    _L0_conv_all = _L0_conv_setup()
    _L0_conv_in = {k: v for k, v in _L0_conv_all.items() if k in ('w_off', 'b_off', 'w_def')}
    del _L0_conv_all

    def _L1_conv_setup():
        import jax, jax.numpy as jnp
        import numpy as np
        B, H, W, C, NH, K = (4, 56, 56, 32, 4, 7)
        key = jax.random.key(seed)
        ks = jax.random.split(key, 6)
        x = jax.random.normal(ks[0], (B, H, W, C), dtype=jnp.float32)
        w_qkv = jax.random.normal(ks[1], (C, 3 * C), dtype=jnp.float32) * 0.02
        b_qkv = jnp.zeros((3 * C,), dtype=jnp.float32)
        rpb = jax.random.normal(ks[2], (NH, 2 * K - 1, 2 * K - 1), dtype=jnp.float32) * 0.02
        w_proj = jax.random.normal(ks[3], (C, C), dtype=jnp.float32) * 0.02
        b_proj = jnp.zeros((C,), dtype=jnp.float32)
        return {'x': x, 'w_qkv': w_qkv, 'b_qkv': b_qkv, 'rpb': rpb, 'w_proj': w_proj, 'b_proj': b_proj}
    _L1_conv_all = _L1_conv_setup()
    _L1_conv_in = {k: v for k, v in _L1_conv_all.items() if k in ('w_qkv', 'b_qkv', 'rpb', 'w_proj', 'b_proj')}
    del _L1_conv_all

    def _L2_conv_setup():
        import jax, jax.numpy as jnp
        import numpy as np
        import math
        from jax import lax
        DIM = 32
        D_STATE = 16
        D_CONV = 4
        EXPAND = 2
        NSLICES = 16
        D_INNER = EXPAND * DIM
        DT_RANK = math.ceil(DIM / 16)
        B_, H_, W_ = (4, 16, 16)
        L = H_ * W_

        def silu(x):
            return x * jax.nn.sigmoid(x)

        def causal_conv1d(x, w, b):
            l = x.shape[-1]
            xp = jnp.pad(x, ((0, 0), (0, 0), (D_CONV - 1, 0)))
            y = sum((w[None, :, k, None] * xp[:, :, k:k + l] for k in range(D_CONV)))
            return y + b[None, :, None]

        def selective_scan(u, delta, A, B, C):
            bsz, d, l = u.shape
            n = A.shape[1]
            u_t = u.transpose(2, 0, 1)
            d_t = delta.transpose(2, 0, 1)
            B_t = B.transpose(2, 0, 1)
            C_t = C.transpose(2, 0, 1)

            def step(h, inp):
                u_, de_, b_, c_ = inp
                dA = jnp.exp(de_[..., None] * A)
                h = h * dA + (de_ * u_)[..., None] * b_[:, None, :]
                y = jnp.einsum('bdn,bn->bd', h, c_)
                return (h, y)
            h0 = jnp.zeros((bsz, d, n), u.dtype)
            _, ys = lax.scan(step, h0, (u_t, d_t, B_t, C_t))
            return ys.transpose(1, 2, 0)

        def mamba_dir(xz, conv_w, conv_b, x_proj_w, dt_w, dt_b, A_log, Dp):
            x, z = jnp.split(xz, 2, axis=1)
            x = silu(causal_conv1d(x, conv_w, conv_b))
            x_dbl = jnp.einsum('rd,bdl->brl', x_proj_w, x)
            dt_raw = x_dbl[:, :DT_RANK]
            Bm = x_dbl[:, DT_RANK:DT_RANK + D_STATE]
            Cm = x_dbl[:, DT_RANK + D_STATE:]
            delta = jax.nn.softplus(jnp.einsum('dr,brl->bdl', dt_w, dt_raw) + dt_b[None, :, None])
            A = -jnp.exp(A_log)
            y = selective_scan(x, delta, A, Bm, Cm)
            y = y + Dp[None, :, None] * x
            return y * silu(z)
        key = jax.random.key(seed)
        ks = iter(jax.random.split(key, 40))

        def rn(shape, scale=0.02):
            return jax.random.normal(next(ks), shape, dtype=jnp.float32) * scale
        inp = {'x_in': jax.random.normal(next(ks), (B_, H_, W_, DIM), dtype=jnp.float32)}
        inp['in_proj_w'] = rn((2 * D_INNER, DIM))
        for suf in ['', '_b', '_s']:
            inp['conv_w' + suf] = rn((D_INNER, D_CONV), 0.1)
            inp['conv_b' + suf] = rn((D_INNER,), 0.1)
            inp['x_proj_w' + suf] = rn((DT_RANK + 2 * D_STATE, D_INNER))
            inp['dt_proj_w' + suf] = rn((D_INNER, DT_RANK), 0.1)
            inp['dt_proj_b' + suf] = rn((D_INNER,), 0.1)
            inp['A_log' + suf] = jnp.log(jnp.tile(jnp.arange(1, D_STATE + 1, dtype=jnp.float32), (D_INNER, 1)))
            inp['D' + suf] = jnp.ones((D_INNER,), jnp.float32)
        inp['out_proj_w'] = rn((DIM, D_INNER))
        return inp
    _L2_conv_all = _L2_conv_setup()
    _L2_conv_in = {k: v for k, v in _L2_conv_all.items() if k in ('in_proj_w', 'conv_w', 'conv_b', 'x_proj_w', 'dt_proj_w', 'dt_proj_b', 'A_log', 'D', 'conv_w_b', 'conv_b_b', 'x_proj_w_b', 'dt_proj_w_b', 'dt_proj_b_b', 'A_log_b', 'D_b', 'conv_w_s', 'conv_b_s', 'x_proj_w_s', 'dt_proj_w_s', 'dt_proj_b_s', 'A_log_s', 'D_s', 'out_proj_w')}
    del _L2_conv_all

    def _L3_conv_setup():
        import jax, jax.numpy as jnp
        import numpy as np
        from jax import lax
        B, H, W_DIM, C = (16, 16, 16, 32)
        KH, KW = (3, 3)
        key = jax.random.key(seed)
        k1, k2 = jax.random.split(key)
        x = jax.random.normal(k1, (B, H, W_DIM, C), dtype=jnp.float32)
        W = jax.random.normal(k2, (KH, KW, C, 2 * C), dtype=jnp.float32) * 0.05
        b = jnp.zeros((2 * C,), dtype=jnp.float32)
        return {'x': x, 'W': W, 'b': b}
    _L3_conv_all = _L3_conv_setup()
    _L3_conv_in = {k: v for k, v in _L3_conv_all.items() if k in ('W', 'b')}
    del _L3_conv_all
    return {'x': x, 'L0_conv_w_off': _L0_conv_in['w_off'], 'L0_conv_b_off': _L0_conv_in['b_off'], 'L0_conv_w_def': _L0_conv_in['w_def'], 'L1_conv_w_qkv': _L1_conv_in['w_qkv'], 'L1_conv_b_qkv': _L1_conv_in['b_qkv'], 'L1_conv_rpb': _L1_conv_in['rpb'], 'L1_conv_w_proj': _L1_conv_in['w_proj'], 'L1_conv_b_proj': _L1_conv_in['b_proj'], 'L2_conv_in_proj_w': _L2_conv_in['in_proj_w'], 'L2_conv_conv_w': _L2_conv_in['conv_w'], 'L2_conv_conv_b': _L2_conv_in['conv_b'], 'L2_conv_x_proj_w': _L2_conv_in['x_proj_w'], 'L2_conv_dt_proj_w': _L2_conv_in['dt_proj_w'], 'L2_conv_dt_proj_b': _L2_conv_in['dt_proj_b'], 'L2_conv_A_log': _L2_conv_in['A_log'], 'L2_conv_D': _L2_conv_in['D'], 'L2_conv_conv_w_b': _L2_conv_in['conv_w_b'], 'L2_conv_conv_b_b': _L2_conv_in['conv_b_b'], 'L2_conv_x_proj_w_b': _L2_conv_in['x_proj_w_b'], 'L2_conv_dt_proj_w_b': _L2_conv_in['dt_proj_w_b'], 'L2_conv_dt_proj_b_b': _L2_conv_in['dt_proj_b_b'], 'L2_conv_A_log_b': _L2_conv_in['A_log_b'], 'L2_conv_D_b': _L2_conv_in['D_b'], 'L2_conv_conv_w_s': _L2_conv_in['conv_w_s'], 'L2_conv_conv_b_s': _L2_conv_in['conv_b_s'], 'L2_conv_x_proj_w_s': _L2_conv_in['x_proj_w_s'], 'L2_conv_dt_proj_w_s': _L2_conv_in['dt_proj_w_s'], 'L2_conv_dt_proj_b_s': _L2_conv_in['dt_proj_b_s'], 'L2_conv_A_log_s': _L2_conv_in['A_log_s'], 'L2_conv_D_s': _L2_conv_in['D_s'], 'L2_conv_out_proj_w': _L2_conv_in['out_proj_w'], 'L3_conv_W': _L3_conv_in['W'], 'L3_conv_b': _L3_conv_in['b']}

def reference(x, L0_conv_w_off, L0_conv_b_off, L0_conv_w_def, L1_conv_w_qkv, L1_conv_b_qkv, L1_conv_rpb, L1_conv_w_proj, L1_conv_b_proj, L2_conv_in_proj_w, L2_conv_conv_w, L2_conv_conv_b, L2_conv_x_proj_w, L2_conv_dt_proj_w, L2_conv_dt_proj_b, L2_conv_A_log, L2_conv_D, L2_conv_conv_w_b, L2_conv_conv_b_b, L2_conv_x_proj_w_b, L2_conv_dt_proj_w_b, L2_conv_dt_proj_b_b, L2_conv_A_log_b, L2_conv_D_b, L2_conv_conv_w_s, L2_conv_conv_b_s, L2_conv_x_proj_w_s, L2_conv_dt_proj_w_s, L2_conv_dt_proj_b_s, L2_conv_A_log_s, L2_conv_D_s, L2_conv_out_proj_w, L3_conv_W, L3_conv_b):
    import jax
    import jax.numpy as jnp

    def _L0_conv_ref(x, w_off, b_off, w_def):
        import jax, jax.numpy as jnp
        import numpy as np
        B, CIN, COUT, H, W = (4, 32, 32, 32, 32)
        K, G, PAD = (3, 4, 1)
        CG = CIN // G

        def _deform_conv(x, offset, w):
            off = offset.reshape(B, G, K * K, 2, H, W)
            ky, kx = np.meshgrid(np.arange(K), np.arange(K), indexing='ij')
            ky = jnp.asarray(ky.reshape(-1), jnp.float32)
            kx = jnp.asarray(kx.reshape(-1), jnp.float32)
            py = off[:, :, :, 0] + (ky - PAD).reshape(1, 1, K * K, 1, 1) + jnp.arange(H, dtype=jnp.float32).reshape(1, 1, 1, H, 1)
            px = off[:, :, :, 1] + (kx - PAD).reshape(1, 1, K * K, 1, 1) + jnp.arange(W, dtype=jnp.float32).reshape(1, 1, 1, 1, W)
            y0 = jnp.floor(py)
            x0 = jnp.floor(px)
            wy1 = py - y0
            wx1 = px - x0
            wy0 = 1.0 - wy1
            wx0 = 1.0 - wx1
            y0i = y0.astype(jnp.int32)
            x0i = x0.astype(jnp.int32)
            xg = x.reshape(B, G, CG, H * W)

            def gather(yi, xi):
                valid = (yi >= 0) & (yi < H) & (xi >= 0) & (xi < W)
                idx = (jnp.clip(yi, 0, H - 1) * W + jnp.clip(xi, 0, W - 1)).reshape(B, G, 1, K * K * H * W)
                v = jnp.take_along_axis(xg, idx, axis=3).reshape(B, G, CG, K * K, H, W)
                return v * valid[:, :, None].astype(x.dtype)
            val = gather(y0i, x0i) * (wy0 * wx0)[:, :, None]
            val = val + gather(y0i, x0i + 1) * (wy0 * wx1)[:, :, None]
            val = val + gather(y0i + 1, x0i) * (wy1 * wx0)[:, :, None]
            val = val + gather(y0i + 1, x0i + 1) * (wy1 * wx1)[:, :, None]
            wg = w.reshape(COUT, G, CG, K * K)
            return jnp.einsum('bgckhw,ogck->bohw', val, wg)
        offset = jnp.einsum('bchw,oc->bohw', x, w_off) + b_off[None, :, None, None]
        return jax.nn.relu(_deform_conv(x, offset, w_def))

    def _L1_conv_ref(x, w_qkv, b_qkv, rpb, w_proj, b_proj):
        import jax, jax.numpy as jnp
        import numpy as np
        B, H, W, C, NH, K = (4, 56, 56, 32, 4, 7)
        B_, H_, W_, C_ = x.shape
        nh = rpb.shape[0]
        k = (rpb.shape[1] + 1) // 2
        hd = C_ // nh
        nb = k // 2
        scale = hd ** (-0.5)
        qkv = (x @ w_qkv + b_qkv).reshape(B_, H_, W_, 3, nh, hd)
        q = qkv[:, :, :, 0].transpose(0, 3, 1, 2, 4) * scale
        kk = qkv[:, :, :, 1].transpose(0, 3, 1, 2, 4)
        v = qkv[:, :, :, 2].transpose(0, 3, 1, 2, 4)
        si = jnp.clip(jnp.arange(H_) - nb, 0, H_ - k)
        sj = jnp.clip(jnp.arange(W_) - nb, 0, W_ - k)
        idx_i = si[:, None] + jnp.arange(k)
        idx_j = sj[:, None] + jnp.arange(k)
        k_win = kk[:, :, idx_i][:, :, :, :, idx_j]
        v_win = v[:, :, idx_i][:, :, :, :, idx_j]
        rel_i = idx_i - jnp.arange(H_)[:, None] + (k - 1)
        rel_j = idx_j - jnp.arange(W_)[:, None] + (k - 1)
        bias = rpb[:, rel_i][:, :, :, rel_j]
        bias = bias.transpose(0, 1, 3, 2, 4)
        attn = jnp.einsum('bnijd,bnipjqd->bnijpq', q, k_win) + bias[None]
        attn = jax.nn.softmax(attn.reshape(B_, nh, H_, W_, k * k), axis=-1)
        attn = attn.reshape(B_, nh, H_, W_, k, k)
        out = jnp.einsum('bnijpq,bnipjqd->bnijd', attn, v_win)
        out = out.transpose(0, 2, 3, 1, 4).reshape(B_, H_, W_, C_)
        return out @ w_proj + b_proj

    def _L2_conv_ref(x_in, in_proj_w, conv_w, conv_b, x_proj_w, dt_proj_w, dt_proj_b, A_log, D, conv_w_b, conv_b_b, x_proj_w_b, dt_proj_w_b, dt_proj_b_b, A_log_b, D_b, conv_w_s, conv_b_s, x_proj_w_s, dt_proj_w_s, dt_proj_b_s, A_log_s, D_s, out_proj_w):
        import jax, jax.numpy as jnp
        import numpy as np
        import math
        from jax import lax
        DIM = 32
        D_STATE = 16
        D_CONV = 4
        EXPAND = 2
        NSLICES = 16
        D_INNER = EXPAND * DIM
        DT_RANK = math.ceil(DIM / 16)
        B_, H_, W_ = (4, 16, 16)
        L = H_ * W_

        def silu(x):
            return x * jax.nn.sigmoid(x)

        def causal_conv1d(x, w, b):
            l = x.shape[-1]
            xp = jnp.pad(x, ((0, 0), (0, 0), (D_CONV - 1, 0)))
            y = sum((w[None, :, k, None] * xp[:, :, k:k + l] for k in range(D_CONV)))
            return y + b[None, :, None]

        def selective_scan(u, delta, A, B, C):
            bsz, d, l = u.shape
            n = A.shape[1]
            u_t = u.transpose(2, 0, 1)
            d_t = delta.transpose(2, 0, 1)
            B_t = B.transpose(2, 0, 1)
            C_t = C.transpose(2, 0, 1)

            def step(h, inp):
                u_, de_, b_, c_ = inp
                dA = jnp.exp(de_[..., None] * A)
                h = h * dA + (de_ * u_)[..., None] * b_[:, None, :]
                y = jnp.einsum('bdn,bn->bd', h, c_)
                return (h, y)
            h0 = jnp.zeros((bsz, d, n), u.dtype)
            _, ys = lax.scan(step, h0, (u_t, d_t, B_t, C_t))
            return ys.transpose(1, 2, 0)

        def mamba_dir(xz, conv_w, conv_b, x_proj_w, dt_w, dt_b, A_log, Dp):
            x, z = jnp.split(xz, 2, axis=1)
            x = silu(causal_conv1d(x, conv_w, conv_b))
            x_dbl = jnp.einsum('rd,bdl->brl', x_proj_w, x)
            dt_raw = x_dbl[:, :DT_RANK]
            Bm = x_dbl[:, DT_RANK:DT_RANK + D_STATE]
            Cm = x_dbl[:, DT_RANK + D_STATE:]
            delta = jax.nn.softplus(jnp.einsum('dr,brl->bdl', dt_w, dt_raw) + dt_b[None, :, None])
            A = -jnp.exp(A_log)
            y = selective_scan(x, delta, A, Bm, Cm)
            y = y + Dp[None, :, None] * x
            return y * silu(z)
        b, h, w, c = x_in.shape
        l = h * w
        x = x_in.reshape(b, l, c)
        xz = jnp.einsum('pd,bld->bpl', in_proj_w, x)
        y_f = mamba_dir(xz, conv_w, conv_b, x_proj_w, dt_proj_w, dt_proj_b, A_log, D)
        y_b = jnp.flip(mamba_dir(jnp.flip(xz, -1), conv_w_b, conv_b_b, x_proj_w_b, dt_proj_w_b, dt_proj_b_b, A_log_b, D_b), -1)
        m = l // NSLICES
        xz_s = xz.reshape(b, 2 * D_INNER, NSLICES, m).swapaxes(-1, -2).reshape(b, 2 * D_INNER, l)
        y_s = mamba_dir(xz_s, conv_w_s, conv_b_s, x_proj_w_s, dt_proj_w_s, dt_proj_b_s, A_log_s, D_s)
        y_s = y_s.reshape(b, D_INNER, m, NSLICES).swapaxes(-1, -2).reshape(b, D_INNER, l)
        y = y_f + y_b + y_s
        out = jnp.einsum('od,bdl->blo', out_proj_w, y)
        return out.reshape(b, h, w, c)

    def _L3_conv_ref(x, W, b):
        import jax, jax.numpy as jnp
        import numpy as np
        from jax import lax
        B, H, W_DIM, C = (16, 16, 16, 32)
        KH, KW = (3, 3)
        bsz, h, w, c = x.shape
        offsets = lax.conv_general_dilated(x, W, window_strides=(1, 1), padding='SAME', dimension_numbers=('NHWC', 'HWIO', 'NHWC')) + b
        off = offsets.transpose(0, 3, 1, 2).reshape(-1, h, w, 2)
        xf = x.transpose(0, 3, 1, 2).reshape(-1, h, w)
        bc = xf.shape[0]
        grid = jnp.stack(jnp.meshgrid(jnp.arange(h), jnp.arange(w), indexing='ij'), axis=-1)
        grid = grid.reshape(-1, 2).astype(jnp.float32)
        coords = off.reshape(bc, -1, 2) + grid[None]
        c0 = jnp.clip(coords[..., 0], 0.0, jnp.float32(w - 1))
        c1 = jnp.clip(coords[..., 1], 0.0, jnp.float32(h - 1))
        lt0 = jnp.floor(c0).astype(jnp.int32)
        lt1 = jnp.floor(c1).astype(jnp.int32)
        rb0 = jnp.ceil(c0).astype(jnp.int32)
        rb1 = jnp.ceil(c1).astype(jnp.int32)
        flat = xf.reshape(bc, h * w)

        def gather(i0, i1):
            return jnp.take_along_axis(flat, i0 * w + i1, axis=1)
        vals_lt = gather(lt0, lt1)
        vals_rb = gather(rb0, rb1)
        vals_lb = gather(lt0, rb1)
        vals_rt = gather(rb0, lt1)
        f0 = c0 - lt0.astype(jnp.float32)
        f1 = c1 - lt1.astype(jnp.float32)
        vals_t = vals_lt + (vals_rt - vals_lt) * f0
        vals_b = vals_lb + (vals_rb - vals_lb) * f0
        mapped = vals_t + (vals_b - vals_t) * f1
        return mapped.reshape(bsz, c, h, w).transpose(0, 2, 3, 1)

    def _gn(v, G=32, eps=1e-05):
        B_, H_, W_, C_ = v.shape
        g = v.reshape(B_, H_, W_, G, C_ // G)
        m = jnp.mean(g, axis=(1, 2, 4), keepdims=True)
        s = jnp.var(g, axis=(1, 2, 4), keepdims=True)
        return ((g - m) / jnp.sqrt(s + eps)).reshape(v.shape)

    def _ln_c(v, eps=1e-06):
        m = jnp.mean(v, axis=-1, keepdims=True)
        s = jnp.var(v, axis=-1, keepdims=True)
        return (v - m) / jnp.sqrt(s + eps)

    def _ln_t(v, eps=1e-05):
        m = jnp.mean(v, axis=-1, keepdims=True)
        s = jnp.var(v, axis=-1, keepdims=True)
        return (v - m) / jnp.sqrt(s + eps)

    def _to_tokens(v):
        B_, H_, W_, C_ = v.shape
        return v.reshape(B_, H_ * W_, C_)

    def _from_tokens(t, like):
        return t.reshape(like.shape)
    x = x + _L0_conv_ref(_gn(x), L0_conv_w_off, L0_conv_b_off, L0_conv_w_def)
    x = x + _L1_conv_ref(_gn(x), L1_conv_w_qkv, L1_conv_b_qkv, L1_conv_rpb, L1_conv_w_proj, L1_conv_b_proj)
    x = x + _L2_conv_ref(_gn(x), L2_conv_in_proj_w, L2_conv_conv_w, L2_conv_conv_b, L2_conv_x_proj_w, L2_conv_dt_proj_w, L2_conv_dt_proj_b, L2_conv_A_log, L2_conv_D, L2_conv_conv_w_b, L2_conv_conv_b_b, L2_conv_x_proj_w_b, L2_conv_dt_proj_w_b, L2_conv_dt_proj_b_b, L2_conv_A_log_b, L2_conv_D_b, L2_conv_conv_w_s, L2_conv_conv_b_s, L2_conv_x_proj_w_s, L2_conv_dt_proj_w_s, L2_conv_dt_proj_b_s, L2_conv_A_log_s, L2_conv_D_s, L2_conv_out_proj_w)
    x = x + _L3_conv_ref(_gn(x), L3_conv_W, L3_conv_b)
    return x

_drawn_inputs = setup_inputs


def setup_inputs(seed=0):
    import zlib

    import numpy as np

    out = dict(_drawn_inputs(seed))
    spreads = {'L1_conv_b_qkv': (0.0, 0.8),
     'L1_conv_b_proj': (0.0, 0.8),
     'L2_conv_D': (1.0, 0.6),
     'L2_conv_D_b': (1.0, 0.6),
     'L2_conv_D_s': (1.0, 0.6),
     'L3_conv_b': (0.0, 2.0)}
    factors = {'L1_conv_w_qkv': 8.0,
     'L1_conv_rpb': 8.0,
     'L1_conv_w_proj': 8.0,
     'L2_conv_in_proj_w': 8.0,
     'L2_conv_conv_w': 8.0,
     'L2_conv_conv_b': 8.0,
     'L2_conv_x_proj_w': 8.0,
     'L2_conv_dt_proj_w': 8.0,
     'L2_conv_dt_proj_b': 8.0,
     'L2_conv_A_log': 8.0,
     'L2_conv_conv_w_b': 8.0,
     'L2_conv_conv_b_b': 8.0,
     'L2_conv_x_proj_w_b': 8.0,
     'L2_conv_dt_proj_w_b': 8.0,
     'L2_conv_dt_proj_b_b': 8.0,
     'L2_conv_A_log_b': 8.0,
     'L2_conv_conv_w_s': 8.0,
     'L2_conv_conv_b_s': 8.0,
     'L2_conv_x_proj_w_s': 8.0,
     'L2_conv_dt_proj_w_s': 8.0,
     'L2_conv_dt_proj_b_s': 8.0,
     'L2_conv_A_log_s': 8.0,
     'L2_conv_out_proj_w': 8.0}
    for name, (base, spread) in spreads.items():
        noise = np.random.default_rng([zlib.crc32(name.encode()), seed]).standard_normal(out[name].shape)
        drawn = base * np.exp(spread * noise) if base else spread * noise
        out[name] = jnp.asarray(drawn.astype(out[name].dtype))
    for name, factor in factors.items():
        out[name] = (out[name] * factor).astype(out[name].dtype)
    return out
```

```python
from contextlib import ExitStack

import concourse.bass as bass
from concourse import mybir
from concourse.alu_op_type import AluOpType as ALU

ACT = mybir.ActivationFunctionType
F32 = mybir.dt.float32
BF16 = mybir.dt.bfloat16
I32 = mybir.dt.int32
U16 = mybir.dt.uint16
AX = mybir.AxisListType

P = 128
B = 4
C = 32
T = C * C
HALF = 512
BIG = 1e30

G, CG, TAPS = 4, 8, 9
PAD = 2
W1 = C + 2 * PAD

NCHK = 3
KQ = 2 * TAPS // NCHK
CHK = KQ * B * G

NH, HD, WIN = 4, 8, 7
QROWS = 4
NBLK = C // QROWS
EDGE, INNER = 2 * P, 3 * P
NSB = 4
BIASW = EDGE + INNER + EDGE

DI, NS, KC, RANK = 64, 16, 4, 2
DIRS, PAIRS = 3, 2
DP = DIRS * PAIRS
NPAR = KC + 3 + NS
SLICES = 16

CGRP, CPER = 4, 8


def key_tiles(i):
    lo, hi = max(i - 1, 0), min(i + 1, NBLK - 1)
    off = 0 if i == 0 else (EDGE if i < NBLK - 1 else EDGE + INNER)
    return list(range(lo, hi + 1)), off


LOOPED = {
    "tensor": "sc ptp pv b_rep c_rep y_acc crep rowmix gath far_d far_q far_out",
    "vector": "qz neg pt vz rinv dbu y_read scan nhat prod far_off far_pos far_st far_prod",
    "scalar": "ot_b pe c_copied da abs far_hat far_abs",
    "gpsimd": "pn hc stat",
}


def above(n):
    return n + 1


class Tally:

    def __init__(self, eng, sem):
        self.eng, self.sem, self.n = eng, sem, 0

    def __call__(self, ins):
        self.n += 1
        ins.then_inc(self.sem, 1)
        return self.n

    def sync(self, n=None):
        self.eng.wait_ge(self.sem, self.n if n is None else n)


def build(nc, d, out):
    with ExitStack() as ctx:
        def sb(name, shape, dt=F32):
            return ctx.enter_context(nc.sbuf_tensor(name, shape, dt))

        def sem(name):
            return ctx.enter_context(nc.semaphore(name))

        ps = ctx.enter_context(nc.psum_tensor("ps", [P, 8, HALF], F32))

        def bank2(i):
            return ps[:, i:i + 2, :].rearrange("p a n -> p (a n)")

        x0 = sb("x0", [P, T])
        x1 = sb("x1", [P, T])
        x1t = sb("x1t", [P, T])
        x2t = sb("x2t", [P, T])
        x3t = sb("x3t", [P, T])
        xn = sb("xn", [P, T])
        ident = sb("ident", [P, P])
        ones_b = sb("ones_b", [P, P])
        qmask = sb("qmask", [P, B * NH])
        ycol = sb("ycol", [P, 1])
        nycol = sb("nycol", [P, 1])
        gate = sb("gate", [P, NSB])
        small = sb("small", [P, 64])
        w_attn = sb("w_attn", [P, 4, P])
        b_attn = sb("b_attn", [P, 4])
        bv_row = sb("bv_row", [C, 1])
        w_in = sb("w_in", [P, 4, P])
        w_xp = sb("w_xp", [P, DIRS, 2, 3, 2, NS])
        w_xd = sb("w_xd", [P, DIRS, 2, RANK])
        xp_raw = sb("xp_raw", [P, DIRS, RANK + 2 * NS])
        w_dt = sb("w_dt", [2 * RANK, DIRS, P])
        w_out = sb("w_out", [P, PAIRS, P])
        par = sb("par", [P, DIRS, NPAR])
        a_col = sb("a_col", [P, DIRS, PAIRS, NS])
        d_col = sb("d_col", [P, DIRS, PAIRS])
        b_conv = sb("b_conv", [P, 2])
        bmask = sb("bmask", [P, B])
        bsel = sb("bsel", [P, B, B])
        far = sb("far", [P, 4])
        is_far = sb("is_far", [1, 1], I32)

        ARENA = 40300
        arena = sb("arena", [P, ARENA])

        class Carve:
            def __init__(self):
                self.at = 0

            def __call__(self, *free, dt=F32, rows=P):
                n = 1
                for f in free:
                    n *= f
                words = n if dt == F32 else (n + 1) // 2
                v = arena[0:rows, self.at:self.at + words]
                self.at += words
                assert self.at <= ARENA, self.at
                if dt != F32:
                    v = v.bitcast(dt)
                if len(free) > 1:
                    names = "abcdef"[:len(free)]
                    v = v.rearrange(f"p ({' '.join(names)}) -> p {' '.join(names)}",
                                    **dict(zip(names, free)))
                return v

        cv = Carve()
        w_off = cv(TAPS, 2, B, G, CG)
        w_off_raw = cv(TAPS * 2, G)
        w_def = cv(TAPS, P)
        b_off = cv(TAPS * 2)
        b_off_neg = cv(TAPS * 2)
        stat1 = cv(3, C)
        img = cv(9, W1, W1)
        hats = cv(2, 4, T)
        term = cv(2, 3, T)
        tmp_v = cv(4, T)
        tmp_p = cv(2, T)
        xc, sq = tmp_v[:, 0], tmp_v[:, 1]
        absd = cv(NCHK, T, rows=CHK)
        b_chk = cv(NCHK, rows=CHK)
        cv = Carve()
        cv.at = TAPS * 2 * P + TAPS * 2 * G + TAPS * P + 2 * TAPS * 2 + 3 * C + 9 * W1 * W1
        far_grid = cv(2, T)
        far_hat = cv(2, T)
        far_prod = cv(T)
        far_img = cv(B, CG, C)
        far_w = cv(CG, TAPS, C)
        far_b = cv(2 * TAPS)
        far_tap = cv(2 * TAPS)
        far_off = cv(2, G, C)
        far_xst = cv(G, C)
        far_wst = cv(B, C)
        IMG_0, IMG_XM, IMG_XP, IMG_YM, IMG_YP, IMG_MM, IMG_MP, IMG_PM, IMG_PP = range(9)
        cv = Carve()
        kt = cv(T)
        qt = cv(T)
        vt = cv(NBLK, P)
        vz = cv(NBLK, NH, C)
        qz = cv(2, T)
        bias = cv(NH, BIASW)

        sc = cv(NSB, INNER)
        pexp = cv(NSB, INNER)
        pn = cv(NSB, INNER)
        pt = cv(NSB, INNER)
        nmax = cv(NSB)
        sum_row = cv(NSB)
        rinv = cv(NSB)
        ot_b = cv(B, T, rows=C)
        ot = cv(T)
        cv = Carve()
        zs = cv(PAIRS, T)
        u = cv(DIRS, PAIRS, T)
        delta = cv(DP, T)
        du = cv(DP, T)
        split_b = cv(DP, T, dt=BF16, rows=96)
        split_c = cv(DP, T, dt=BF16, rows=96)
        sel = cv(NS, P, dt=BF16, rows=96)
        da = cv(2, T)
        dbu = cv(2, T)
        hs = cv(2, T)
        c_sb = cv(2, T)
        hc = cv(2, T)
        xs = cv(2, T + KC - 1)
        dt_raw = x0[0:2 * RANK, :]
        acc_c = da
        res96 = dbu
        mid96 = hs
        sp = [c_sb, hc]
        cv = Carve()
        WP = C + 2
        w_conv = cv(9, 2, P)
        xpad = cv(WP, WP)
        xrow = cv(C, C)
        grid = cv(2, T)
        coord = cv(2, T)
        chi = cv(2, T, dt=BF16)
        cmid = cv(2, T, dt=BF16)
        clo = cv(2, T, dt=BF16)
        crow = cv(CPER, T, dt=BF16, rows=96)
        selc = cv(CGRP, 2, P, dt=BF16, rows=96)
        chsel = cv(B, 2 * C - 1)
        xstat = cv(2, B, C)
        ostat = cv(2, B, C)
        NU = 2
        ahat = cv(NU, 2, HALF)
        nhat = cv(NU, 2, HALF)
        prod = cv(NU, HALF)
        zero_w = cv(P)
        y4 = cv(T)
        yout = cv(T)

        xn_rows = nc.dram_tensor("xn_rows", (P, C, C), F32, kind="Internal").ap()
        rpb_pad = nc.dram_tensor("rpb_pad", (NH, 13, C, C), F32, kind="Internal").ap()

        s_ld = {k: sem("ld_" + k) for k in
                ("x", "off", "def", "attn", "mamba", "conv", "pad", "rpb", "bias", "sel", "b4",
                 "ot", "rows")}
        s_zero = sem("weights_zeroed")
        v_own, a_own, g_own = sem("vector_own"), sem("scalar_own"), sem("gpsimd_own")
        s = {}

        def S(name):
            if name not in s:
                s[name] = sem(name)
            return s[name]

        OFF_LOADS = 16 * (B * (1 + G) + 3)
        FAR_LOADS = 16 * (G + G + 2 + 1 + B * G)
        ATTN_LOADS = 16 * (B * 7 + 2)
        MAMBA_LOADS = 16 * (4 * 3 + 6 + B + 1)
        NT = 2 * CGRP
        units = [(n, i) for n in range(NH) for i in range(NBLK)]
        NUNIT = len(units)
        block = ctx.enter_context(nc.Block())

        @block.sync
        def _(eng):
            eng.dma_start(x0[:], d["x"]).then_inc(s_ld["x"], 16)
            eng.dma_start(ones_b[:], d["c_ones"]).then_inc(s_ld["x"], 16)
            eng.dma_start(ident[:], d["c_ident"]).then_inc(s_ld["x"], 16)
            for b in range(B):
                q = slice(C * b, C * b + C)
                eng.dma_start(w_off_raw[q], d["woff"].rearrange("c (k g) -> c k g", g=G)).then_inc(s_ld["off"], 16)
                for g in range(G):
                    r = C * b + CG * g
                    eng.dma_start(b_off[r:r + CG], d["boff"][g:g + 1, :].to_broadcast([CG, 2 * TAPS])).then_inc(s_ld["off"], 16)
            eng.dma_start(b_chk, d["bchk"]).then_inc(s_ld["off"], 16)
            eng.dma_start(bmask[:], d["c_bmask"]).then_inc(s_ld["off"], 16)
            eng.dma_start(bsel[:], d["c_bsel"]).then_inc(s_ld["off"], 16)
            eng.wait_ge(s_zero, 1)
            for b in range(B):
                q = slice(C * b, C * b + C)
                eng.dma_start(w_def[q, :, q], d["wdef"]).then_inc(s_ld["def"], 16)
            eng.dma_start(rpb_pad.rearrange("n r j k -> (n r) (j k)"), d["c_far"]).then_inc(s_ld["pad"], 16)
            eng.wait_ge(s_ld["pad"], 16)
            lo, hi = WIN // 2, C - WIN // 2 - 1
            for n in range(NH):
                flat = rpb_pad[n].rearrange("r j k -> r (j k)")
                for j in list(range(lo)) + list(range(hi + 1, C)):
                    k0 = min(max(j - lo, 0), C - WIN)
                    eng.dma_start(rpb_pad[n, :, j, k0:k0 + WIN],
                                  d["rpb"][n, :, k0 - j + WIN - 1:k0 - j + 2 * WIN - 1]).then_inc(s_ld["rpb"], 16)
                dst = flat[:, lo * C:lo * C + (hi - lo + 1) * (C + 1)]
                dst = dst.rearrange("r (j k) -> r j k", k=C + 1)[:, :, 0:WIN]
                src = d["rpb"][n, :, WIN - 1 - lo:WIN - 1 - lo + WIN].unsqueeze(1).to_broadcast([13, hi - lo + 1, WIN])
                eng.dma_start(dst, src).then_inc(s_ld["rpb"], 16)
            for b in range(B):
                q = slice(C * b, C * b + C)
                for m in range(3):
                    eng.dma_start(w_attn[q, m, q], d["wqkv"][:, C * m:C * m + C]).then_inc(s_ld["attn"], 16)
                    if m < 2:
                        eng.dma_start(b_attn[q, m:m + 1], d["bqkv"][C * m:C * m + C].rearrange("(c a) -> c a", a=1)).then_inc(s_ld["attn"], 16)
                eng.dma_start(w_attn[q, 3, q], d["wproj"]).then_inc(s_ld["attn"], 16)
                eng.dma_start(b_attn[q, 3:4], d["bproj"].rearrange("(c a) -> c a", a=1)).then_inc(s_ld["attn"], 16)
            eng.dma_start(bv_row[:], d["bqkv"][2 * C:3 * C].rearrange("(c a) -> c a", a=1)).then_inc(s_ld["attn"], 16)
            eng.dma_start(qmask[:], d["c_qmask"]).then_inc(s_ld["attn"], 16)
            for p in range(PAIRS):
                for j in range(2):
                    b = 2 * p + j
                    q = slice(C * b, C * b + C)
                    r = slice(DI * j, DI * j + DI)
                    for part in range(2):
                        eng.dma_start(w_in[q, 2 * part + p, r], d["win"][:, DI * part:DI * part + DI]).then_inc(s_ld["mamba"], 16)
                    eng.dma_start(w_out[r, p, q], d["wout"]).then_inc(s_ld["mamba"], 16)
            for j in range(2):
                r = slice(DI * j, DI * j + DI)
                eng.dma_start(xp_raw[r], d["xproj"]).then_inc(s_ld["mamba"], 16)
                eng.dma_start(par[r], d["par"]).then_inc(s_ld["mamba"], 16)
                eng.dma_start(w_dt[RANK * j:RANK * j + RANK, :, r], d["dtw"]).then_inc(s_ld["mamba"], 16)
            for b in range(B):
                q = slice(C * b, C * b + C)
                eng.dma_start(b_conv[q], d["bconv"]).then_inc(s_ld["mamba"], 16)
            eng.dma_start(ycol[:], d["c_ycol"]).then_inc(s_ld["mamba"], 16)

            eng.wait_ge(S("tap"), TAPS)
            eng.wait_ge(S("is_far"), 1)
            with eng.If(eng.value_load(is_far[:], min_val=0, max_val=1) >= 1):
                eng.dma_start(xn_rows, img[:, IMG_0, PAD:PAD + C, PAD:PAD + C]).then_inc(S("xn_rows"), 16)
                for g in range(G):
                    q = slice(C * g, C * g + C)
                    eng.dma_start(far_w[q].rearrange("p a k n -> p (a k n)"),
                                  d["wdef"][CG * g:CG * g + CG].rearrange("(z a) k n -> z (a k n)", z=1)
                                  .to_broadcast([C, CG * TAPS * C])).then_inc(S("far_loaded"), 16)
                    eng.dma_start(far_b[q], d["boff"][g:g + 1, :].to_broadcast([C, 2 * TAPS])).then_inc(S("far_loaded"), 16)
                for q in range(2):
                    eng.dma_start(far_grid[:, q, :], d["c_grid"][q:q + 1, :].to_broadcast([P, T])).then_inc(S("far_loaded"), 16)
                eng.dma_start(far_tap, d["c_tap"]).then_inc(S("far_loaded"), 16)
                eng.wait_ge(S("xn_rows"), 16)
                for b in range(B):
                    for g in range(G):
                        r = C * b + CG * g
                        eng.dma_start(far_img[C * g:C * g + C, b], xn_rows[r:r + CG].rearrange("a y x -> y a x")).then_inc(S("far_loaded"), 16)
                eng.wait_ge(S("far_loaded"), FAR_LOADS)

            eng.wait_ge(s_ld["rpb"], 16 * NH * (2 * lo + 1))
            eng.wait_ge(S("x1t"), 1)
            eng.wait_ge(S("bias_cleared"), 1)
            for r in range(QROWS):
                q = slice(C * r, C * r + C)
                for off, first, d0 in ((0, 0, WIN - 1 - r), (EDGE, r + 1, WIN // 2), (EDGE + INNER, 1, WIN // 2 - r)):
                    for n in range(NH):
                        eng.dma_start(
                            bias[q, n, off + C * first:off + C * (first + WIN)].rearrange("j (r k) -> j r k", k=C),
                            rpb_pad[n, d0:d0 + WIN, :, :].rearrange("r j k -> j r k")).then_inc(s_ld["bias"], 16)
            eng.wait_ge(S("ot_b"), above(B))
            for b in range(B):
                eng.dma_start(ot[C * b:C * b + C, :], ot_b[:, b, :]).then_inc(s_ld["ot"], 16)
            eng.wait_ge(S("x2t"), 1)
            eng.dma_start(sel.bitcast(U16), d["c_sel"].rearrange("p (n m) -> p n m", m=P)).then_inc(s_ld["sel"], 16)
            eng.wait_ge(S("x3t"), 1)
            eng.wait_ge(S("conv_cleared"), 1)
            for b in range(B):
                q = slice(C * b, C * b + C)
                eng.dma_start(w_conv[q, :, :, q].rearrange("p t a n -> p (t a) n"),
                              d["wconv"].rearrange("c t a n -> c (t a) n")).then_inc(s_ld["conv"], 16)
            for q in range(2):
                eng.dma_start(grid[:, q, :], d["c_grid"][q:q + 1, :].to_broadcast([P, T])).then_inc(s_ld["conv"], 16)
            eng.dma_start(selc.bitcast(U16), d["c_selc"].rearrange("p (g q m) -> p g q m", g=CGRP, q=2)).then_inc(s_ld["b4"], 16)
            eng.dma_start(chsel, d["c_chsel"].rearrange("p (b n) -> p b n", b=B)).then_inc(s_ld["b4"], 16)
            for q in range(2):
                for k, part in enumerate((chi, cmid, clo)):
                    eng.wait_ge(S("coord_part"), q * 3 + k + 1)
                    r = (q * 3 + k) * 16
                    eng.dma_start(crow[r:r + 16].rearrange("p j t -> p (j t)"), part[:, q, :]).then_inc(s_ld["rows"], 16)
            for h in range(2):
                eng.wait_ge(S("yout"), h + 1)
                for b in range(B):
                    eng.dma_start(out[b, 16 * h:16 * h + 16].rearrange("h w c -> w h c"),
                                  yout[C * b:C * b + C, HALF * h:HALF * h + HALF].rearrange("p (h c) -> p h c", c=C)).then_inc(S("stored"), 16)
            eng.wait_ge(S("stored"), 16 * 2 * B)

        @block.tensor
        def _(pe):
            for name in LOOPED["tensor"].split():
                pe.sem_inc(S(name), 1)
            def mm(o, l, r, start=True, stop=True, **k):
                return pe.matmul(o, l, r, start=start, stop=stop, **k)

            def halves(dst, lhs, rhs, start=True, stop=True):
                for h in range(2):
                    last = mm(dst[:, HALF * h:HALF * h + HALF], lhs, rhs(h), start, stop)
                return last

            pe.wait_ge(s_ld["x"], 48)
            pe.wait_ge(S("sum1"), 1)
            mm(ps[:, 6, 0:C], ones_b[:], small[:, 0:C]).then_inc(S("mean1"), 1)
            pe.wait_ge(S("sum2"), 1)
            mm(ps[:, 7, 0:C], ones_b[:], small[:, C:2 * C]).then_inc(S("var1"), 1)

            def rows(kind, ky, kx, h):
                r0 = ky + 1 + 16 * h
                return img[:, kind, r0:r0 + 16, kx + 1:kx + 1 + C]

            pe.wait_ge(S("w_off"), B)
            pe.wait_ge(S("img"), 1)

            def offsets(k):
                if k:
                    pe.wait_ge(S("hats"), 4 * k)
                for q in range(2):
                    last = halves(bank2(2 * q), w_off[:, k, q].rearrange("p b g c -> p (b g c)"),
                                  lambda h: img[:, IMG_0, PAD + 16 * h:PAD + 16 * h + 16, PAD:PAD + C])
                last.then_inc(S("off"), 1)

            offsets(0)
            for m in range(NCHK):
                if m:
                    pe.wait_ge(S("absd"), m)
                w = w_off[:, :, :, :, :, 0].rearrange("p k q b g -> p (k q) (b g)")[:, KQ * m:KQ * m + KQ]
                halves(bank2(6)[0:CHK], w,
                       lambda h: img[:, IMG_0, PAD + 16 * h:PAD + 16 * h + 16, PAD:PAD + C]).then_inc(S("chk"), 1)
            pe.wait_ge(s_ld["def"], 16 * B)
            for k in range(TAPS):
                if k + 1 < TAPS:
                    offsets(k + 1)
                ky, kx = divmod(k, 3)
                o = bank2(4)
                halves(o, w_def[:, k], lambda h: rows(IMG_0, ky, kx, h), start=(k == 0), stop=False)
                for j, what in enumerate(("term_a", "term_m", "term_p")):
                    pe.wait_ge(S(what), k + 1)
                    last = halves(o, w_def[:, k], lambda h: term[:, k % 2, j, HALF * h:HALF * h + HALF],
                                  start=False, stop=(k == TAPS - 1 and j == 2))
                last.then_inc(S("tap"), 1)
                if k == 6:
                    pe.wait_ge(S("far"), 1)
                    pe.transpose(ps[0:1, 6, 0:CHK], far[0:CHK, 3:4], ident[0:CHK, 0:CHK]).then_inc(S("far_t"), 1)

            pe.wait_ge(S("is_far"), 1)
            with pe.If(pe.value_load(is_far[:], min_val=0, max_val=1) >= 1):
                pe.wait_ge(S("far_zeroed"), 1)
                for h in range(2):
                    mm(ps[:, 4 + h, :], far_wst.rearrange("p b n -> p (b n)"), x0[:, HALF * h:HALF * h + HALF],
                       start=True, stop=False, skip_group_check=True).then_inc(S("far_open"), 1)
                with pe.Fori(0, TAPS) as k:
                    with pe.Fori(0, B) as b:
                        pe.wait_ge(S("far_off"), above(k * (2 * B) + b * 2 + 2))
                        for q in range(2):
                            last = halves(bank2(2 * q), far_off[:, q].rearrange("p g y -> p (g y)"),
                                          lambda h: img[:, IMG_0, PAD + 16 * h:PAD + 16 * h + 16, PAD:PAD + C])
                        last.then_inc(S("far_d"), 1)
                        pe.wait_ge(S("far_hat"), above(k * (2 * B) + b * 2 + 2))
                        for a in range(CG):
                            pe.wait_ge(S("far_st"), above(k * (2 * B * CG) + b * (2 * CG) + (2 * a + 2)))
                            halves(bank2(6), far_xst.rearrange("p g x -> p (g x)"),
                                   lambda h: far_hat[:, 0, HALF * h:HALF * h + HALF]).then_inc(S("far_q"), 1)
                            pe.wait_ge(S("far_prod"), above(k * (B * CG) + b * CG + (a + 1)))
                            for h in range(2):
                                last = mm(ps[:, 4 + h, :], far_wst.rearrange("p b n -> p (b n)"),
                                          far_prod[:, HALF * h:HALF * h + HALF], start=False, stop=False, skip_group_check=True)
                            last.then_inc(S("far_out"), 1)
                pe.wait_ge(S("far_rezeroed"), 1)
                for h in range(2):
                    mm(ps[:, 4 + h, :], far_wst.rearrange("p b n -> p (b n)"), x0[:, HALF * h:HALF * h + HALF],
                       start=False, stop=True, skip_group_check=True)
            mm(ps[:, 6, 0:C], ones_b[:], ones_b[:, 0:C]).then_inc(S("deform"), 1)

            pe.wait_ge(s_ld["attn"], ATTN_LOADS)
            pe.wait_ge(S("xn2"), 1)
            for m in range(2):
                last = halves(bank2(2 * m), w_attn[:, m], lambda h: xn[:, HALF * h:HALF * h + HALF])
                last.then_inc(S("qk"), 1)
            for i in range(NBLK):
                last = mm(ps[:, 6 + i // 4, P * (i % 4):P * (i % 4) + P], xn[:, P * i:P * i + P], w_attn[:, 2])
                if i % 4 == 3:
                    last.then_inc(S("v"), 1)

            pe.wait_ge(S("qkv_copied"), 4)
            with pe.Fori(0, B) as b:
                def scores(t):
                    n, i = units[t]
                    if i == 0:
                        pe.wait_ge(S("qz"), above(b * NH + (n + 1)))
                    pe.wait_ge(S("neg"), above(b * NUNIT + max(t - 1, 0)))
                    tiles, _ = key_tiles(i)
                    w = P * len(tiles)
                    mm(ps[:, t % 2, 0:w], qz[:, n % 2, P * i:P * i + P],
                       kt[:, P * tiles[0]:P * tiles[0] + w]).then_inc(S("sc"), 1)

                def turn(t):
                    n, i = units[t]
                    tiles, _ = key_tiles(i)
                    pe.wait_ge(S("pn"), above(b * NUNIT + (t + 1)))
                    pe.wait_ge(S("pt"), above(b * NUNIT + max(t - 1, 0)))
                    for c in range(len(tiles)):
                        last = pe.transpose(ps[:, 2 + t % 2, P * c:P * c + P], pn[:, t % NSB, P * c:P * c + P], ident[:])
                    last.then_inc(S("ptp"), 1)

                def values(t):
                    n, i = units[t]
                    tiles, _ = key_tiles(i)
                    if t == 0:
                        pe.wait_ge(S("vz"), above(b + 1))
                        pe.wait_ge(S("ot_b"), above(b))
                    pe.wait_ge(S("pt"), above(b * NUNIT + (t + 1)))
                    for c, tile in enumerate(tiles):
                        last = mm(ps[0:C, 4 + i // 4, P * (i % 4):P * (i % 4) + P], vz[:, tile, n, :],
                                  pt[:, t % NSB, P * c:P * c + P], start=(n == 0 and i % 4 == 0 and c == 0),
                                  stop=(n == NH - 1 and c == len(tiles) - 1), skip_group_check=True)
                    last.then_inc(S("pv"), 1)

                LAG1, LAG2 = 2, 3
                for t in range(len(units) + LAG2):
                    if t < len(units):
                        scores(t)
                    if 0 <= t - LAG1 < len(units):
                        turn(t - LAG1)
                    if 0 <= t - LAG2:
                        values(t - LAG2)

            pe.wait_ge(s_ld["ot"], 16 * B)
            halves(bank2(0), w_attn[:, 3], lambda h: ot[:, HALF * h:HALF * h + HALF]).then_inc(S("proj"), 1)

            pe.wait_ge(s_ld["mamba"], MAMBA_LOADS)
            pe.wait_ge(S("xn3"), 1)
            for m in range(4):
                halves(bank2(2 * m), w_in[:, m], lambda h: xn[:, HALF * h:HALF * h + HALF]).then_inc(S("xz"), 1)
            pe.wait_ge(S("w_xp"), 14)
            pe.wait_ge(S("xs"), DP)
            for t in range(DP):
                dr, p = divmod(t, PAIRS)
                pe.wait_ge(S("u"), t + 1)
                if t:
                    pe.wait_ge(S("bc_read"), 2 * t)
                for w in range(2):
                    halves(bank2(2 * w)[0:96], w_xp[:, dr, w].rearrange("p s j n -> p (s j n)"),
                           lambda h: u[:, dr, p, HALF * h:HALF * h + HALF]).then_inc(S("bc"), 1)
                halves(bank2(4)[0:2 * RANK], w_xd[:, dr].rearrange("p j r -> p (j r)"),
                       lambda h: u[:, dr, p, HALF * h:HALF * h + HALF]).then_inc(S("dtr"), 1)
                pe.wait_ge(S("dtr_copied"), t + 1)
                if t:
                    pe.wait_ge(S("relu_dt"), t)
                    pe.wait_ge(S("e_dt"), t)
                halves(bank2(6), w_dt[:, dr], lambda h: dt_raw[:, HALF * h:HALF * h + HALF]).then_inc(S("dtf"), 1)

            pe.wait_ge(s_ld["sel"], 16)
            pe.wait_ge(S("du"), DP)
            with pe.Fori(0, DP) as t:
                def spread(n):
                    pe.wait_ge(S("dbu"), above(t * NS + max(n - 1, 0)))
                    for h in range(2):
                        last = mm(ps[:, 2 * (n % 2) + h, :], sel[:, n], split_b[:, t, HALF * h:HALF * h + HALF])
                    last.then_inc(S("b_rep"), 1)
                    pe.wait_ge(S("c_copied"), above(t * NS + n))
                    for h in range(2):
                        last = mm(ps[:, 4 + h, :], sel[:, n], split_c[:, t, HALF * h:HALF * h + HALF])
                    last.then_inc(S("c_rep"), 1)

                def collect(n):
                    pe.wait_ge(S("hc"), above(t * NS + (n + 1)))
                    if n == 0:
                        pe.wait_ge(S("y_read"), above(t))
                    for h in range(2):
                        last = mm(ps[:, 6 + h, :], ident[:], hc[:, n % 2, HALF * h:HALF * h + HALF],
                                  start=(n == 0), stop=(n == NS - 1))
                    last.then_inc(S("y_acc"), 1)

                LAG = 2
                for n in range(NS + LAG):
                    if n < NS:
                        spread(n)
                    if n >= LAG:
                        collect(n - LAG)
            pe.wait_ge(S("gated"), PAIRS)
            for p in range(PAIRS):
                for h in range(2):
                    last = mm(ps[:, h, :], w_out[:, p], u[:, 0, p, HALF * h:HALF * h + HALF],
                              start=(p == 0), stop=(p == PAIRS - 1))
            last.then_inc(S("mamba"), 1)

            pe.wait_ge(s_ld["conv"], 16 * (B + 2))
            pe.wait_ge(S("xpad"), 1)
            for par_ in range(2):
                for k in range(9):
                    ky, kx = divmod(k, 3)
                    for h in range(2):
                        last = mm(ps[:, 2 * par_ + h, :], w_conv[:, k, par_],
                                  xpad[:, ky + 16 * h:ky + 16 * h + 16, kx:kx + C], start=(k == 0), stop=(k == 8))
                last.then_inc(S("conv"), 1)
            pe.wait_ge(S("zero_w"), 1)
            for h in range(2):
                mm(ps[:, 6 + h, :], zero_w, x3t[:, HALF * h:HALF * h + HALF], start=True, stop=False,
                   skip_group_check=True)
            pe.wait_ge(s_ld["rows"], 16 * 6)
            pe.wait_ge(s_ld["b4"], 32)
            pe.wait_ge(S("coords_read"), 1)
            with pe.Fori(0, CPER) as j:
                def spread4(t):
                    g, h = divmod(t, 2)
                    pe.wait_ge(S("abs"), above(j * NT + max(t - 1, 0)))
                    for q in range(2):
                        last = mm(ps[:, 2 * (t % 2) + q, :], selc[:, g, q], crow[:, j, HALF * h:HALF * h + HALF])
                    last.then_inc(S("crep"), 1)

                def sample(t):
                    g, h = divmod(t, 2)
                    if h == 0:
                        pe.wait_ge(S("stat"), above(j * (2 * CGRP) + (2 * g + 2)))
                    pe.wait_ge(S("nhat"), above(j * NT + (t + 1)))
                    pe.wait_ge(S("prod"), above(j * NT + max(t - 1, 0)))
                    mm(ps[:, 4 + t % 2, :], xstat[:, g % 2].rearrange("p b x -> p (b x)"),
                       nhat[:, t % 2, 0, :]).then_inc(S("rowmix"), 1)

                def gather(t):
                    g, h = divmod(t, 2)
                    pe.wait_ge(S("prod"), above(j * NT + (t + 1)))
                    mm(ps[:, 6 + h, :], ostat[:, g % 2].rearrange("p b c -> p (b c)"),
                       prod[:, t % 2, :], start=False, stop=False, skip_group_check=True).then_inc(S("gath"), 1)

                for t in range(NT + 2):
                    if t < NT:
                        spread4(t)
                    if 0 <= t - 1 < NT:
                        sample(t - 1)
                    if t >= 2:
                        gather(t - 2)
            for h in range(2):
                last = mm(ps[:, 6 + h, :], zero_w, x3t[:, HALF * h:HALF * h + HALF], start=False, stop=True,
                          skip_group_check=True)
            last.then_inc(S("mapped"), 1)

        @block.vector
        def _(ve):
            for name in LOOPED["vector"].split():
                ve.sem_inc(S(name), 1)
            own = Tally(ve, v_own)

            def tt(o, a, b, op):
                return ve.tensor_tensor(o, a, b, op)

            for w in (w_def, w_attn[:], w_in[:], w_out[:], w_dt[:]):
                last = ve.memset(w, 0.0)
            last.then_inc(s_zero, 1)
            own(ve.memset(img[:, IMG_0], 0.0))
            x3 = x0[:].rearrange("p (h w) -> p h w", w=C)
            xc3 = xc.rearrange("p (h w) -> p h w", w=C)
            ve.wait_ge(s_ld["x"], 48)
            ve.tensor_reduce(small[:, 0:C], x3.rearrange("p h w -> p w h"), AX.X, ALU.add).then_inc(S("sum1"), 1)
            ve.wait_ge(S("mean1"), 1)
            own(tt(xc3, x3, ps[:, 6, 0:C].unsqueeze(1).to_broadcast([P, C, C]), ALU.subtract))
            own.sync()
            own(tt(sq, xc, xc, ALU.mult))
            own.sync()
            ve.tensor_reduce(small[:, C:2 * C], sq.rearrange("p (h w) -> p w h", w=C), AX.X, ALU.add).then_inc(S("sum2"), 1)
            ve.wait_ge(S("var1"), 1)
            ve.tensor_scalar(stat1[:, 0], ps[:, 7, 0:C], 1e-5, None, ALU.add).then_inc(S("var1e"), 1)
            ve.wait_ge(S("std1"), 1)
            own(ve.reciprocal(stat1[:, 2], stat1[:, 1]))
            own.sync()
            inner = slice(PAD, PAD + C)
            tt(img[:, IMG_0, inner, inner], xc3, stat1[:, 2].unsqueeze(1).to_broadcast([P, C, C]), ALU.mult).then_inc(S("img"), 1)
            ve.wait_ge(S("img"), 1)

            def shifted(kind, dy, dx, r0=1, r1=W1 - 1):
                return img[:, kind, r0 + dy:r1 + dy, 1 + dx:W1 - 1 + dx]

            for kind, dx in ((IMG_XM, -1), (IMG_XP, 1)):
                own(tt(shifted(kind, 0, 0, 0, W1), shifted(IMG_0, 0, dx, 0, W1), shifted(IMG_0, 0, 0, 0, W1), ALU.subtract))
            for kind, dy in ((IMG_YM, -1), (IMG_YP, 1)):
                own(tt(shifted(kind, 0, 0), shifted(IMG_0, dy, 0), shifted(IMG_0, 0, 0), ALU.subtract))
            own.sync()
            for kind, of, dy in ((IMG_MM, IMG_XM, -1), (IMG_MP, IMG_XP, -1), (IMG_PM, IMG_XM, 1), (IMG_PP, IMG_XP, 1)):
                last = tt(shifted(kind, 0, 0), shifted(of, dy, 0), shifted(of, 0, 0), ALU.subtract)
            last.then_inc(S("diffs"), 1)
            ve.wait_ge(S("diffs"), 1)

            for k in range(TAPS):
                ky, kx = divmod(k, 3)

                def im(kind):
                    return img[:, kind, ky + 1:ky + 1 + C, kx + 1:kx + 1 + C]

                def square(a):
                    return a.rearrange("p (h w) -> p h w", w=C)

                hat = [square(hats[:, k % 2, j]) for j in range(4)]
                ve.wait_ge(S("hats"), 4 * (k + 1))
                if k:
                    ve.wait_ge(S("term_p"), k)
                if k >= 2:
                    ve.wait_ge(S("tap"), k - 1)
                own(tt(square(tmp_v[:, 2]), hat[0], im(IMG_PM), ALU.mult))
                own(tt(square(tmp_v[:, 3]), hat[1], im(IMG_PP), ALU.mult))
                own(tt(square(tmp_v[:, 0]), hat[0], im(IMG_XM), ALU.mult))
                own(tt(square(tmp_v[:, 1]), hat[1], im(IMG_XP), ALU.mult))
                own.sync(own.n - 2)
                own(tt(tmp_v[:, 2], tmp_v[:, 2], tmp_v[:, 3], ALU.add))
                own.sync(own.n - 1)
                tt(term[:, k % 2, 0], tmp_v[:, 0], tmp_v[:, 1], ALU.add).then_inc(S("term_a"), 1)
                own.sync()
                own(tt(square(tmp_v[:, 3]), square(tmp_v[:, 2]), im(IMG_YP), ALU.add))
                own.sync()
                tt(term[:, k % 2, 2], hats[:, k % 2, 3], tmp_v[:, 3], ALU.mult).then_inc(S("term_p"), 1)
                if k == 3:
                    ve.wait_ge(S("absd"), NCHK)
                    own(ve.tensor_reduce(far[0:CHK, 0:NCHK], absd, AX.X, ALU.max))
                    own.sync()
                    ve.tensor_reduce(far[0:CHK, 3:4], far[0:CHK, 0:NCHK], AX.X, ALU.max).then_inc(S("far"), 1)
                if k == 7:
                    ve.wait_ge(S("far_t"), 1)
                    own(ve.tensor_reduce(small[0:1, 60:61], ps[0:1, 6, 0:CHK], AX.X, ALU.max))
                    own.sync()
                    ve.tensor_scalar(is_far[:], small[0:1, 60:61], 1.0, None, ALU.is_gt).then_inc(S("is_far"), 1)
            ve.wait_ge(S("is_far"), 1)
            with ve.If(ve.value_load(is_far[:], min_val=0, max_val=1) >= 1):
                ve.wait_ge(S("tap"), TAPS)
                ve.wait_ge(S("far_loaded"), FAR_LOADS)
                ve.memset(far_wst, 0.0).then_inc(S("far_zeroed"), 1)
                ve.wait_ge(S("far_zeroed"), 1)
                raw = w_off_raw.rearrange("p (k q) g -> p k q g", q=2)
                with ve.Fori(0, TAPS) as k:
                    with ve.Fori(0, B) as b:
                        ve.wait_ge(S("far_out"), above(k * (B * CG) + b * CG))
                        ve.wait_ge(S("far_open"), 2)
                        for q in range(2):
                            tt(far_off[:, q], raw[:, bass.ds(k, 1), q].rearrange("p a g -> p g a").to_broadcast([P, G, C]),
                               bmask[:, bass.ds(b, 1)].unsqueeze(2).to_broadcast([P, G, C]), ALU.mult).then_inc(S("far_off"), 1)
                        ve.wait_ge(S("far_d"), above(k * B + b + 1))
                        ve.wait_ge(S("far_open"), 2)
                        for q in range(2):
                            ve.scalar_tensor_tensor(out=far_hat[:, q], in0=bank2(2 * q), scalar=far_b[:, bass.ds(k * 2 + q, 1)],
                                                    in1=far_grid[:, q], op0=ALU.add, op1=ALU.add).then_inc(S("far_pos"), 1)
                        for a in range(CG):
                            at = k * (B * CG) + b * CG + a
                            ve.wait_ge(S("far_out"), above(at))
                            ve.wait_ge(S("far_open"), 2)
                            tt(far_xst, far_img[:, bass.ds(b, 1), a].to_broadcast([P, G, C]),
                               bmask[:].unsqueeze(2).to_broadcast([P, G, C]), ALU.mult).then_inc(S("far_st"), 1)
                            tt(far_wst, far_w[:, a, bass.ds(k, 1), :].to_broadcast([P, B, C]),
                               bsel[:, bass.ds(b, 1), :].rearrange("p z b -> p b z").to_broadcast([P, B, C]), ALU.mult).then_inc(S("far_st"), 1)
                            ve.wait_ge(S("far_q"), above(at + 1))
                            ve.wait_ge(S("far_hat"), above(k * (2 * B) + b * 2 + 2))
                            tt(far_prod, bank2(6), far_hat[:, 1], ALU.mult).then_inc(S("far_prod"), 1)
                ve.wait_ge(S("far_out"), above(TAPS * B * CG))
                ve.memset(far_wst, 0.0).then_inc(S("far_rezeroed"), 1)
            ve.wait_ge(S("deform"), 1)
            own(ve.scalar_tensor_tensor(out=x1[:], in0=bank2(4), scalar=0.0, in1=x0[:], op0=ALU.max, op1=ALU.add))
            own.sync()
            ve.transpose(x1t[:].rearrange("p (c h) -> p h c", h=C), x1[:].rearrange("p (h w) -> p h w", w=C)).then_inc(S("x1t"), 1)
            ve.wait_ge(S("x1t"), 1)

            def normalize(x, name):
                for h in range(2):
                    own(ve.bn_stats(small[:, 8 + 6 * h:14 + 6 * h], x[:, HALF * h:HALF * h + HALF]))
                own.sync()
                own(ve.bn_aggr(small[:, 20:22], small[:, 8:20]))
                own.sync()
                ve.tensor_scalar(small[:, 22:23], small[:, 21:22], 1e-5, None, ALU.add).then_inc(S(name + "_var"), 1)
                ve.wait_ge(S(name + "_std"), 1)
                own(ve.reciprocal(small[:, 24:25], small[:, 23:24]))
                own.sync()
                ve.tensor_scalar(xn[:], x[:], small[:, 20:21], small[:, 24:25], ALU.subtract, ALU.mult).then_inc(S(name), 1)

            ve.memset(bias, -BIG).then_inc(S("bias_cleared"), 1)
            normalize(x1t, "xn2")
            own(ve.memset(vz, 0.0))
            ve.wait_ge(S("v"), 2)
            for h in range(2):
                ve.tensor_copy(vt[:, 4 * h:4 * h + 4].rearrange("p a n -> p (a n)"), ps[:, 6 + h, :]).then_inc(S("qkv_copied"), 1)
            ve.wait_ge(S("bias_cleared"), 1)
            ve.wait_ge(s_ld["bias"], 16 * QROWS * 3 * NH)
            own(ve.tensor_scalar(bias, bias, -1.0, None, ALU.mult))
            own.sync()
            ve.wait_ge(S("qkv_copied"), 4)
            with ve.Fori(0, B) as b:
                ve.wait_ge(S("pv"), above(b * NUNIT))
                ve.wait_ge(s_zero, 1)
                for n in range(NH):
                    last = ve.tensor_copy(vz[:, :, n, HD * n:HD * n + HD], vt[:, :, bass.ds(b * C + HD * n, HD)])
                last.then_inc(S("vz"), 1)

                def mask_q(n):
                    ve.wait_ge(S("sc"), above(b * NUNIT + NBLK * max(n - 1, 0)))
                    ve.tensor_scalar(qz[:, n % 2], qt, qmask[:, bass.ds(b * NH + n, 1)], None, ALU.mult).then_inc(S("qz"), 1)

                def wait_scores(t):
                    ve.wait_ge(S("sc"), above(b * NUNIT + (t + 1)))
                    ve.wait_ge(S("pe"), above(b * NUNIT + max(t - NSB + 1, 0)))

                def negate_max(t):
                    n, i = units[t]
                    tiles, off = key_tiles(i)
                    w = P * len(tiles)
                    ve.tensor_tensor_reduce(sc[:, t % NSB, 0:w], ps[:, t % 2, 0:w], bias[:, n, off:off + w], 1.0, 4 * BIG,
                                            ALU.add, ALU.min, nmax[:, t % NSB:t % NSB + 1]).then_inc(S("neg"), 1)

                def inverse(t):
                    ve.wait_ge(S("pe"), above(b * NUNIT + (t + 1)))
                    ve.wait_ge(S("pn"), above(b * NUNIT + max(t - NSB + 1, 0)))
                    ve.reciprocal(rinv[:, t % NSB:t % NSB + 1], sum_row[:, t % NSB:t % NSB + 1]).then_inc(S("rinv"), 1)

                def copy_turned(t):
                    w = P * len(key_tiles(units[t][1])[0])
                    ve.wait_ge(S("ptp"), above(b * NUNIT + (t + 1)))
                    ve.wait_ge(S("pv"), above(b * NUNIT + max(t - NSB + 1, 0)))
                    ve.tensor_copy(pt[:, t % NSB, 0:w], ps[:, 2 + t % 2, 0:w]).then_inc(S("pt"), 1)

                mask_q(0)
                mask_q(1)
                for t in range(NUNIT + 3):
                    if t < NUNIT:
                        wait_scores(t)
                    if t >= 3:
                        copy_turned(t - 3)
                    else:
                        ve.tensor_copy(small[:, 61 + t:62 + t], qmask[:, 0:1])
                    if t < NUNIT:
                        negate_max(t)
                        n = t // NBLK
                        if t % NBLK == 1 and 2 <= n + 1 < NH:
                            mask_q(n + 1)
                    if 0 <= t - 1 < NUNIT:
                        inverse(t - 1)
            ve.wait_ge(S("proj"), 1)
            ve.scalar_tensor_tensor(out=x2t[:], in0=bank2(0), scalar=b_attn[:, 3:4], in1=x1t[:], op0=ALU.add, op1=ALU.add).then_inc(S("x2t"), 1)
            ve.wait_ge(S("x2t"), 1)

            normalize(x2t, "xn3")
            ve.wait_ge(s_ld["mamba"], MAMBA_LOADS)
            own(ve.memset(xs[:, :, 0:KC - 1], 0.0))
            ve.wait_ge(S("xz"), 2)
            own.sync()
            for t in range(DP):
                dr, p = divmod(t, PAIRS)
                src = bank2(2 * p)
                dst = xs[:, t % 2, KC - 1:KC - 1 + T]
                if dr == 1:
                    src = src[:, ::-1]
                elif dr == 2:
                    dst = dst.rearrange("p (m s) -> p m s", s=SLICES)
                    src = src.rearrange("p (s m) -> p m s", s=SLICES)
                ve.tensor_copy(dst, src).then_inc(S("xs"), 1)
                ve.wait_ge(S("xs"), t + 1)
                a = acc_c[:, t % 2]
                if t >= 2:
                    ve.wait_ge(S("u"), t - 1)
                own(ve.tensor_scalar(a, xs[:, t % 2, 0:T], par[:, dr, 0:1], par[:, dr, KC:KC + 1], ALU.mult, ALU.add))
                for k in range(1, KC):
                    own.sync()
                    last = ve.scalar_tensor_tensor(out=a, in0=xs[:, t % 2, k:k + T], scalar=par[:, dr, k:k + 1], in1=a,
                                                   op0=ALU.mult, op1=ALU.add)
                    if k < KC - 1:
                        own(last)
                last.then_inc(S("conv1d"), 1)
                ve.wait_ge(S("conv1d"), t + 1)
            for t in range(DP):
                dr, p = divmod(t, PAIRS)
                for w, dst in enumerate((split_b, split_c)):
                    ve.wait_ge(S("hi"), 2 * t + w + 1)
                    if t:
                        own.sync()
                    r96 = res96[0:96, w]
                    tt(r96, bank2(2 * w)[0:96], dst[:, t], ALU.subtract).then_inc(S("bc_read"), 1)
                    ve.wait_ge(S("bc_read"), 2 * t + w + 1)
                    own(ve.tensor_copy(dst[32:64, t], r96[32:64]))
                    mid = mid96[64:96, w, 0:T // 2].bitcast(BF16)
                    own(ve.tensor_copy(mid, r96[64:96]))
                    own.sync()
                    own(tt(dst[64:96, t], r96[64:96], mid, ALU.subtract))
                ve.wait_ge(S("dtf"), t + 1)
                ve.wait_ge(S("e_dt"), t + 1)
                ve.tensor_scalar(delta[:, t], bank2(6), par[:, dr, KC + 1:KC + 2], 0.0, ALU.add, ALU.max).then_inc(S("relu_dt"), 1)
                ve.wait_ge(S("one_e"), t + 1)
                e, l = sp[0][:, t % 2], sp[1][:, t % 2]
                ve.scalar_tensor_tensor(out=e, in0=l, scalar=-1.0, in1=e, op0=ALU.add, op1=ALU.subtract).then_inc(S("round_e"), 1)
                ve.wait_ge(S("ln"), t + 1)
                ve.wait_ge(S("relu_dt"), t + 1)
                own(tt(delta[:, t], delta[:, t], sp[1][:, t % 2], ALU.add))
                own.sync()
                own(tt(delta[:, t], delta[:, t], sp[0][:, t % 2], ALU.subtract))
                own.sync()
                tt(du[:, t], delta[:, t], u[:, dr, p], ALU.mult).then_inc(S("du"), 1)
            ve.wait_ge(S("du"), DP)
            with ve.Fori(0, DP) as t:
                def inject(n):
                    ve.wait_ge(S("b_rep"), above(t * NS + (n + 1)))
                    ve.wait_ge(S("scan"), above(t * NS + max(n - 1, 0)))
                    ve.wait_ge(s_zero, 1)
                    tt(dbu[:, n % 2], du[:, t], bank2(2 * (n % 2)), ALU.mult).then_inc(S("dbu"), 1)

                def scan(n):
                    ve.wait_ge(S("da"), above(t * NS + (n + 1)))
                    ve.wait_ge(S("dbu"), above(t * NS + (n + 1)))
                    ve.wait_ge(S("hc"), above(t * NS + max(n - 1, 0)))
                    ve.tensor_tensor_scan(hs[:, n % 2], da[:, n % 2], dbu[:, n % 2], 0.0, ALU.mult, ALU.add).then_inc(S("scan"), 1)

                inject(0)
                for n in range(NS):
                    if n + 1 < NS:
                        inject(n + 1)
                    scan(n)
                ve.wait_ge(S("y_acc"), above((t + 1) * NS))
                ud = u.rearrange("p d q t -> p (d q) t")[:, t]
                ve.wait_ge(s_zero, 1)
                ve.scalar_tensor_tensor(out=ud, in0=ud, scalar=d_col[:].rearrange("p d q -> p (d q)")[:, bass.ds(t, 1)],
                                        in1=bank2(6), op0=ALU.mult, op1=ALU.add).then_inc(S("y_read"), 1)
            ve.wait_ge(S("y_read"), above(DP))
            for p in range(PAIRS):
                own(tt(u[:, 0, p], u[:, 0, p], u[:, 1, p, ::-1], ALU.add))
                own.sync()
                y0 = u[:, 0, p].rearrange("p (s m) -> p m s", s=SLICES)
                own(tt(y0, y0, u[:, 2, p].rearrange("p (m s) -> p m s", s=SLICES), ALU.add))
                own.sync()
                tt(u[:, 0, p], u[:, 0, p], zs[:, p], ALU.mult).then_inc(S("gated"), 1)
            ve.wait_ge(S("mamba"), 1)
            tt(x3t[:], bank2(0), x2t[:], ALU.add).then_inc(S("x3t"), 1)
            ve.wait_ge(S("x3t"), 1)

            ve.memset(w_conv, 0.0).then_inc(S("conv_cleared"), 1)
            ve.memset(zero_w, 0.0).then_inc(S("zero_w"), 1)
            own(ve.memset(xpad, 0.0))
            normalize(x3t, "xn4")
            ve.wait_ge(S("xn4"), 1)
            ve.tensor_copy(xpad[:, 1:1 + C, 1:1 + C], xn[:].rearrange("p (h w) -> p h w", w=C)).then_inc(S("xpad"), 1)
            ve.transpose(xrow, xn[:].rearrange("p (r c) -> p c r", c=C)).then_inc(S("xrow"), 1)
            ve.wait_ge(s_ld["conv"], 16 * (B + 2))
            ve.wait_ge(S("conv"), 2)
            for q in range(2):
                for odd in range(2):
                    cols = slice(HALF * odd, HALF * odd + HALF)
                    last = ve.scalar_tensor_tensor(out=coord[:, q, cols], in0=bank2(2 * odd)[:, q::2], scalar=b_conv[:, odd:odd + 1],
                                                   in1=grid[:, q, cols], op0=ALU.add, op1=ALU.add)
            last.then_inc(S("coords_read"), 1)
            ve.wait_ge(S("coords_read"), 1)
            own(ve.tensor_scalar(coord, coord, 0.0, float(C - 1), ALU.max, ALU.min))
            own.sync()
            for q in range(2):
                ve.tensor_copy(chi[:, q], coord[:, q]).then_inc(S("coord_part"), 1)
                ve.wait_ge(S("coord_part"), 3 * q + 1)
                own(tt(coord[:, q], coord[:, q], chi[:, q], ALU.subtract))
                own.sync()
                ve.tensor_copy(cmid[:, q], coord[:, q]).then_inc(S("coord_part"), 1)
                ve.wait_ge(S("coord_part"), 3 * q + 2)
                tt(clo[:, q], coord[:, q], cmid[:, q], ALU.subtract).then_inc(S("coord_part"), 1)
            with ve.Fori(0, CPER) as j:
                def hat4(t):
                    ve.wait_ge(S("abs"), above(j * NT + (t + 1)))
                    ve.wait_ge(S("rowmix"), above(j * NT + max(t - 1, 0)))
                    ve.wait_ge(S("prod"), above(j * NT + max(t - 1, 0)))
                    ve.tensor_scalar(nhat[:, t % 2], ahat[:, t % 2], 1.0, 1.0, ALU.min, ALU.subtract).then_inc(S("nhat"), 1)

                def product(t):
                    ve.wait_ge(S("rowmix"), above(j * NT + (t + 1)))
                    ve.wait_ge(S("nhat"), above(j * NT + (t + 1)))
                    ve.wait_ge(S("gath"), above(j * NT + max(t - 1, 0)))
                    tt(prod[:, t % 2], ps[:, 4 + t % 2, :], nhat[:, t % 2, 1], ALU.mult).then_inc(S("prod"), 1)

                for t in range(NT + 1):
                    if t < NT:
                        hat4(t)
                    if t >= 1:
                        product(t - 1)
            ve.wait_ge(S("mapped"), 1)
            for h in range(2):
                cols = slice(HALF * h, HALF * h + HALF)
                own(tt(y4[:, cols], ps[:, 6 + h, :], x3t[:, cols], ALU.add))
                own.sync()
                ve.transpose(yout[:, cols], y4[:, cols]).then_inc(S("yout"), 1)

        @block.scalar
        def _(ac):
            for name in LOOPED["scalar"].split():
                ac.sem_inc(S(name), 1)
            own = Tally(ac, a_own)
            ac.wait_ge(S("var1e"), 1)
            ac.activation(stat1[:, 1], stat1[:, 0], ACT.Sqrt).then_inc(S("std1"), 1)
            ac.wait_ge(s_ld["off"], OFF_LOADS)
            ac.wait_ge(S("b_off_neg"), 1)
            for k in range(TAPS):
                if k == 1:
                    for m in range(NCHK):
                        ac.wait_ge(S("chk"), m + 1)
                        ac.activation(absd[:, m], bank2(6)[0:CHK], ACT.Abs, bias=b_chk[:, m:m + 1]).then_inc(S("absd"), 1)
                ac.wait_ge(S("off"), k + 1)
                if k >= 2:
                    ac.wait_ge(S("term_m"), k - 1)
                    ac.wait_ge(S("term_p"), k - 1)
                for j, (q, sign) in enumerate(((1, -1.0), (1, 1.0), (0, -1.0), (0, 1.0))):
                    col = (b_off if sign > 0 else b_off_neg)[:, 2 * k + q:2 * k + q + 1]
                    ac.activation(hats[:, k % 2, j], bank2(2 * q), ACT.Relu, bias=col, scale=sign).then_inc(S("hats"), 1)

            ac.wait_ge(S("is_far"), 1)
            with ac.If(ac.value_load(is_far[:], min_val=0, max_val=1) >= 1):
                with ac.Fori(0, TAPS) as k:
                    with ac.Fori(0, B) as b:
                        for q in range(2):
                            ac.wait_ge(S("far_pos"), above(k * (2 * B) + b * 2 + (q + 1)))
                            ac.wait_ge(S("is_far"), 1)
                            ac.activation(far_hat[:, q], far_hat[:, q], ACT.Abs, bias=far_tap[:, bass.ds(k * 2 + q, 1)]).then_inc(S("far_abs"), 1)
                            ac.wait_ge(S("far_abs"), above(k * (2 * B) + b * 2 + (q + 1)))
                            ac.activation(far_hat[:, q], far_hat[:, q], ACT.Relu, bias=1.0, scale=-1.0).then_inc(S("far_hat"), 1)

            def root(name):
                ac.wait_ge(S(name + "_var"), 1)
                ac.activation(small[:, 23:24], small[:, 22:23], ACT.Sqrt).then_inc(S(name + "_std"), 1)

            root("xn2")
            ac.wait_ge(s_ld["attn"], ATTN_LOADS)
            for m, dst in enumerate((qt, kt)):
                ac.wait_ge(S("qk"), m + 1)
                ac.activation(dst, bank2(2 * m), ACT.Identity, bias=b_attn[:, m:m + 1]).then_inc(S("qkv_copied"), 1)
            with ac.Fori(0, B) as b:
                for t, (n, i) in enumerate(units):
                    w = P * len(key_tiles(i)[0])
                    ac.wait_ge(S("neg"), above(b * NUNIT + (t + 1)))
                    ac.wait_ge(S("pn"), above(b * NUNIT + max(t - NSB + 1, 0)))
                    ac.activation(pexp[:, t % NSB, 0:w], sc[:, t % NSB, 0:w], ACT.Exp, bias=nmax[:, t % NSB:t % NSB + 1],
                                  scale=-1.0, accum_out=sum_row[:, t % NSB:t % NSB + 1]).then_inc(S("pe"), 1)
                ac.wait_ge(S("pv"), above((b + 1) * NUNIT))
                ac.wait_ge(s_ld["attn"], ATTN_LOADS)
                ac.activation(ot_b[:, b, :], bank2(4)[0:C], ACT.Identity, bias=bv_row[:, 0:1]).then_inc(S("ot_b"), 1)

            root("xn3")
            for p in range(PAIRS):
                ac.wait_ge(S("xz"), 3 + p)
                ac.activation(zs[:, p], bank2(4 + 2 * p), ACT.Silu).then_inc(S("zs"), 1)
            for t in range(DP):
                dr, p = divmod(t, PAIRS)
                ac.wait_ge(S("conv1d"), t + 1)
                ac.activation(u[:, dr, p], acc_c[:, t % 2], ACT.Silu).then_inc(S("u"), 1)
            a_all = a_col[:].rearrange("p d q n -> p (d q n)")
            ac.wait_ge(S("a_log"), PAIRS)
            own(ac.activation(a_all, a_all, ACT.Exp))
            own.sync()
            ac.mul(a_all, a_all, -1.0).then_inc(S("a_neg"), 1)
            for t in range(DP):
                dr, p = divmod(t, PAIRS)
                for w, dst in enumerate((split_b, split_c)):
                    ac.wait_ge(S("bc"), 2 * t + w + 1)
                    ac.activation(dst[:, t], bank2(2 * w)[0:96], ACT.Copy).then_inc(S("hi"), 1)
                ac.wait_ge(S("dtr"), t + 1)
                ac.activation(dt_raw, bank2(4)[0:2 * RANK], ACT.Copy).then_inc(S("dtr_copied"), 1)
                ac.wait_ge(S("dtf"), t + 1)
                if t >= 2:
                    ac.wait_ge(S("du"), t - 1)
                e, l = sp[0][:, t % 2], sp[1][:, t % 2]
                own(ac.activation(l, bank2(6), ACT.Abs, bias=par[:, dr, KC + 1:KC + 2]))
                own.sync()
                ac.activation(e, l, ACT.Exp, scale=-1.0).then_inc(S("e_dt"), 1)
                ac.wait_ge(S("round_e"), t + 1)
                ac.activation(l, l, ACT.Ln).then_inc(S("ln"), 1)
            ac.wait_ge(S("du"), DP)
            ac.wait_ge(S("a_neg"), 1)
            with ac.Fori(0, DP) as t:
                for n in range(NS):
                    ac.wait_ge(S("scan"), above(t * NS + max(n - 1, 0)))
                    ac.wait_ge(S("a_neg"), 1)
                    ac.activation(da[:, n % 2], delta[:, t], ACT.Exp, scale=a_all[:, bass.ds(t * NS + n, 1)]).then_inc(S("da"), 1)
                    ac.wait_ge(S("c_rep"), above(t * NS + (n + 1)))
                    ac.wait_ge(S("hc"), above(t * NS + max(n - 1, 0)))
                    ac.activation(c_sb[:, n % 2], bank2(4), ACT.Copy).then_inc(S("c_copied"), 1)

            root("xn4")
            ac.wait_ge(S("nycol"), 1)
            with ac.Fori(0, CPER) as j:
                for t in range(NT):
                    ac.wait_ge(S("crep"), above(j * NT + (t + 1)))
                    ac.wait_ge(S("nhat"), above(j * NT + max(t - 1, 0)))
                    ac.activation(ahat[:, t % 2].rearrange("p q n -> p (q n)"), bank2(2 * (t % 2)), ACT.Abs,
                                  bias=nycol[:, 0:1]).then_inc(S("abs"), 1)

        @block.gpsimd
        def _(gp):
            for name in LOOPED["gpsimd"].split():
                gp.sem_inc(S(name), 1)
            own = Tally(gp, g_own)

            def mul(o, a, b):
                return gp.tensor_tensor(o, a, b, ALU.mult)

            def add(o, a, b):
                return gp.tensor_tensor(o, a, b, ALU.add)

            gp.wait_ge(s_ld["off"], OFF_LOADS)
            own(gp.tensor_scalar(b_off_neg, b_off, -1.0, None, ALU.mult))
            own.sync()
            gp.memset(w_off, 0.0).then_inc(S("b_off_neg"), 1)
            gp.wait_ge(S("b_off_neg"), 1)
            wo = w_off.rearrange("p k q b g c -> p (k q) b g c")
            for b in range(B):
                q = slice(C * b, C * b + C)
                gp.tensor_copy(wo[q, :, b], w_off_raw[q].unsqueeze(3).to_broadcast([C, 2 * TAPS, G, CG])).then_inc(S("w_off"), 1)
                gp.wait_ge(S("w_off"), b + 1)
            own(gp.memset(w_xp[:], 0.0))
            own(gp.memset(w_xd[:], 0.0))
            gp.wait_ge(S("diffs"), 1)
            for k in range(TAPS):
                ky, kx = divmod(k, 3)

                def im(kind):
                    return img[:, kind, ky + 1:ky + 1 + C, kx + 1:kx + 1 + C]

                def square(a):
                    return a.rearrange("p (h w) -> p h w", w=C)

                gp.wait_ge(S("hats"), 4 * (k + 1))
                if k:
                    gp.wait_ge(S("term_m"), k)
                own(mul(square(tmp_p[:, 0]), square(hats[:, k % 2, 0]), im(IMG_MM)))
                own(mul(square(tmp_p[:, 1]), square(hats[:, k % 2, 1]), im(IMG_MP)))
                own.sync()
                own(add(tmp_p[:, 0], tmp_p[:, 0], tmp_p[:, 1]))
                own.sync()
                own(add(square(tmp_p[:, 1]), square(tmp_p[:, 0]), im(IMG_YM)))
                own.sync()
                if k >= 2:
                    gp.wait_ge(S("tap"), k - 1)
                mul(term[:, k % 2, 1], hats[:, k % 2, 2], tmp_p[:, 1]).then_inc(S("term_m"), 1)

            gp.wait_ge(S("x1t"), 1)
            gp.wait_ge(s_ld["mamba"], MAMBA_LOADS)
            with gp.Fori(0, B) as b:
                for t, (n, i) in enumerate(units):
                    w = P * len(key_tiles(i)[0])
                    gp.wait_ge(S("ptp"), above(b * NUNIT + max(t - NSB + 1, 0)))
                    gp.wait_ge(S("rinv"), above(b * NUNIT + (t + 1)))
                    gp.tensor_tensor(gate[:, t % NSB:t % NSB + 1], ycol[:], ycol[:], ALU.mult)
                    gp.tensor_scalar(pn[:, t % NSB, 0:w], pexp[:, t % NSB, 0:w], rinv[:, t % NSB:t % NSB + 1], None,
                                     ALU.mult).then_inc(S("pn"), 1)

            gp.wait_ge(s_ld["mamba"], MAMBA_LOADS)
            own.sync()
            for j in range(2):
                r = slice(DI * j, DI * j + DI)
                for w in range(2):
                    raw = xp_raw[r, :, RANK + NS * w:RANK + NS * w + NS]
                    for k in range(3):
                        gp.tensor_copy(w_xp[r, :, w, k, j, :], raw).then_inc(S("w_xp"), 1)
                gp.tensor_copy(w_xd[r, :, j, :], xp_raw[r, :, 0:RANK]).then_inc(S("w_xp"), 1)
                gp.wait_ge(S("w_xp"), 7 * (j + 1))
            for p in range(PAIRS):
                own(gp.tensor_copy(d_col[:, :, p:p + 1], par[:, :, KC + 2:KC + 3]))
                gp.tensor_copy(a_col[:, :, p, :], par[:, :, KC + 3:]).then_inc(S("a_log"), 1)
            gp.tensor_scalar(nycol[:], ycol[:], -1.0, None, ALU.mult).then_inc(S("nycol"), 1)
            for t in range(DP):
                e, l = sp[0][:, t % 2], sp[1][:, t % 2]
                gp.wait_ge(S("e_dt"), t + 1)
                gp.tensor_scalar(l, e, 1.0, None, ALU.add).then_inc(S("one_e"), 1)
            gp.wait_ge(S("du"), DP)
            with gp.Fori(0, DP) as t:
                for n in range(NS):
                    gp.wait_ge(S("scan"), above(t * NS + (n + 1)))
                    gp.wait_ge(S("c_copied"), above(t * NS + (n + 1)))
                    gp.wait_ge(S("y_acc"), above(t * NS + max(n - 1, 0)))
                    gp.wait_ge(S("du"), DP)
                    mul(hc[:, n % 2], hs[:, n % 2], c_sb[:, n % 2]).then_inc(S("hc"), 1)

            gp.wait_ge(S("xrow"), 1)
            gp.wait_ge(s_ld["b4"], 32)
            with gp.Fori(0, CPER) as j:
                for g in range(CGRP):
                    gp.wait_ge(S("gath"), above(j * NT + max(2 * (g - 1), 0)))
                    gp.wait_ge(S("xrow"), 1)
                    gp.tensor_tensor(xstat[:, g % 2],
                                     xrow[:, :, bass.ds(j + CPER * g, 1)].rearrange("p x a -> p a x").to_broadcast([P, B, C]),
                                     bmask[:].unsqueeze(2).to_broadcast([P, B, C]), ALU.mult).then_inc(S("stat"), 1)
                    gp.tensor_copy(ostat[:, g % 2], chsel[:, :, bass.ds(C - 1 - CPER * g - j, C)]).then_inc(S("stat"), 1)
    return nc


def constants():
    import numpy as np

    p = np.arange(P)
    quad, low = p // C, p % C
    same = quad[:, None] == quad[None, :]
    c = {
        "c_ident": np.eye(P, dtype=np.float32),
        "c_ones": (same / float(T)).astype(np.float32),
        "c_far": np.full((NH * 13, T), -BIG, np.float32),
        "c_ycol": low[:, None].astype(np.float32),
        "c_bmask": (quad[:, None] == np.arange(B)[None, :]).astype(np.float32),
        "c_grid": np.stack([np.arange(T) // C, np.arange(T) % C]).astype(np.float32),
    }
    sel_b = np.broadcast_to(np.eye(B, dtype=np.float32), (P, B, B))
    c["c_bsel"] = sel_b.astype(np.float32)
    tap = np.stack([np.arange(TAPS) // 3 - 1, np.arange(TAPS) % 3 - 1], 1).reshape(-1)
    c["c_tap"] = (tap[None, :] - low[:, None]).astype(np.float32)
    head = (quad[:, None] * NH + low[:, None] // HD) == np.arange(B * NH)[None, :]
    c["c_qmask"] = (head * -(float(HD) ** -0.5)).astype(np.float32)
    r = np.arange(96)
    batch, state = (r % 32) // NS, r % NS
    sel = (state[:, None, None] == np.arange(NS)[None, :, None]) & (batch[:, None, None] == (p // DI)[None, None, :])
    one = np.uint16(0x3F80)
    c["c_sel"] = sel.reshape(96, NS * P) * one
    q, rb, rg = r // 48, (r % 16) // CGRP, r % CGRP
    selc = ((rg[:, None, None, None] == np.arange(CGRP)[None, :, None, None])
            & (q[:, None, None, None] == np.arange(2)[None, None, :, None])
            & (rb[:, None, None, None] == quad[None, None, None, :]))
    c["c_selc"] = selc.reshape(96, CGRP * 2 * P) * one
    chsel = np.zeros((P, B, 2 * C - 1), np.float32)
    chsel[p, quad, C - 1] = 1.0
    c["c_chsel"] = chsel.reshape(P, -1)
    return c


def laid_out(i):
    import numpy as np

    a = {k: np.asarray(v) for k, v in i.items()}
    sfx = ("", "_b", "_s")
    cols = [np.stack([a["L2_conv_conv_w" + x] for x in sfx], 1)]
    for name in ("conv_b", "dt_proj_b", "D"):
        cols.append(np.stack([a["L2_conv_" + name + x] for x in sfx], 1)[:, :, None])
    cols.append(np.stack([a["L2_conv_A_log" + x] for x in sfx], 1))
    m = {
        "x": a["x"].reshape(P, T),
        "woff": a["L0_conv_w_off"].reshape(G, TAPS * 2, C).transpose(2, 1, 0).reshape(C, TAPS * 2 * G),
        "boff": a["L0_conv_b_off"].reshape(G, TAPS * 2),
        "bchk": np.broadcast_to(a["L0_conv_b_off"].reshape(1, G, 3, 6).transpose(3, 0, 1, 2), (6, B, G, 3)).reshape(6 * B * G, 3),
        "wdef": a["L0_conv_w_def"].reshape(C, C, TAPS).transpose(1, 2, 0),
        "wqkv": a["L1_conv_w_qkv"], "bqkv": a["L1_conv_b_qkv"], "rpb": a["L1_conv_rpb"],
        "wproj": a["L1_conv_w_proj"], "bproj": a["L1_conv_b_proj"],
        "win": a["L2_conv_in_proj_w"].T,
        "par": np.concatenate(cols, 2),
        "xproj": np.stack([a["L2_conv_x_proj_w" + x].T for x in sfx], 1),
        "dtw": np.stack([a["L2_conv_dt_proj_w" + x].T for x in sfx], 1),
        "wout": a["L2_conv_out_proj_w"].T,
        "wconv": a["L3_conv_W"].reshape(9, C, C, 2).transpose(1, 0, 3, 2),
        "bconv": a["L3_conv_b"].reshape(C, 2),
    }
    m.update(constants())
    return {k: np.ascontiguousarray(v) for k, v in m.items()}


def kernel(**inputs):
    import numpy as _np
    import concourse.bacc as _bacc
    from concourse import mybir as _mybir
    from concourse.bass_utils import run_bass_kernel_spmd as _run

    nc = _bacc.Bacc("TRN2", target_bir_lowering=False, num_devices=1)
    arrays, d = {}, {}
    for name, a in laid_out(inputs).items():
        arrays[f"in_{name}"] = a
        d[name] = nc.dram_tensor(f"in_{name}", a.shape, _mybir.dt.from_np(a.dtype), kind="ExternalInput").ap()
    out = nc.dram_tensor("out_0", (B, C, C, C), _mybir.dt.float32, kind="ExternalOutput").ap()
    build(nc, d, out)
    return _run(nc, [arrays], core_ids=[0]).results[0]["out_0"]
```

```python
from contextlib import ExitStack

import concourse.bass as bass
from concourse import mybir
from concourse.alu_op_type import AluOpType as ALU

ACT = mybir.ActivationFunctionType
F32 = mybir.dt.float32
BF16 = mybir.dt.bfloat16
I32 = mybir.dt.int32
U16 = mybir.dt.uint16
AX = mybir.AxisListType

P = 128
B = 4
C = 32
T = C * C
HALF = 512
BIG = 1e30

G, CG, TAPS = 4, 8, 9
PAD = 2
W1 = C + 2 * PAD

NCHK = 3
KQ = 2 * TAPS // NCHK
CHK = KQ * B * G

NH, HD, WIN = 4, 8, 7
QROWS = 4
NBLK = C // QROWS
EDGE, INNER = 2 * P, 3 * P
NSB = 4
BIASW = EDGE + INNER + EDGE

DI, NS, KC, RANK = 64, 16, 4, 2
DIRS, PAIRS = 3, 2
DP = DIRS * PAIRS
NPAR = KC + 3 + NS
SLICES = 16

CGRP, CPER = 4, 8


def key_tiles(i):
    lo, hi = max(i - 1, 0), min(i + 1, NBLK - 1)
    off = 0 if i == 0 else (EDGE if i < NBLK - 1 else EDGE + INNER)
    near = (0, EDGE) if hi - lo == 1 else (P - C * (WIN // 2), 2 * P + C * (WIN // 2))
    return list(range(lo, hi + 1)), off, near


LEAD = 4
LOOPED = {
    "tensor": "sc turned pv b_rep c_rep y_acc crep rowmix gath far_d far_q far_out",
    "vector": "qz neg pt_v vz dbu y_read scan nhat prod far_off far_pos far_st far_prod",
    "scalar": "ot_b pexp pt_a c_copied da abs far_hat far_abs",
    "gpsimd": "hc stat",
}


def above(n):
    return n + LEAD


class Tally:

    def __init__(self, eng, sem):
        self.eng, self.sem, self.n = eng, sem, 0

    def __call__(self, ins):
        self.n += 1
        ins.then_inc(self.sem, 1)
        return self.n

    def sync(self, n=None):
        self.eng.wait_ge(self.sem, self.n if n is None else n)


def build(nc, d, out):
    with ExitStack() as ctx:
        def sb(name, shape, dt=F32):
            return ctx.enter_context(nc.sbuf_tensor(name, shape, dt))

        def sem(name):
            return ctx.enter_context(nc.semaphore(name))

        ps = ctx.enter_context(nc.psum_tensor("ps", [P, 8, HALF], F32))

        def bank2(i):
            return ps[:, i:i + 2, :].rearrange("p a n -> p (a n)")

        x0 = sb("x0", [P, T])
        x1 = sb("x1", [P, T])
        x1t = sb("x1t", [P, T])
        x2t = sb("x2t", [P, T])
        x3t = sb("x3t", [P, T])
        xn = sb("xn", [P, T])
        ident = sb("ident", [P, P])
        ones_b = sb("ones_b", [P, P])
        qmask = sb("qmask", [P, B * NH + 1])
        ycol = sb("ycol", [P, 1])
        nycol = sb("nycol", [P, 1])
        small = sb("small", [P, 64])
        w_attn = sb("w_attn", [P, 4, P])
        b_attn = sb("b_attn", [P, 4])
        w_in = sb("w_in", [P, 4, P])
        w_xp = sb("w_xp", [P, DIRS, 2, 3, 2, NS])
        w_xd = sb("w_xd", [P, DIRS, 2, RANK])
        xp_raw = sb("xp_raw", [P, DIRS, RANK + 2 * NS])
        w_dt = sb("w_dt", [2 * RANK, DIRS, P])
        w_out = sb("w_out", [P, PAIRS, P])
        par = sb("par", [P, DIRS, NPAR])
        a_col = sb("a_col", [P, DIRS, PAIRS, NS])
        d_col = sb("d_col", [P, DIRS, PAIRS])
        b_conv = sb("b_conv", [P, 2])
        bmask = sb("bmask", [P, B])
        bsel = sb("bsel", [P, B, B])
        far = sb("far", [P, 4])
        is_far = sb("is_far", [1, 1], I32)

        ARENA = 40300
        arena = sb("arena", [P, ARENA])

        class Carve:
            def __init__(self):
                self.at = 0

            def __call__(self, *free, dt=F32, rows=P):
                n = 1
                for f in free:
                    n *= f
                words = n if dt == F32 else (n + 1) // 2
                v = arena[0:rows, self.at:self.at + words]
                self.at += words
                assert self.at <= ARENA, self.at
                if dt != F32:
                    v = v.bitcast(dt)
                if len(free) > 1:
                    names = "abcdef"[:len(free)]
                    v = v.rearrange(f"p ({' '.join(names)}) -> p {' '.join(names)}",
                                    **dict(zip(names, free)))
                return v

        cv = Carve()
        w_off = cv(TAPS, 2, B, G, CG)
        w_off_raw = cv(TAPS * 2, G)
        w_def = cv(TAPS, P)
        b_off = cv(TAPS * 2)
        b_off_neg = cv(TAPS * 2)
        stat1 = cv(3, C)
        img = cv(9, W1, W1)
        hats = cv(2, 4, T)
        term = cv(2, 3, T)
        tmp_v = cv(4, T)
        tmp_p = cv(2, T)
        xc, sq = tmp_v[:, 0], tmp_v[:, 1]
        absd_at = cv.at
        absd = cv(NCHK, T, rows=CHK)
        b_chk = cv(NCHK, rows=CHK)
        cv = Carve()
        cv.at = TAPS * 2 * P + TAPS * 2 * G + TAPS * P + 2 * TAPS * 2 + 3 * C + 9 * W1 * W1
        far_grid = cv(2, T)
        far_hat = cv(2, T)
        far_prod = cv(T)
        far_img = cv(B, CG, C)
        far_w = cv(CG, TAPS, C)
        far_b = cv(2 * TAPS)
        far_tap = cv(2 * TAPS)
        far_off = cv(2, G, C)
        far_xst = cv(G, C)
        far_wst = cv(B, C)
        assert cv.at <= absd_at
        IMG_0, IMG_XM, IMG_XP, IMG_YM, IMG_YP, IMG_MM, IMG_MP, IMG_PM, IMG_PP = range(9)
        cv = Carve()
        kt = cv(T)
        qt = cv(T)
        vt = cv(NBLK, P)
        vz = cv(NBLK, NH, 2, C)
        qz = cv(2, T)
        sc = cv(NSB, INNER)
        pexp = cv(NSB + 2, INNER)
        pt = cv(NSB, INNER)
        nmax = cv(NSB)
        ot_b = cv(B, T, rows=2 * C)
        ot = cv(T)
        os = cv(T)
        assert cv.at <= absd_at
        cv.at = absd_at
        bias_late = cv(2, BIASW)
        bias = [x2t[:, 0:BIASW], x3t[:, 0:BIASW], bias_late[:, 0], bias_late[:, 1]]
        cv = Carve()
        zs = cv(PAIRS, T)
        u = cv(DIRS, PAIRS, T)
        delta = cv(DP, T)
        du = cv(DP, T)
        split_b = cv(DP, T, dt=BF16, rows=96)
        split_c = cv(DP, T, dt=BF16, rows=96)
        sel = cv(NS, P, dt=BF16, rows=96)
        da = cv(2, T)
        dbu = cv(2, T)
        hs = cv(2, T)
        c_sb = cv(2, T)
        hc = cv(2, T)
        xs = cv(2, T + KC - 1)
        dt_raw = x0[0:2 * RANK, :]
        acc_c = da
        res96 = dbu
        mid96 = hs
        sp = [c_sb, hc]
        RING = 4
        hs_ring = [hs[:, 0], hs[:, 1], xs[:, 0, 0:T], xs[:, 1, 0:T]]
        c_ring = [c_sb[:, 0], c_sb[:, 1], x1[:], x1t[:]]
        hc_ring = [hc[:, 0], hc[:, 1], x3t[:], xn[:]]
        cv = Carve()
        WP = C + 2
        w_conv = cv(9, 2, P)
        xpad = cv(WP, WP)
        xrow = cv(C, C)
        grid = cv(2, T)
        coord = cv(2, T)
        chi = cv(2, T, dt=BF16)
        cmid = cv(2, T, dt=BF16)
        clo = cv(2, T, dt=BF16)
        crow = cv(CPER, T, dt=BF16, rows=96)
        selc = cv(CGRP, 2, P, dt=BF16, rows=96)
        chsel = cv(B, 2 * C - 1)
        xstat = cv(2, B, C)
        ostat = cv(2, B, C)
        NU = 2
        ahat = cv(NU, 2, HALF)
        nhat = cv(NU, 2, HALF)
        prod = cv(NU, HALF)
        zero_w = cv(P)
        y4 = cv(T)
        yout = cv(T)

        xn_rows = nc.dram_tensor("xn_rows", (P, C, C), F32, kind="Internal").ap()
        rpb_pad = nc.dram_tensor("rpb_pad", (NH, 13, C, C), F32, kind="Internal").ap()

        s_ld = {k: sem("ld_" + k) for k in
                ("x", "off", "def", "attn", "mamba", "conv", "pad", "rpb", "fill", "bias", "sel", "b4",
                 "ot", "rows")}
        s_zero = sem("weights_zeroed")
        v_own, a_own, g_own = sem("vector_own"), sem("scalar_own"), sem("gpsimd_own")
        s = {}

        def S(name):
            if name not in s:
                s[name] = sem(name)
            return s[name]

        OFF_LOADS = 16 * (B * (1 + G) + 3)
        FAR_LOADS = 16 * (G + G + 2 + 1 + B * G)
        ATTN_LOADS = 16 * (B * 8 + 1)
        MAMBA_LOADS = 16 * (4 * 3 + 6 + B + 1)
        NT = 2 * CGRP
        units = [(n, i) for n in range(NH) for i in range(NBLK)]
        NUNIT = len(units)
        LAG_TURN, LAG_COPY, LAG_PV = 2, 3, 4

        def pexp_buffer(t):
            i = units[t][1]
            return NSB if i == 0 else (NSB + 1 if i == NBLK - 1 else t % NSB)

        block = ctx.enter_context(nc.Block())

        @block.sync
        def _(eng):
            eng.dma_start(x0[:], d["x"]).then_inc(s_ld["x"], 16)
            eng.dma_start(ones_b[:], d["c_ones"]).then_inc(s_ld["x"], 16)
            eng.dma_start(ident[:], d["c_ident"]).then_inc(s_ld["x"], 16)
            for b in range(B):
                q = slice(C * b, C * b + C)
                eng.dma_start(w_off_raw[q], d["woff"].rearrange("c (k g) -> c k g", g=G)).then_inc(s_ld["off"], 16)
                for g in range(G):
                    r = C * b + CG * g
                    eng.dma_start(b_off[r:r + CG], d["boff"][g:g + 1, :].to_broadcast([CG, 2 * TAPS])).then_inc(s_ld["off"], 16)
            eng.dma_start(b_chk, d["bchk"]).then_inc(s_ld["off"], 16)
            eng.dma_start(bmask[:], d["c_bmask"]).then_inc(s_ld["off"], 16)
            eng.dma_start(bsel[:], d["c_bsel"]).then_inc(s_ld["off"], 16)
            eng.wait_ge(s_zero, 1)
            for b in range(B):
                q = slice(C * b, C * b + C)
                eng.dma_start(w_def[q, :, q], d["wdef"]).then_inc(s_ld["def"], 16)
            eng.dma_start(rpb_pad.rearrange("n r j k -> (n r) (j k)"), d["c_far"]).then_inc(s_ld["pad"], 16)
            eng.wait_ge(s_ld["pad"], 16)
            lo, hi = WIN // 2, C - WIN // 2 - 1
            for n in range(NH):
                flat = rpb_pad[n].rearrange("r j k -> r (j k)")
                for j in list(range(lo)) + list(range(hi + 1, C)):
                    k0 = min(max(j - lo, 0), C - WIN)
                    eng.dma_start(rpb_pad[n, :, j, k0:k0 + WIN],
                                  d["rpb"][n, :, k0 - j + WIN - 1:k0 - j + 2 * WIN - 1]).then_inc(s_ld["rpb"], 16)
                dst = flat[:, lo * C:lo * C + (hi - lo + 1) * (C + 1)]
                dst = dst.rearrange("r (j k) -> r j k", k=C + 1)[:, :, 0:WIN]
                src = d["rpb"][n, :, WIN - 1 - lo:WIN - 1 - lo + WIN].unsqueeze(1).to_broadcast([13, hi - lo + 1, WIN])
                eng.dma_start(dst, src).then_inc(s_ld["rpb"], 16)
            for b in range(B):
                q = slice(C * b, C * b + C)
                for m in range(3):
                    eng.dma_start(w_attn[q, m, q], d["wqkv"][:, C * m:C * m + C]).then_inc(s_ld["attn"], 16)
                    eng.dma_start(b_attn[q, m:m + 1], d["bqkv"][C * m:C * m + C].rearrange("(c a) -> c a", a=1)).then_inc(s_ld["attn"], 16)
                eng.dma_start(w_attn[q, 3, q], d["wproj"]).then_inc(s_ld["attn"], 16)
                eng.dma_start(b_attn[q, 3:4], d["bproj"].rearrange("(c a) -> c a", a=1)).then_inc(s_ld["attn"], 16)
            eng.dma_start(qmask[:], d["c_qmask"]).then_inc(s_ld["attn"], 16)
            for p in range(PAIRS):
                for j in range(2):
                    b = 2 * p + j
                    q = slice(C * b, C * b + C)
                    r = slice(DI * j, DI * j + DI)
                    for part in range(2):
                        eng.dma_start(w_in[q, 2 * part + p, r], d["win"][:, DI * part:DI * part + DI]).then_inc(s_ld["mamba"], 16)
                    eng.dma_start(w_out[r, p, q], d["wout"]).then_inc(s_ld["mamba"], 16)
            for j in range(2):
                r = slice(DI * j, DI * j + DI)
                eng.dma_start(xp_raw[r], d["xproj"]).then_inc(s_ld["mamba"], 16)
                eng.dma_start(par[r], d["par"]).then_inc(s_ld["mamba"], 16)
                eng.dma_start(w_dt[RANK * j:RANK * j + RANK, :, r], d["dtw"]).then_inc(s_ld["mamba"], 16)
            for b in range(B):
                q = slice(C * b, C * b + C)
                eng.dma_start(b_conv[q], d["bconv"]).then_inc(s_ld["mamba"], 16)
            eng.dma_start(ycol[:], d["c_ycol"]).then_inc(s_ld["mamba"], 16)

            eng.wait_ge(s_ld["rpb"], 16 * NH * (2 * lo + 1))
            eng.wait_ge(S("far"), 1)
            for n in range(NH):
                eng.dma_start(bias[n], d["c_far"][0:1, 0:BIASW].to_broadcast([P, BIASW])).then_inc(s_ld["fill"], 16)
            eng.wait_ge(s_ld["fill"], 16 * NH)
            for r in range(QROWS):
                q = slice(C * r, C * r + C)
                for off, first, d0 in ((0, 0, WIN - 1 - r), (EDGE, r + 1, WIN // 2), (EDGE + INNER, 1, WIN // 2 - r)):
                    for n in range(NH):
                        eng.dma_start(
                            bias[n][q, off + C * first:off + C * (first + WIN)].rearrange("j (r k) -> j r k", k=C),
                            rpb_pad[n, d0:d0 + WIN, :, :].rearrange("r j k -> j r k")).then_inc(s_ld["bias"], 16)

            eng.wait_ge(S("tap"), TAPS)
            eng.wait_ge(S("is_far"), 1)
            with eng.If(eng.value_load(is_far[:], min_val=0, max_val=1) >= 1):
                eng.dma_start(xn_rows, img[:, IMG_0, PAD:PAD + C, PAD:PAD + C]).then_inc(S("xn_rows"), 16)
                for g in range(G):
                    q = slice(C * g, C * g + C)
                    eng.dma_start(far_w[q].rearrange("p a k n -> p (a k n)"),
                                  d["wdef"][CG * g:CG * g + CG].rearrange("(z a) k n -> z (a k n)", z=1)
                                  .to_broadcast([C, CG * TAPS * C])).then_inc(S("far_loaded"), 16)
                    eng.dma_start(far_b[q], d["boff"][g:g + 1, :].to_broadcast([C, 2 * TAPS])).then_inc(S("far_loaded"), 16)
                for q in range(2):
                    eng.dma_start(far_grid[:, q, :], d["c_grid"][q:q + 1, :].to_broadcast([P, T])).then_inc(S("far_loaded"), 16)
                eng.dma_start(far_tap, d["c_tap"]).then_inc(S("far_loaded"), 16)
                eng.wait_ge(S("xn_rows"), 16)
                for b in range(B):
                    for g in range(G):
                        r = C * b + CG * g
                        eng.dma_start(far_img[C * g:C * g + C, b], xn_rows[r:r + CG].rearrange("a y x -> y a x")).then_inc(S("far_loaded"), 16)
                eng.wait_ge(S("far_loaded"), FAR_LOADS)

            for b in range(B):
                eng.wait_ge(S("ot_b"), above(b + 1))
                eng.dma_start(ot[C * b:C * b + C, :], ot_b[0:C, b, :]).then_inc(s_ld["ot"], 16)
                eng.dma_start(os[C * b:C * b + C, :], ot_b[C:2 * C, b, :]).then_inc(s_ld["ot"], 16)
            eng.wait_ge(S("x2t"), 1)
            eng.dma_start(sel.bitcast(U16), d["c_sel"].rearrange("p (n m) -> p n m", m=P)).then_inc(s_ld["sel"], 16)
            eng.wait_ge(S("x3t"), 1)
            eng.wait_ge(S("conv_cleared"), 1)
            for b in range(B):
                q = slice(C * b, C * b + C)
                eng.dma_start(w_conv[q, :, :, q].rearrange("p t a n -> p (t a) n"),
                              d["wconv"].rearrange("c t a n -> c (t a) n")).then_inc(s_ld["conv"], 16)
            for q in range(2):
                eng.dma_start(grid[:, q, :], d["c_grid"][q:q + 1, :].to_broadcast([P, T])).then_inc(s_ld["conv"], 16)
            eng.dma_start(selc.bitcast(U16), d["c_selc"].rearrange("p (g q m) -> p g q m", g=CGRP, q=2)).then_inc(s_ld["b4"], 16)
            eng.dma_start(chsel, d["c_chsel"].rearrange("p (b n) -> p b n", b=B)).then_inc(s_ld["b4"], 16)
            for q in range(2):
                for k, part in enumerate((chi, cmid, clo)):
                    eng.wait_ge(S("coord_part"), q * 3 + k + 1)
                    r = (q * 3 + k) * 16
                    eng.dma_start(crow[r:r + 16].rearrange("p j t -> p (j t)"), part[:, q, :]).then_inc(s_ld["rows"], 16)
            for h in range(2):
                eng.wait_ge(S("yout"), h + 1)
                for b in range(B):
                    eng.dma_start(out[b, 16 * h:16 * h + 16].rearrange("h w c -> w h c"),
                                  yout[C * b:C * b + C, HALF * h:HALF * h + HALF].rearrange("p (h c) -> p h c", c=C)).then_inc(S("stored"), 16)
            eng.wait_ge(S("stored"), 16 * 2 * B)

        @block.tensor
        def _(pe):
            for name in LOOPED["tensor"].split():
                pe.sem_inc(S(name), LEAD)
            def mm(o, l, r, start=True, stop=True, **k):
                return pe.matmul(o, l, r, start=start, stop=stop, **k)

            def halves(dst, lhs, rhs, start=True, stop=True):
                for h in range(2):
                    last = mm(dst[:, HALF * h:HALF * h + HALF], lhs, rhs(h), start, stop)
                return last

            pe.wait_ge(s_ld["x"], 48)
            pe.wait_ge(S("sum1"), 1)
            mm(ps[:, 6, 0:C], ones_b[:], small[:, 0:C]).then_inc(S("mean1"), 1)
            pe.wait_ge(S("sum2"), 1)
            mm(ps[:, 7, 0:C], ones_b[:], small[:, C:2 * C]).then_inc(S("var1"), 1)

            def rows(kind, ky, kx, h):
                r0 = ky + 1 + 16 * h
                return img[:, kind, r0:r0 + 16, kx + 1:kx + 1 + C]

            pe.wait_ge(S("w_off"), B)
            pe.wait_ge(S("img"), 1)

            def offsets(k):
                if k:
                    pe.wait_ge(S("hats"), 4 * k)
                for q in range(2):
                    last = halves(bank2(2 * q), w_off[:, k, q].rearrange("p b g c -> p (b g c)"),
                                  lambda h: img[:, IMG_0, PAD + 16 * h:PAD + 16 * h + 16, PAD:PAD + C])
                last.then_inc(S("off"), 1)

            offsets(0)
            for m in range(NCHK):
                if m:
                    pe.wait_ge(S("absd"), m)
                w = w_off[:, :, :, :, :, 0].rearrange("p k q b g -> p (k q) (b g)")[:, KQ * m:KQ * m + KQ]
                halves(bank2(6)[0:CHK], w,
                       lambda h: img[:, IMG_0, PAD + 16 * h:PAD + 16 * h + 16, PAD:PAD + C]).then_inc(S("chk"), 1)
            pe.wait_ge(s_ld["def"], 16 * B)
            for k in range(TAPS):
                if k + 1 < TAPS:
                    offsets(k + 1)
                ky, kx = divmod(k, 3)
                o = bank2(4)
                halves(o, w_def[:, k], lambda h: rows(IMG_0, ky, kx, h), start=(k == 0), stop=False)
                for j, what in enumerate(("term_a", "term_m", "term_p")):
                    pe.wait_ge(S(what), k + 1)
                    last = halves(o, w_def[:, k], lambda h: term[:, k % 2, j, HALF * h:HALF * h + HALF],
                                  start=False, stop=(k == TAPS - 1 and j == 2))
                last.then_inc(S("tap"), 1)
                if k == 6:
                    pe.wait_ge(S("far"), 1)
                    pe.transpose(ps[0:1, 6, 0:CHK], far[0:CHK, 3:4], ident[0:CHK, 0:CHK]).then_inc(S("far_t"), 1)

            pe.wait_ge(S("is_far"), 1)
            with pe.If(pe.value_load(is_far[:], min_val=0, max_val=1) >= 1):
                pe.wait_ge(S("far_zeroed"), 1)
                for h in range(2):
                    mm(ps[:, 4 + h, :], far_wst.rearrange("p b n -> p (b n)"), x0[:, HALF * h:HALF * h + HALF],
                       start=True, stop=False, skip_group_check=True).then_inc(S("far_open"), 1)
                with pe.Fori(0, TAPS) as k:
                    with pe.Fori(0, B) as b:
                        pe.wait_ge(S("far_off"), above(k * (2 * B) + b * 2 + 2))
                        for q in range(2):
                            last = halves(bank2(2 * q), far_off[:, q].rearrange("p g y -> p (g y)"),
                                          lambda h: img[:, IMG_0, PAD + 16 * h:PAD + 16 * h + 16, PAD:PAD + C])
                        last.then_inc(S("far_d"), 1)
                        pe.wait_ge(S("far_hat"), above(k * (2 * B) + b * 2 + 2))
                        for a in range(CG):
                            pe.wait_ge(S("far_st"), above(k * (2 * B * CG) + b * (2 * CG) + (2 * a + 2)))
                            halves(bank2(6), far_xst.rearrange("p g x -> p (g x)"),
                                   lambda h: far_hat[:, 0, HALF * h:HALF * h + HALF]).then_inc(S("far_q"), 1)
                            pe.wait_ge(S("far_prod"), above(k * (B * CG) + b * CG + (a + 1)))
                            for h in range(2):
                                last = mm(ps[:, 4 + h, :], far_wst.rearrange("p b n -> p (b n)"),
                                          far_prod[:, HALF * h:HALF * h + HALF], start=False, stop=False, skip_group_check=True)
                            last.then_inc(S("far_out"), 1)
                pe.wait_ge(S("far_rezeroed"), 1)
                for h in range(2):
                    mm(ps[:, 4 + h, :], far_wst.rearrange("p b n -> p (b n)"), x0[:, HALF * h:HALF * h + HALF],
                       start=False, stop=True, skip_group_check=True)
            mm(ps[:, 6, 0:C], ones_b[:], ones_b[:, 0:C]).then_inc(S("deform"), 1)

            pe.wait_ge(s_ld["attn"], ATTN_LOADS)
            pe.wait_ge(S("xn2"), 1)
            for m in range(2):
                last = halves(bank2(2 * m), w_attn[:, m], lambda h: xn[:, HALF * h:HALF * h + HALF])
                last.then_inc(S("qk"), 1)
            for i in range(NBLK):
                last = mm(ps[:, 6 + i // 4, P * (i % 4):P * (i % 4) + P], xn[:, P * i:P * i + P], w_attn[:, 2])
                if i % 4 == 3:
                    last.then_inc(S("v"), 1)

            pe.wait_ge(S("qkv_copied"), 4)

            def scores(b, t):
                n, i = units[t]
                if i == 0:
                    pe.wait_ge(S("qz"), above(b * NH + (n + 1)))
                pe.wait_ge(S("neg"), above(b * NUNIT + (t - 2 if t >= 3 else t - 1)))
                tiles, _, (lo, hi) = key_tiles(i)
                mm(ps[:, (0, 1, 6)[t % 3], lo:hi], qz[:, n % 2, P * i:P * i + P],
                   kt[:, P * tiles[0] + lo:P * tiles[0] + hi]).then_inc(S("sc"), 1)

            def pt_done(b, t):
                pe.wait_ge(S("pt_a" if t % 2 else "pt_v"), above(b * (NUNIT // 2) + (t // 2 + 1)))

            def turn(b, t):
                tiles, _, _ = key_tiles(units[t % NUNIT][1])
                pe.wait_ge(S("pexp"), above(b * NUNIT + (t + 1)))
                pt_done(b, t - 3 if t % NUNIT >= 3 else t - 2)
                for c in range(len(tiles)):
                    last = pe.transpose(ps[:, (2, 3, 7)[t % NUNIT % 3], P * c:P * c + P],
                                        pexp[:, pexp_buffer(t % NUNIT), P * c:P * c + P], ident[:])
                last.then_inc(S("turned"), 1)

            def values(b, t):
                n, i = units[t % NUNIT]
                tiles, _, _ = key_tiles(i)
                if t == 0:
                    pe.wait_ge(S("vz"), above(b + 1))
                    pe.wait_ge(S("ot_b"), above(b))
                pt_done(b, t)
                for c, tile in enumerate(tiles):
                    last = mm(ps[0:2 * C, 4 + i // 4, P * (i % 4):P * (i % 4) + P], vz[:, tile, n].rearrange("p a c -> p (a c)"),
                              pt[:, t % NSB, P * c:P * c + P], start=(n == 0 and i % 4 == 0 and c == 0),
                              stop=(n == NH - 1 and c == len(tiles) - 1), skip_group_check=True)
                last.then_inc(S("pv"), 1)

            def attend(b, first):
                for t in range(NUNIT):
                    scores(b, t)
                    if t >= LAG_TURN or not first:
                        turn(b, t - LAG_TURN)
                    if t >= LAG_PV or not first:
                        values(b, t - LAG_PV)

            attend(0, True)
            with pe.Fori(1, B) as b:
                attend(b, False)
            for t in range(LAG_PV):
                if t < LAG_TURN:
                    turn(B, t - LAG_TURN)
                values(B, t - LAG_PV)

            pe.wait_ge(S("attended"), 1)
            halves(bank2(0), w_attn[:, 3], lambda h: ot[:, HALF * h:HALF * h + HALF]).then_inc(S("proj"), 1)

            pe.wait_ge(s_ld["mamba"], MAMBA_LOADS)
            pe.wait_ge(S("xn3"), 1)
            for m in range(4):
                halves(bank2(2 * m), w_in[:, m], lambda h: xn[:, HALF * h:HALF * h + HALF]).then_inc(S("xz"), 1)
            pe.wait_ge(S("w_xp"), 14)
            pe.wait_ge(S("xs"), DP)
            for t in range(DP):
                dr, p = divmod(t, PAIRS)
                pe.wait_ge(S("u"), t + 1)
                if t:
                    pe.wait_ge(S("bc_read"), 2 * t)
                for w in range(2):
                    halves(bank2(2 * w)[0:96], w_xp[:, dr, w].rearrange("p s j n -> p (s j n)"),
                           lambda h: u[:, dr, p, HALF * h:HALF * h + HALF]).then_inc(S("bc"), 1)
                halves(bank2(4)[0:2 * RANK], w_xd[:, dr].rearrange("p j r -> p (j r)"),
                       lambda h: u[:, dr, p, HALF * h:HALF * h + HALF]).then_inc(S("dtr"), 1)
                pe.wait_ge(S("dtr_copied"), t + 1)
                if t:
                    pe.wait_ge(S("relu_dt"), t)
                    pe.wait_ge(S("e_dt"), t)
                halves(bank2(6), w_dt[:, dr], lambda h: dt_raw[:, HALF * h:HALF * h + HALF]).then_inc(S("dtf"), 1)

            pe.wait_ge(s_ld["sel"], 16)
            pe.wait_ge(S("du"), DP)

            def spread(t, n):
                pe.wait_ge(S("dbu"), above(t * NS + (n - 1)))
                for h in range(2):
                    last = mm(ps[:, 2 * (n % 2) + h, :], sel[:, n], split_b[:, t, HALF * h:HALF * h + HALF])
                last.then_inc(S("b_rep"), 1)
                pe.wait_ge(S("c_copied"), above(t * NS + n))
                for h in range(2):
                    last = mm(ps[:, 4 + h, :], sel[:, n], split_c[:, t, HALF * h:HALF * h + HALF])
                last.then_inc(S("c_rep"), 1)

            def collect(t, n):
                pe.wait_ge(S("hc"), above(t * NS + (n + 1)))
                if n == 0:
                    pe.wait_ge(S("y_read"), above(t))
                for h in range(2):
                    last = mm(ps[:, 6 + h, :], ident[:], hc_ring[n % RING][:, HALF * h:HALF * h + HALF],
                              start=(n == 0), stop=(n == NS - 1))
                last.then_inc(S("y_acc"), 1)

            def states(t, more):
                for n in range(NS):
                    if n + AHEAD < NS:
                        spread(t, n + AHEAD)
                    elif more:
                        spread(t + 1, n + AHEAD - NS)
                    collect(t, n)

            AHEAD = 3
            for n in range(AHEAD):
                spread(0, n)
            with pe.Fori(0, DP - 1) as t:
                states(t, True)
            states(DP - 1, False)
            pe.wait_ge(S("gated"), PAIRS)
            for p in range(PAIRS):
                for h in range(2):
                    last = mm(ps[:, h, :], w_out[:, p], u[:, 0, p, HALF * h:HALF * h + HALF],
                              start=(p == 0), stop=(p == PAIRS - 1))
            last.then_inc(S("mamba"), 1)

            pe.wait_ge(s_ld["conv"], 16 * (B + 2))
            pe.wait_ge(S("xpad"), 1)
            for par_ in range(2):
                for k in range(9):
                    ky, kx = divmod(k, 3)
                    for h in range(2):
                        last = mm(ps[:, 2 * par_ + h, :], w_conv[:, k, par_],
                                  xpad[:, ky + 16 * h:ky + 16 * h + 16, kx:kx + C], start=(k == 0), stop=(k == 8))
                last.then_inc(S("conv"), 1)
            pe.wait_ge(S("zero_w"), 1)
            for h in range(2):
                mm(ps[:, 6 + h, :], zero_w, x3t[:, HALF * h:HALF * h + HALF], start=True, stop=False,
                   skip_group_check=True)
            pe.wait_ge(s_ld["rows"], 16 * 6)
            pe.wait_ge(s_ld["b4"], 32)
            pe.wait_ge(S("coords_read"), 1)
            with pe.Fori(0, CPER) as j:
                def spread4(t):
                    g, h = divmod(t, 2)
                    pe.wait_ge(S("abs"), above(j * NT + t - 1))
                    for q in range(2):
                        last = mm(ps[:, 2 * (t % 2) + q, :], selc[:, g, q], crow[:, j, HALF * h:HALF * h + HALF])
                    last.then_inc(S("crep"), 1)

                def sample(t):
                    g, h = divmod(t, 2)
                    if h == 0:
                        pe.wait_ge(S("stat"), above(j * (2 * CGRP) + (2 * g + 2)))
                    pe.wait_ge(S("nhat"), above(j * NT + (t + 1)))
                    pe.wait_ge(S("prod"), above(j * NT + t - 1))
                    mm(ps[:, 4 + t % 2, :], xstat[:, g % 2].rearrange("p b x -> p (b x)"),
                       nhat[:, t % 2, 0, :]).then_inc(S("rowmix"), 1)

                def gather(t):
                    g, h = divmod(t, 2)
                    pe.wait_ge(S("prod"), above(j * NT + (t + 1)))
                    mm(ps[:, 6 + h, :], ostat[:, g % 2].rearrange("p b c -> p (b c)"),
                       prod[:, t % 2, :], start=False, stop=False, skip_group_check=True).then_inc(S("gath"), 1)

                for t in range(NT + 2):
                    if t < NT:
                        spread4(t)
                    if 0 <= t - 1 < NT:
                        sample(t - 1)
                    if t >= 2:
                        gather(t - 2)
            for h in range(2):
                last = mm(ps[:, 6 + h, :], zero_w, x3t[:, HALF * h:HALF * h + HALF], start=False, stop=True,
                          skip_group_check=True)
            last.then_inc(S("mapped"), 1)

        @block.vector
        def _(ve):
            for name in LOOPED["vector"].split():
                ve.sem_inc(S(name), LEAD)
            own = Tally(ve, v_own)

            def tt(o, a, b, op):
                return ve.tensor_tensor(o, a, b, op)

            for w in (w_def, w_attn[:], w_in[:], w_out[:], w_dt[:]):
                last = ve.memset(w, 0.0)
            last.then_inc(s_zero, 1)
            own(ve.memset(img[:, IMG_0], 0.0))
            x3 = x0[:].rearrange("p (h w) -> p h w", w=C)
            xc3 = xc.rearrange("p (h w) -> p h w", w=C)
            ve.wait_ge(s_ld["x"], 48)
            ve.tensor_reduce(small[:, 0:C], x3.rearrange("p h w -> p w h"), AX.X, ALU.add).then_inc(S("sum1"), 1)
            ve.wait_ge(S("mean1"), 1)
            own(tt(xc3, x3, ps[:, 6, 0:C].unsqueeze(1).to_broadcast([P, C, C]), ALU.subtract))
            own.sync()
            own(tt(sq, xc, xc, ALU.mult))
            own.sync()
            ve.tensor_reduce(small[:, C:2 * C], sq.rearrange("p (h w) -> p w h", w=C), AX.X, ALU.add).then_inc(S("sum2"), 1)
            ve.wait_ge(S("var1"), 1)
            ve.tensor_scalar(stat1[:, 0], ps[:, 7, 0:C], 1e-5, None, ALU.add).then_inc(S("var1e"), 1)
            ve.wait_ge(S("std1"), 1)
            own(ve.reciprocal(stat1[:, 2], stat1[:, 1]))
            own.sync()
            inner = slice(PAD, PAD + C)
            tt(img[:, IMG_0, inner, inner], xc3, stat1[:, 2].unsqueeze(1).to_broadcast([P, C, C]), ALU.mult).then_inc(S("img"), 1)
            ve.wait_ge(S("img"), 1)

            def shifted(kind, dy, dx, r0=1, r1=W1 - 1):
                return img[:, kind, r0 + dy:r1 + dy, 1 + dx:W1 - 1 + dx]

            for kind, dx in ((IMG_XM, -1), (IMG_XP, 1)):
                own(tt(shifted(kind, 0, 0, 0, W1), shifted(IMG_0, 0, dx, 0, W1), shifted(IMG_0, 0, 0, 0, W1), ALU.subtract))
            for kind, dy in ((IMG_YM, -1), (IMG_YP, 1)):
                own(tt(shifted(kind, 0, 0), shifted(IMG_0, dy, 0), shifted(IMG_0, 0, 0), ALU.subtract))
            own.sync()
            for kind, of, dy in ((IMG_MM, IMG_XM, -1), (IMG_MP, IMG_XP, -1), (IMG_PM, IMG_XM, 1), (IMG_PP, IMG_XP, 1)):
                last = tt(shifted(kind, 0, 0), shifted(of, dy, 0), shifted(of, 0, 0), ALU.subtract)
            last.then_inc(S("diffs"), 1)
            ve.wait_ge(S("diffs"), 1)

            for k in range(TAPS):
                ky, kx = divmod(k, 3)

                def im(kind):
                    return img[:, kind, ky + 1:ky + 1 + C, kx + 1:kx + 1 + C]

                def square(a):
                    return a.rearrange("p (h w) -> p h w", w=C)

                hat = [square(hats[:, k % 2, j]) for j in range(4)]
                ve.wait_ge(S("hats"), 4 * (k + 1))
                if k:
                    ve.wait_ge(S("term_p"), k)
                if k >= 2:
                    ve.wait_ge(S("tap"), k - 1)
                own(tt(square(tmp_v[:, 2]), hat[0], im(IMG_PM), ALU.mult))
                own(tt(square(tmp_v[:, 3]), hat[1], im(IMG_PP), ALU.mult))
                own(tt(square(tmp_v[:, 0]), hat[0], im(IMG_XM), ALU.mult))
                own(tt(square(tmp_v[:, 1]), hat[1], im(IMG_XP), ALU.mult))
                own.sync(own.n - 2)
                own(tt(tmp_v[:, 2], tmp_v[:, 2], tmp_v[:, 3], ALU.add))
                own.sync(own.n - 1)
                tt(term[:, k % 2, 0], tmp_v[:, 0], tmp_v[:, 1], ALU.add).then_inc(S("term_a"), 1)
                own.sync()
                own(tt(square(tmp_v[:, 3]), square(tmp_v[:, 2]), im(IMG_YP), ALU.add))
                own.sync()
                tt(term[:, k % 2, 2], hats[:, k % 2, 3], tmp_v[:, 3], ALU.mult).then_inc(S("term_p"), 1)
                if k == 3:
                    ve.wait_ge(S("absd"), NCHK)
                    own(ve.tensor_reduce(far[0:CHK, 0:NCHK], absd, AX.X, ALU.max))
                    own.sync()
                    ve.tensor_reduce(far[0:CHK, 3:4], far[0:CHK, 0:NCHK], AX.X, ALU.max).then_inc(S("far"), 1)
                if k == 7:
                    ve.wait_ge(S("far_t"), 1)
                    own(ve.tensor_reduce(small[0:1, 60:61], ps[0:1, 6, 0:CHK], AX.X, ALU.max))
                    own.sync()
                    ve.tensor_scalar(is_far[:], small[0:1, 60:61], 1.0, None, ALU.is_gt).then_inc(S("is_far"), 1)
            ve.wait_ge(S("is_far"), 1)
            with ve.If(ve.value_load(is_far[:], min_val=0, max_val=1) >= 1):
                ve.wait_ge(S("tap"), TAPS)
                ve.wait_ge(S("far_loaded"), FAR_LOADS)
                ve.memset(far_wst, 0.0).then_inc(S("far_zeroed"), 1)
                ve.wait_ge(S("far_zeroed"), 1)
                raw = w_off_raw.rearrange("p (k q) g -> p k q g", q=2)
                with ve.Fori(0, TAPS) as k:
                    with ve.Fori(0, B) as b:
                        ve.wait_ge(S("far_out"), above(k * (B * CG) + b * CG))
                        ve.wait_ge(S("far_open"), 2)
                        for q in range(2):
                            tt(far_off[:, q], raw[:, bass.ds(k, 1), q].rearrange("p a g -> p g a").to_broadcast([P, G, C]),
                               bmask[:, bass.ds(b, 1)].unsqueeze(2).to_broadcast([P, G, C]), ALU.mult).then_inc(S("far_off"), 1)
                        ve.wait_ge(S("far_d"), above(k * B + b + 1))
                        ve.wait_ge(S("far_open"), 2)
                        for q in range(2):
                            ve.scalar_tensor_tensor(out=far_hat[:, q], in0=bank2(2 * q), scalar=far_b[:, bass.ds(k * 2 + q, 1)],
                                                    in1=far_grid[:, q], op0=ALU.add, op1=ALU.add).then_inc(S("far_pos"), 1)
                        for a in range(CG):
                            at = k * (B * CG) + b * CG + a
                            ve.wait_ge(S("far_out"), above(at))
                            ve.wait_ge(S("far_open"), 2)
                            tt(far_xst, far_img[:, bass.ds(b, 1), a].to_broadcast([P, G, C]),
                               bmask[:].unsqueeze(2).to_broadcast([P, G, C]), ALU.mult).then_inc(S("far_st"), 1)
                            tt(far_wst, far_w[:, a, bass.ds(k, 1), :].to_broadcast([P, B, C]),
                               bsel[:, bass.ds(b, 1), :].rearrange("p z b -> p b z").to_broadcast([P, B, C]), ALU.mult).then_inc(S("far_st"), 1)
                            ve.wait_ge(S("far_q"), above(at + 1))
                            ve.wait_ge(S("far_hat"), above(k * (2 * B) + b * 2 + 2))
                            tt(far_prod, bank2(6), far_hat[:, 1], ALU.mult).then_inc(S("far_prod"), 1)
                ve.wait_ge(S("far_out"), above(TAPS * B * CG))
                ve.memset(far_wst, 0.0).then_inc(S("far_rezeroed"), 1)
            ve.wait_ge(S("deform"), 1)
            own(ve.scalar_tensor_tensor(out=x1[:], in0=bank2(4), scalar=0.0, in1=x0[:], op0=ALU.max, op1=ALU.add))
            own.sync()
            ve.transpose(x1t[:].rearrange("p (c h) -> p h c", h=C), x1[:].rearrange("p (h w) -> p h w", w=C)).then_inc(S("x1t"), 1)
            ve.wait_ge(S("x1t"), 1)

            def normalize(x, name):
                for h in range(2):
                    own(ve.bn_stats(small[:, 8 + 6 * h:14 + 6 * h], x[:, HALF * h:HALF * h + HALF]))
                own.sync()
                own(ve.bn_aggr(small[:, 20:22], small[:, 8:20]))
                own.sync()
                ve.tensor_scalar(small[:, 22:23], small[:, 21:22], 1e-5, None, ALU.add).then_inc(S(name + "_var"), 1)
                ve.wait_ge(S(name + "_std"), 1)
                own(ve.reciprocal(small[:, 24:25], small[:, 23:24]))
                own.sync()
                ve.tensor_scalar(xn[:], x[:], small[:, 20:21], small[:, 24:25], ALU.subtract, ALU.mult).then_inc(S(name), 1)

            normalize(x1t, "xn2")
            ve.wait_ge(S("v"), 2)
            for h in range(2):
                ve.tensor_copy(vt[:, 4 * h:4 * h + 4].rearrange("p a n -> p (a n)"), ps[:, 6 + h, :]).then_inc(S("qkv_copied"), 1)
            ve.wait_ge(S("qkv_copied"), 4)
            ve.wait_ge(S("vz_cleared"), 1)

            def place_values(b):
                ve.wait_ge(S("pv"), above(b * NUNIT))
                ve.wait_ge(s_zero, 1)
                for n in range(NH):
                    last = ve.tensor_copy(vz[:, :, n, 0, HD * n:HD * n + HD], vt[:, :, bass.ds(b * C + HD * n, HD)])
                last.then_inc(S("vz"), 1)

            def mask_q(b, n):
                ve.wait_ge(S("sc"), above(b * NUNIT + NBLK * (n - 1) if n else 0))
                ve.tensor_scalar(qz[:, n % 2], qt, qmask[:, bass.ds(b * NH + n, 1)], None, ALU.mult).then_inc(S("qz"), 1)

            def copy_turned(b, t):
                w = P * len(key_tiles(units[t % NUNIT][1])[0])
                ve.wait_ge(S("turned"), above(b * NUNIT + (t + 1)))
                ve.wait_ge(S("pv"), above(b * NUNIT + (t - NSB + 1)))
                ve.tensor_copy(pt[:, t % NSB, 0:w], ps[:, (2, 3, 7)[t % NUNIT % 3], 0:w]).then_inc(S("pt_v"), 1)

            def attend(b, first):
                for t in range(NUNIT):
                    n, i = units[t]
                    if t == LAG_PV and not first:
                        place_values(b)
                    ve.wait_ge(S("sc"), above(b * NUNIT + (t + 1)))
                    ve.wait_ge(S("pexp"), above(b * NUNIT + (t - NSB + 1)))
                    if (t - LAG_COPY) % 2 == 0 and (t >= LAG_COPY or not first):
                        copy_turned(b, t - LAG_COPY)
                    else:
                        ve.tensor_copy(small[:, 50 + t % 8:51 + t % 8], qmask[:, 0:1])
                    tiles, off, (lo, hi) = key_tiles(i)
                    ve.tensor_tensor_reduce(sc[:, t % NSB, lo:hi], ps[:, (0, 1, 6)[t % 3], lo:hi], bias[n][:, off + lo:off + hi],
                                            1.0, 4 * BIG, ALU.add, ALU.min, nmax[:, t % NSB:t % NSB + 1]).then_inc(S("neg"), 1)
                    if t % NBLK == 1:
                        mask_q(b, n + 1)

            mask_q(0, 0)
            place_values(0)
            ve.wait_ge(S("bias_negated"), NH)
            attend(0, True)
            with ve.Fori(1, B) as b:
                attend(b, False)
            for t in range(LAG_COPY):
                if (t - LAG_COPY) % 2 == 0:
                    copy_turned(B, t - LAG_COPY)
            ve.wait_ge(s_ld["ot"], 16 * 2 * B)
            own(ve.reciprocal(os, os))
            own.sync()
            own(tt(ot, ot, os, ALU.mult))
            own.sync()
            ve.tensor_scalar(ot, ot, b_attn[:, 2:3], None, ALU.add).then_inc(S("attended"), 1)
            ve.wait_ge(S("proj"), 1)
            ve.scalar_tensor_tensor(out=x2t[:], in0=bank2(0), scalar=b_attn[:, 3:4], in1=x1t[:], op0=ALU.add, op1=ALU.add).then_inc(S("x2t"), 1)
            ve.wait_ge(S("x2t"), 1)

            normalize(x2t, "xn3")
            ve.wait_ge(s_ld["mamba"], MAMBA_LOADS)
            own(ve.memset(xs[:, :, 0:KC - 1], 0.0))
            ve.wait_ge(S("xz"), 2)
            own.sync()
            for t in range(DP):
                dr, p = divmod(t, PAIRS)
                src = bank2(2 * p)
                dst = xs[:, t % 2, KC - 1:KC - 1 + T]
                if dr == 1:
                    src = src[:, ::-1]
                elif dr == 2:
                    dst = dst.rearrange("p (m s) -> p m s", s=SLICES)
                    src = src.rearrange("p (s m) -> p m s", s=SLICES)
                ve.tensor_copy(dst, src).then_inc(S("xs"), 1)
                ve.wait_ge(S("xs"), t + 1)
                a = acc_c[:, t % 2]
                if t >= 2:
                    ve.wait_ge(S("u"), t - 1)
                own(ve.tensor_scalar(a, xs[:, t % 2, 0:T], par[:, dr, 0:1], par[:, dr, KC:KC + 1], ALU.mult, ALU.add))
                for k in range(1, KC):
                    own.sync()
                    last = ve.scalar_tensor_tensor(out=a, in0=xs[:, t % 2, k:k + T], scalar=par[:, dr, k:k + 1], in1=a,
                                                   op0=ALU.mult, op1=ALU.add)
                    if k < KC - 1:
                        own(last)
                last.then_inc(S("conv1d"), 1)
                ve.wait_ge(S("conv1d"), t + 1)
            for t in range(DP):
                dr, p = divmod(t, PAIRS)
                for w, dst in enumerate((split_b, split_c)):
                    ve.wait_ge(S("hi"), 2 * t + w + 1)
                    if t:
                        own.sync()
                    r96 = res96[0:96, w]
                    tt(r96, bank2(2 * w)[0:96], dst[:, t], ALU.subtract).then_inc(S("bc_read"), 1)
                    ve.wait_ge(S("bc_read"), 2 * t + w + 1)
                    own(ve.tensor_copy(dst[32:64, t], r96[32:64]))
                    mid = mid96[64:96, w, 0:T // 2].bitcast(BF16)
                    own(ve.tensor_copy(mid, r96[64:96]))
                    own.sync()
                    own(tt(dst[64:96, t], r96[64:96], mid, ALU.subtract))
                ve.wait_ge(S("dtf"), t + 1)
                ve.wait_ge(S("e_dt"), t + 1)
                ve.tensor_scalar(delta[:, t], bank2(6), par[:, dr, KC + 1:KC + 2], 0.0, ALU.add, ALU.max).then_inc(S("relu_dt"), 1)
                ve.wait_ge(S("one_e"), t + 1)
                e, l = sp[0][:, t % 2], sp[1][:, t % 2]
                ve.scalar_tensor_tensor(out=e, in0=l, scalar=-1.0, in1=e, op0=ALU.add, op1=ALU.subtract).then_inc(S("round_e"), 1)
                ve.wait_ge(S("ln"), t + 1)
                ve.wait_ge(S("relu_dt"), t + 1)
                own(tt(delta[:, t], delta[:, t], sp[1][:, t % 2], ALU.add))
                own.sync()
                own(tt(delta[:, t], delta[:, t], sp[0][:, t % 2], ALU.subtract))
                own.sync()
                tt(du[:, t], delta[:, t], u[:, dr, p], ALU.mult).then_inc(S("du"), 1)
            ve.wait_ge(S("du"), DP)

            def inject(t, n):
                ve.wait_ge(S("b_rep"), above(t * NS + (n + 1)))
                ve.wait_ge(S("scan"), above(t * NS + (n - 1)))
                ve.wait_ge(s_zero, 1)
                tt(dbu[:, n % 2], du[:, t], bank2(2 * (n % 2)), ALU.mult).then_inc(S("dbu"), 1)

            def scan(t, n):
                ve.wait_ge(S("da"), above(t * NS + (n + 1)))
                ve.wait_ge(S("dbu"), above(t * NS + (n + 1)))
                ve.wait_ge(S("hc"), above(t * NS + (n - RING + 1)))
                ve.tensor_tensor_scan(hs_ring[n % RING], da[:, n % 2], dbu[:, n % 2], 0.0, ALU.mult, ALU.add).then_inc(S("scan"), 1)

            def read_y(t):
                ve.wait_ge(S("y_acc"), above((t + 1) * NS))
                ud = u.rearrange("p d q t -> p (d q) t")[:, t]
                ve.wait_ge(s_zero, 1)
                ve.scalar_tensor_tensor(out=ud, in0=ud, scalar=d_col[:].rearrange("p d q -> p (d q)")[:, bass.ds(t, 1)],
                                        in1=bank2(6), op0=ALU.mult, op1=ALU.add).then_inc(S("y_read"), 1)

            def states(t, first):
                inject(t, 0)
                for n in range(NS):
                    if n + 1 < NS:
                        inject(t, n + 1)
                    scan(t, n)
                    if n == 1 and not first:
                        read_y(t - 1)

            states(0, True)
            with ve.Fori(1, DP) as t:
                states(t, False)
            read_y(DP - 1)
            ve.wait_ge(S("y_read"), above(DP))
            for p in range(PAIRS):
                own(tt(u[:, 0, p], u[:, 0, p], u[:, 1, p, ::-1], ALU.add))
                own.sync()
                y0 = u[:, 0, p].rearrange("p (s m) -> p m s", s=SLICES)
                own(tt(y0, y0, u[:, 2, p].rearrange("p (m s) -> p m s", s=SLICES), ALU.add))
                own.sync()
                tt(u[:, 0, p], u[:, 0, p], zs[:, p], ALU.mult).then_inc(S("gated"), 1)
            ve.wait_ge(S("mamba"), 1)
            tt(x3t[:], bank2(0), x2t[:], ALU.add).then_inc(S("x3t"), 1)
            ve.wait_ge(S("x3t"), 1)

            ve.memset(w_conv, 0.0).then_inc(S("conv_cleared"), 1)
            ve.memset(zero_w, 0.0).then_inc(S("zero_w"), 1)
            own(ve.memset(xpad, 0.0))
            normalize(x3t, "xn4")
            ve.wait_ge(S("xn4"), 1)
            ve.tensor_copy(xpad[:, 1:1 + C, 1:1 + C], xn[:].rearrange("p (h w) -> p h w", w=C)).then_inc(S("xpad"), 1)
            ve.transpose(xrow, xn[:].rearrange("p (r c) -> p c r", c=C)).then_inc(S("xrow"), 1)
            ve.wait_ge(s_ld["conv"], 16 * (B + 2))
            ve.wait_ge(S("conv"), 2)
            for q in range(2):
                for odd in range(2):
                    cols = slice(HALF * odd, HALF * odd + HALF)
                    last = ve.scalar_tensor_tensor(out=coord[:, q, cols], in0=bank2(2 * odd)[:, q::2], scalar=b_conv[:, odd:odd + 1],
                                                   in1=grid[:, q, cols], op0=ALU.add, op1=ALU.add)
            last.then_inc(S("coords_read"), 1)
            ve.wait_ge(S("coords_read"), 1)
            own(ve.tensor_scalar(coord, coord, 0.0, float(C - 1), ALU.max, ALU.min))
            own.sync()
            for q in range(2):
                ve.tensor_copy(chi[:, q], coord[:, q]).then_inc(S("coord_part"), 1)
                ve.wait_ge(S("coord_part"), 3 * q + 1)
                own(tt(coord[:, q], coord[:, q], chi[:, q], ALU.subtract))
                own.sync()
                ve.tensor_copy(cmid[:, q], coord[:, q]).then_inc(S("coord_part"), 1)
                ve.wait_ge(S("coord_part"), 3 * q + 2)
                tt(clo[:, q], coord[:, q], cmid[:, q], ALU.subtract).then_inc(S("coord_part"), 1)
            with ve.Fori(0, CPER) as j:
                def hat4(t):
                    ve.wait_ge(S("abs"), above(j * NT + (t + 1)))
                    ve.wait_ge(S("rowmix"), above(j * NT + t - 1))
                    ve.wait_ge(S("prod"), above(j * NT + t - 1))
                    ve.tensor_scalar(nhat[:, t % 2], ahat[:, t % 2], 1.0, 1.0, ALU.min, ALU.subtract).then_inc(S("nhat"), 1)

                def product(t):
                    ve.wait_ge(S("rowmix"), above(j * NT + (t + 1)))
                    ve.wait_ge(S("nhat"), above(j * NT + (t + 1)))
                    ve.wait_ge(S("gath"), above(j * NT + t - 1))
                    tt(prod[:, t % 2], ps[:, 4 + t % 2, :], nhat[:, t % 2, 1], ALU.mult).then_inc(S("prod"), 1)

                for t in range(NT + 1):
                    if t < NT:
                        hat4(t)
                    if t >= 1:
                        product(t - 1)
            ve.wait_ge(S("mapped"), 1)
            for h in range(2):
                cols = slice(HALF * h, HALF * h + HALF)
                own(tt(y4[:, cols], ps[:, 6 + h, :], x3t[:, cols], ALU.add))
                own.sync()
                ve.transpose(yout[:, cols], y4[:, cols]).then_inc(S("yout"), 1)

        @block.scalar
        def _(ac):
            for name in LOOPED["scalar"].split():
                ac.sem_inc(S(name), LEAD)
            own = Tally(ac, a_own)
            ac.wait_ge(S("var1e"), 1)
            ac.activation(stat1[:, 1], stat1[:, 0], ACT.Sqrt).then_inc(S("std1"), 1)
            ac.wait_ge(s_ld["off"], OFF_LOADS)
            ac.wait_ge(S("b_off_neg"), 1)
            for k in range(TAPS):
                if k == TAPS - 1:
                    ac.wait_ge(s_ld["bias"], 16 * QROWS * 3 * NH)
                    for n in range(NH):
                        ac.mul(bias[n], bias[n], -1.0).then_inc(S("bias_negated"), 1)
                if k == 1:
                    for m in range(NCHK):
                        ac.wait_ge(S("chk"), m + 1)
                        ac.activation(absd[:, m], bank2(6)[0:CHK], ACT.Abs, bias=b_chk[:, m:m + 1]).then_inc(S("absd"), 1)
                ac.wait_ge(S("off"), k + 1)
                if k >= 2:
                    ac.wait_ge(S("term_m"), k - 1)
                    ac.wait_ge(S("term_p"), k - 1)
                for j, (q, sign) in enumerate(((1, -1.0), (1, 1.0), (0, -1.0), (0, 1.0))):
                    col = (b_off if sign > 0 else b_off_neg)[:, 2 * k + q:2 * k + q + 1]
                    ac.activation(hats[:, k % 2, j], bank2(2 * q), ACT.Relu, bias=col, scale=sign).then_inc(S("hats"), 1)

            ac.wait_ge(S("is_far"), 1)
            with ac.If(ac.value_load(is_far[:], min_val=0, max_val=1) >= 1):
                with ac.Fori(0, TAPS) as k:
                    with ac.Fori(0, B) as b:
                        for q in range(2):
                            ac.wait_ge(S("far_pos"), above(k * (2 * B) + b * 2 + (q + 1)))
                            ac.wait_ge(S("is_far"), 1)
                            ac.activation(far_hat[:, q], far_hat[:, q], ACT.Abs, bias=far_tap[:, bass.ds(k * 2 + q, 1)]).then_inc(S("far_abs"), 1)
                            ac.wait_ge(S("far_abs"), above(k * (2 * B) + b * 2 + (q + 1)))
                            ac.activation(far_hat[:, q], far_hat[:, q], ACT.Relu, bias=1.0, scale=-1.0).then_inc(S("far_hat"), 1)

            def root(name):
                ac.wait_ge(S(name + "_var"), 1)
                ac.activation(small[:, 23:24], small[:, 22:23], ACT.Sqrt).then_inc(S(name + "_std"), 1)

            root("xn2")
            ac.wait_ge(s_ld["attn"], ATTN_LOADS)
            for m, dst in enumerate((qt, kt)):
                ac.wait_ge(S("qk"), m + 1)
                ac.activation(dst, bank2(2 * m), ACT.Identity, bias=b_attn[:, m:m + 1]).then_inc(S("qkv_copied"), 1)

            def copy_turned(b, t):
                w = P * len(key_tiles(units[t % NUNIT][1])[0])
                ac.wait_ge(S("turned"), above(b * NUNIT + (t + 1)))
                ac.wait_ge(S("pv"), above(b * NUNIT + (t - NSB + 1)))
                ac.activation(pt[:, t % NSB, 0:w], ps[:, (2, 3, 7)[t % NUNIT % 3], 0:w], ACT.Copy).then_inc(S("pt_a"), 1)

            def copy_sums(b):
                ac.wait_ge(S("pv"), above(b * NUNIT + NUNIT))
                ac.wait_ge(s_ld["attn"], ATTN_LOADS)
                ac.activation(ot_b[:, b, :], bank2(4)[0:2 * C], ACT.Copy).then_inc(S("ot_b"), 1)

            def attend(b, first):
                for t in range(NUNIT):
                    lo, hi = key_tiles(units[t][1])[2]
                    if t == LAG_PV and not first:
                        copy_sums(b - 1)
                    ac.wait_ge(S("neg"), above(b * NUNIT + (t + 1)))
                    ac.wait_ge(S("turned"), above(b * NUNIT + (t - NSB + 1)))
                    ac.activation(pexp[:, pexp_buffer(t), lo:hi], sc[:, t % NSB, lo:hi], ACT.Exp, bias=nmax[:, t % NSB:t % NSB + 1],
                                  scale=-1.0).then_inc(S("pexp"), 1)
                    if (t - LAG_COPY) % 2 and (t >= LAG_COPY or not first):
                        copy_turned(b, t - LAG_COPY)

            ac.wait_ge(S("pexp_cleared"), 1)
            attend(0, True)
            with ac.Fori(1, B) as b:
                attend(b, False)
            for t in range(LAG_COPY):
                if (t - LAG_COPY) % 2:
                    copy_turned(B, t - LAG_COPY)
            copy_sums(B - 1)

            root("xn3")
            for p in range(PAIRS):
                ac.wait_ge(S("xz"), 3 + p)
                ac.activation(zs[:, p], bank2(4 + 2 * p), ACT.Silu).then_inc(S("zs"), 1)
            for t in range(DP):
                dr, p = divmod(t, PAIRS)
                ac.wait_ge(S("conv1d"), t + 1)
                ac.activation(u[:, dr, p], acc_c[:, t % 2], ACT.Silu).then_inc(S("u"), 1)
            a_all = a_col[:].rearrange("p d q n -> p (d q n)")
            ac.wait_ge(S("a_log"), PAIRS)
            own(ac.activation(a_all, a_all, ACT.Exp))
            own.sync()
            ac.mul(a_all, a_all, -1.0).then_inc(S("a_neg"), 1)
            for t in range(DP):
                dr, p = divmod(t, PAIRS)
                for w, dst in enumerate((split_b, split_c)):
                    ac.wait_ge(S("bc"), 2 * t + w + 1)
                    ac.activation(dst[:, t], bank2(2 * w)[0:96], ACT.Copy).then_inc(S("hi"), 1)
                ac.wait_ge(S("dtr"), t + 1)
                ac.activation(dt_raw, bank2(4)[0:2 * RANK], ACT.Copy).then_inc(S("dtr_copied"), 1)
                ac.wait_ge(S("dtf"), t + 1)
                if t >= 2:
                    ac.wait_ge(S("du"), t - 1)
                e, l = sp[0][:, t % 2], sp[1][:, t % 2]
                own(ac.activation(l, bank2(6), ACT.Abs, bias=par[:, dr, KC + 1:KC + 2]))
                own.sync()
                ac.activation(e, l, ACT.Exp, scale=-1.0).then_inc(S("e_dt"), 1)
                ac.wait_ge(S("round_e"), t + 1)
                ac.activation(l, l, ACT.Ln).then_inc(S("ln"), 1)
            ac.wait_ge(S("du"), DP)
            ac.wait_ge(S("a_neg"), 1)
            with ac.Fori(0, DP) as t:
                for n in range(NS):
                    ac.wait_ge(S("scan"), above(t * NS + (n - 1)))
                    ac.wait_ge(S("a_neg"), 1)
                    ac.activation(da[:, n % 2], delta[:, t], ACT.Exp, scale=a_all[:, bass.ds(t * NS + n, 1)]).then_inc(S("da"), 1)
                    ac.wait_ge(S("c_rep"), above(t * NS + (n + 1)))
                    ac.wait_ge(S("hc"), above(t * NS + (n - RING + 1)))
                    ac.activation(c_ring[n % RING], bank2(4), ACT.Copy).then_inc(S("c_copied"), 1)

            root("xn4")
            ac.wait_ge(S("nycol"), 1)
            with ac.Fori(0, CPER) as j:
                for t in range(NT):
                    ac.wait_ge(S("crep"), above(j * NT + (t + 1)))
                    ac.wait_ge(S("nhat"), above(j * NT + t - 1))
                    ac.activation(ahat[:, t % 2].rearrange("p q n -> p (q n)"), bank2(2 * (t % 2)), ACT.Abs,
                                  bias=nycol[:, 0:1]).then_inc(S("abs"), 1)

        @block.gpsimd
        def _(gp):
            for name in LOOPED["gpsimd"].split():
                gp.sem_inc(S(name), LEAD)
            own = Tally(gp, g_own)

            def mul(o, a, b):
                return gp.tensor_tensor(o, a, b, ALU.mult)

            def add(o, a, b):
                return gp.tensor_tensor(o, a, b, ALU.add)

            gp.wait_ge(s_ld["off"], OFF_LOADS)
            own(gp.tensor_scalar(b_off_neg, b_off, -1.0, None, ALU.mult))
            own.sync()
            gp.memset(w_off, 0.0).then_inc(S("b_off_neg"), 1)
            gp.wait_ge(S("b_off_neg"), 1)
            wo = w_off.rearrange("p k q b g c -> p (k q) b g c")
            for b in range(B):
                q = slice(C * b, C * b + C)
                gp.tensor_copy(wo[q, :, b], w_off_raw[q].unsqueeze(3).to_broadcast([C, 2 * TAPS, G, CG])).then_inc(S("w_off"), 1)
                gp.wait_ge(S("w_off"), b + 1)
            own(gp.memset(w_xp[:], 0.0))
            own(gp.memset(w_xd[:], 0.0))
            gp.wait_ge(S("diffs"), 1)
            for k in range(TAPS):
                ky, kx = divmod(k, 3)

                def im(kind):
                    return img[:, kind, ky + 1:ky + 1 + C, kx + 1:kx + 1 + C]

                def square(a):
                    return a.rearrange("p (h w) -> p h w", w=C)

                gp.wait_ge(S("hats"), 4 * (k + 1))
                if k:
                    gp.wait_ge(S("term_m"), k)
                own(mul(square(tmp_p[:, 0]), square(hats[:, k % 2, 0]), im(IMG_MM)))
                own(mul(square(tmp_p[:, 1]), square(hats[:, k % 2, 1]), im(IMG_MP)))
                own.sync()
                own(add(tmp_p[:, 0], tmp_p[:, 0], tmp_p[:, 1]))
                own.sync()
                own(add(square(tmp_p[:, 1]), square(tmp_p[:, 0]), im(IMG_YM)))
                own.sync()
                if k >= 2:
                    gp.wait_ge(S("tap"), k - 1)
                mul(term[:, k % 2, 1], hats[:, k % 2, 2], tmp_p[:, 1]).then_inc(S("term_m"), 1)

            gp.wait_ge(S("x1t"), 1)
            gp.memset(pexp, 0.0).then_inc(S("pexp_cleared"), 1)
            own(gp.memset(vz, 0.0))
            own.sync()
            for n in range(NH):
                last = gp.memset(vz[:, :, n, 1, HD * n:HD * n + HD], 1.0)
            last.then_inc(S("vz_cleared"), 1)

            gp.wait_ge(s_ld["mamba"], MAMBA_LOADS)
            own.sync()
            for j in range(2):
                r = slice(DI * j, DI * j + DI)
                for w in range(2):
                    raw = xp_raw[r, :, RANK + NS * w:RANK + NS * w + NS]
                    for k in range(3):
                        gp.tensor_copy(w_xp[r, :, w, k, j, :], raw).then_inc(S("w_xp"), 1)
                gp.tensor_copy(w_xd[r, :, j, :], xp_raw[r, :, 0:RANK]).then_inc(S("w_xp"), 1)
                gp.wait_ge(S("w_xp"), 7 * (j + 1))
            for p in range(PAIRS):
                own(gp.tensor_copy(d_col[:, :, p:p + 1], par[:, :, KC + 2:KC + 3]))
                gp.tensor_copy(a_col[:, :, p, :], par[:, :, KC + 3:]).then_inc(S("a_log"), 1)
            gp.tensor_scalar(nycol[:], ycol[:], -1.0, None, ALU.mult).then_inc(S("nycol"), 1)
            for t in range(DP):
                e, l = sp[0][:, t % 2], sp[1][:, t % 2]
                gp.wait_ge(S("e_dt"), t + 1)
                gp.tensor_scalar(l, e, 1.0, None, ALU.add).then_inc(S("one_e"), 1)
            gp.wait_ge(S("du"), DP)
            with gp.Fori(0, DP) as t:
                for n in range(NS):
                    gp.wait_ge(S("scan"), above(t * NS + (n + 1)))
                    gp.wait_ge(S("c_copied"), above(t * NS + (n + 1)))
                    gp.wait_ge(S("y_acc"), above(t * NS + (n - RING + 1)))
                    gp.wait_ge(S("du"), DP)
                    mul(hc_ring[n % RING], hs_ring[n % RING], c_ring[n % RING]).then_inc(S("hc"), 1)

            gp.wait_ge(S("xrow"), 1)
            gp.wait_ge(s_ld["b4"], 32)
            with gp.Fori(0, CPER) as j:
                for g in range(CGRP):
                    gp.wait_ge(S("gath"), above(j * NT + 2 * (g - 1)))
                    gp.wait_ge(S("xrow"), 1)
                    gp.tensor_tensor(xstat[:, g % 2],
                                     xrow[:, :, bass.ds(j + CPER * g, 1)].rearrange("p x a -> p a x").to_broadcast([P, B, C]),
                                     bmask[:].unsqueeze(2).to_broadcast([P, B, C]), ALU.mult).then_inc(S("stat"), 1)
                    gp.tensor_copy(ostat[:, g % 2], chsel[:, :, bass.ds(C - 1 - CPER * g - j, C)]).then_inc(S("stat"), 1)
    return nc


def constants():
    import numpy as np

    p = np.arange(P)
    quad, low = p // C, p % C
    same = quad[:, None] == quad[None, :]
    c = {
        "c_ident": np.eye(P, dtype=np.float32),
        "c_ones": (same / float(T)).astype(np.float32),
        "c_far": np.full((NH * 13, T), -BIG, np.float32),
        "c_ycol": low[:, None].astype(np.float32),
        "c_bmask": (quad[:, None] == np.arange(B)[None, :]).astype(np.float32),
        "c_grid": np.stack([np.arange(T) // C, np.arange(T) % C]).astype(np.float32),
    }
    sel_b = np.broadcast_to(np.eye(B, dtype=np.float32), (P, B, B))
    c["c_bsel"] = sel_b.astype(np.float32)
    tap = np.stack([np.arange(TAPS) // 3 - 1, np.arange(TAPS) % 3 - 1], 1).reshape(-1)
    c["c_tap"] = (tap[None, :] - low[:, None]).astype(np.float32)
    head = (quad[:, None] * NH + low[:, None] // HD) == np.arange(B * NH)[None, :]
    head = np.concatenate([head, np.zeros((P, 1), bool)], 1)
    c["c_qmask"] = (head * -(float(HD) ** -0.5)).astype(np.float32)
    r = np.arange(96)
    batch, state = (r % 32) // NS, r % NS
    sel = (state[:, None, None] == np.arange(NS)[None, :, None]) & (batch[:, None, None] == (p // DI)[None, None, :])
    one = np.uint16(0x3F80)
    c["c_sel"] = sel.reshape(96, NS * P) * one
    q, rb, rg = r // 48, (r % 16) // CGRP, r % CGRP
    selc = ((rg[:, None, None, None] == np.arange(CGRP)[None, :, None, None])
            & (q[:, None, None, None] == np.arange(2)[None, None, :, None])
            & (rb[:, None, None, None] == quad[None, None, None, :]))
    c["c_selc"] = selc.reshape(96, CGRP * 2 * P) * one
    chsel = np.zeros((P, B, 2 * C - 1), np.float32)
    chsel[p, quad, C - 1] = 1.0
    c["c_chsel"] = chsel.reshape(P, -1)
    return c


def laid_out(i):
    import numpy as np

    a = {k: np.asarray(v) for k, v in i.items()}
    sfx = ("", "_b", "_s")
    cols = [np.stack([a["L2_conv_conv_w" + x] for x in sfx], 1)]
    for name in ("conv_b", "dt_proj_b", "D"):
        cols.append(np.stack([a["L2_conv_" + name + x] for x in sfx], 1)[:, :, None])
    cols.append(np.stack([a["L2_conv_A_log" + x] for x in sfx], 1))
    m = {
        "x": a["x"].reshape(P, T),
        "woff": a["L0_conv_w_off"].reshape(G, TAPS * 2, C).transpose(2, 1, 0).reshape(C, TAPS * 2 * G),
        "boff": a["L0_conv_b_off"].reshape(G, TAPS * 2),
        "bchk": np.broadcast_to(a["L0_conv_b_off"].reshape(1, G, 3, 6).transpose(3, 0, 1, 2), (6, B, G, 3)).reshape(6 * B * G, 3),
        "wdef": a["L0_conv_w_def"].reshape(C, C, TAPS).transpose(1, 2, 0),
        "wqkv": a["L1_conv_w_qkv"], "bqkv": a["L1_conv_b_qkv"], "rpb": a["L1_conv_rpb"],
        "wproj": a["L1_conv_w_proj"], "bproj": a["L1_conv_b_proj"],
        "win": a["L2_conv_in_proj_w"].T,
        "par": np.concatenate(cols, 2),
        "xproj": np.stack([a["L2_conv_x_proj_w" + x].T for x in sfx], 1),
        "dtw": np.stack([a["L2_conv_dt_proj_w" + x].T for x in sfx], 1),
        "wout": a["L2_conv_out_proj_w"].T,
        "wconv": a["L3_conv_W"].reshape(9, C, C, 2).transpose(1, 0, 3, 2),
        "bconv": a["L3_conv_b"].reshape(C, 2),
    }
    m.update(constants())
    return {k: np.ascontiguousarray(v) for k, v in m.items()}


def kernel(**inputs):
    import numpy as _np
    import concourse.bacc as _bacc
    from concourse import mybir as _mybir
    from concourse.bass_utils import run_bass_kernel_spmd as _run

    nc = _bacc.Bacc("TRN2", target_bir_lowering=False, num_devices=1)
    arrays, d = {}, {}
    for name, a in laid_out(inputs).items():
        arrays[f"in_{name}"] = a
        d[name] = nc.dram_tensor(f"in_{name}", a.shape, _mybir.dt.from_np(a.dtype), kind="ExternalInput").ap()
    out = nc.dram_tensor("out_0", (B, C, C, C), _mybir.dt.float32, kind="ExternalOutput").ap()
    build(nc, d, out)
    return _run(nc, [arrays], core_ids=[0]).results[0]["out_0"]
```

```python
from contextlib import ExitStack

import concourse.bass as bass
from concourse import mybir
from concourse.alu_op_type import AluOpType as ALU

ACT = mybir.ActivationFunctionType
F32 = mybir.dt.float32
BF16 = mybir.dt.bfloat16
I32 = mybir.dt.int32
U16 = mybir.dt.uint16
AX = mybir.AxisListType

P = 128
B = 4
C = 32
T = C * C
HALF = 512
BIG = 1e30

G, CG, TAPS = 4, 8, 9
PAD = 2
W1 = C + 2 * PAD

NCHK = 3
KQ = 2 * TAPS // NCHK
CHK = KQ * B * G

NH, HD, WIN = 4, 8, 7
QROWS = 4
NBLK = C // QROWS
EDGE, INNER = 2 * P, 3 * P
NSB = 4
BIASW = EDGE + INNER + EDGE
PARTS = 3
PROD = PARTS * PARTS * HD
QH = 2

DI, NS, KC, RANK = 64, 16, 4, 2
DIRS, PAIRS = 3, 2
DP = DIRS * PAIRS
NPAR = KC + 3 + NS
SLICES = 16

CGRP, CPER = 4, 8


def key_tiles(i):
    lo, hi = max(i - 1, 0), min(i + 1, NBLK - 1)
    off = 0 if i == 0 else (EDGE if i < NBLK - 1 else EDGE + INNER)
    near = (0, EDGE) if hi - lo == 1 else (P - C * (WIN // 2), 2 * P + C * (WIN // 2))
    return list(range(lo, hi + 1)), off, near


def seeing(i):
    tiles, _, _ = key_tiles(i)
    spans = [(0, P)] * 2 if len(tiles) == 2 else [(0, P - C), (0, P), (C, P)]
    at, out = 0, []
    for q0, q1 in spans:
        out.append((at, at + q1 - q0, q0, q1))
        at += q1 - q0
    return out


LEAD = 4
LOOPED = {
    "tensor": "sc turned pv b_rep c_rep y_acc crep rowmix prod_turned far_d far_q far_out",
    "vector": "neg pt_v vz dbu scan nhat prod summed far_off far_pos far_st far_prod",
    "scalar": "ot_b pexp pt_a c_copied da y_turned abs hat_y far_hat far_abs",
    "gpsimd": "hc stat",
}


def above(n):
    return n + LEAD


class Tally:

    def __init__(self, eng, sem):
        self.eng, self.sem, self.n = eng, sem, 0

    def __call__(self, ins):
        self.n += 1
        ins.then_inc(self.sem, 1)
        return self.n

    def sync(self, n=None):
        self.eng.wait_ge(self.sem, self.n if n is None else n)


def build(nc, d, out):
    with ExitStack() as ctx:
        def sb(name, shape, dt=F32):
            return ctx.enter_context(nc.sbuf_tensor(name, shape, dt))

        def sem(name):
            return ctx.enter_context(nc.semaphore(name))

        ps = ctx.enter_context(nc.psum_tensor("ps", [P, 8, HALF], F32))

        def bank2(i):
            return ps[:, i:i + 2, :].rearrange("p a n -> p (a n)")

        x0 = sb("x0", [P, T])
        x1 = sb("x1", [P, T])
        x1t = sb("x1t", [P, T])
        x2t = sb("x2t", [P, T])
        x3t = sb("x3t", [P, T])
        xn = sb("xn", [P, T])
        ident = sb("ident", [P, P])
        ones_b = sb("ones_b", [P, P])
        ycol = sb("ycol", [P, 1])
        nycol = sb("nycol", [P, 1])
        small = sb("small", [P, 64])
        w_attn = sb("w_attn", [P, 4, P])
        b_attn = sb("b_attn", [P, 4])
        w_in = sb("w_in", [P, 4, P])
        w_xp = sb("w_xp", [P, DIRS, 2, 2, NS])
        xp_raw = sb("xp_raw", [P, DIRS, RANK + 2 * NS])
        w_low = sb("w_low", [2 * RANK, DIRS, P])
        w_dt = sb("w_dt", [2 * RANK, DIRS, P])
        w_step = sb("w_step", [P, DIRS, P])
        w_out = sb("w_out", [P, PAIRS, P])
        par = sb("par", [P, DIRS, NPAR])
        a_col = sb("a_col", [P, DIRS, PAIRS, NS])
        d_col = sb("d_col", [P, DIRS, PAIRS])
        b_conv = sb("b_conv", [P, 2])
        bmask = sb("bmask", [P, B])
        bsel = sb("bsel", [P, B, B])
        far = sb("far", [P, 4])
        is_far = sb("is_far", [1, 1], I32)

        w_conv = sb("w_conv", [P, 9, 2, P])
        grid_x = sb("grid_x", [P, T])
        grid = [x0[:], grid_x[:]]
        selc = w_attn[0:96].rearrange("p m n -> p (m n)").bitcast(BF16)
        selc = selc.rearrange("p (g q m) -> p g q m", g=CGRP, q=2)

        ARENA = 39948
        arena = sb("arena", [P, ARENA])

        class Carve:
            def __init__(self):
                self.at = 0

            def __call__(self, *free, dt=F32, rows=P):
                n = 1
                for f in free:
                    n *= f
                words = n if dt == F32 else (n + 1) // 2
                v = arena[0:rows, self.at:self.at + words]
                self.at += words
                assert self.at <= ARENA, self.at
                if dt != F32:
                    v = v.bitcast(dt)
                if len(free) > 1:
                    names = "abcdef"[:len(free)]
                    v = v.rearrange(f"p ({' '.join(names)}) -> p {' '.join(names)}",
                                    **dict(zip(names, free)))
                return v

        cv = Carve()
        w_off = cv(TAPS, 2, B, G, CG)
        w_off_raw = cv(TAPS * 2, G)
        w_def = cv(TAPS, P)
        b_off = cv(TAPS * 2)
        b_off_neg = cv(TAPS * 2)
        stat1 = cv(3, C)
        img = cv(9, W1, W1)
        hats = cv(2, 4, T)
        term = cv(2, 3, T)
        tmp_v = cv(4, T)
        tmp_p = cv(T)
        tmp_m = cv(2, T)
        xc, sq = tmp_v[:, 0], tmp_v[:, 1]
        absd = cv(NCHK, T, rows=CHK)
        b_chk = cv(NCHK, rows=CHK)
        cv = Carve()
        cv.at = TAPS * 2 * P + TAPS * 2 * G + TAPS * P + 2 * TAPS * 2 + 3 * C + 9 * W1 * W1
        far_grid = cv(2, T)
        far_hat = cv(2, T)
        far_prod = cv(T)
        far_img = cv(B, CG, C)
        far_w = cv(CG, TAPS, C)
        far_b = cv(2 * TAPS)
        far_tap = cv(2 * TAPS)
        far_off = cv(2, G, C)
        far_xst = cv(G, C)
        far_wst = cv(B, C)
        IMG_0, IMG_XM, IMG_XP, IMG_YM, IMG_YP, IMG_MM, IMG_MP, IMG_PM, IMG_PP = range(9)
        cv = Carve()
        qk_full = cv(2, T)
        qk_part = cv(2, PARTS, T, dt=BF16)
        q_rows = cv(B * NH, T, dt=BF16, rows=PROD)
        k_rows = cv(B * NH, T, dt=BF16, rows=PROD)
        vt = cv(NBLK, P)
        vz = cv(NBLK, NH, 2, C)
        sc = cv(NSB, INNER)
        pexp = cv(NSB + 2, INNER)
        pt = cv(NSB, INNER)
        nmax = cv(NSB)
        ot_b = cv(B, T, rows=2 * C)
        ot = cv(T)
        ot_turned = cv(NBLK, B, C)
        rsum = cv(B, NBLK, NH)
        bias = [x2t[:, 0:BIASW], x3t[:, 0:BIASW]]
        bias += [w_conv[:].rearrange("p k a n -> p (k a n)")[:, BIASW * n:BIASW * n + BIASW] for n in range(2)]
        cv = Carve()
        zs = cv(PAIRS, T)
        u = cv(DIRS, PAIRS, T)
        delta = cv(DP, T)
        du = cv(DP, T)
        split_b = cv(DP, T, dt=BF16, rows=96)
        split_c = cv(DP, T, dt=BF16, rows=96)
        sel = cv(NS, P, dt=BF16, rows=96)
        scan_at = cv.at
        da = cv(2, T)
        dbu = cv(2, T)
        hs = cv(2, T)
        c_sb = cv(2, T)
        hc = cv(2, T)
        xs = cv(2, T + 2 * (KC - 1))
        xs_sliced = [v[:, 4:6].rearrange("p t n -> p (t n)")[:, 0:T + KC - 1] for v in (du, delta)]
        w_diag = delta[:, 3, 0:KC * P].rearrange("p (k n) -> p k n", k=KC)
        acc_c = da
        one_e = [c_sb[:, 0], c_sb[:, 1], hc[:, 0], hc[:, 1], hs[:, 0], hs[:, 1]]
        rest = dbu
        parts = [[v[:, HALF * k:HALF * k + HALF].bitcast(BF16) for k in range(2)] for v in (x1, x1t, x3t)]
        spare = w_conv[:].rearrange("p k a n -> p (k a n)")
        dbu_ring = [dbu[:, 0], dbu[:, 1], spare[:, 0:T], spare[:, T:2 * T]]
        RING = 4
        hs_ring = [hs[:, 0], hs[:, 1], xs[:, 0, 0:T], xs[:, 1, 0:T]]
        c_ring = [c_sb[:, 0], c_sb[:, 1], x1[:], x1t[:]]
        hc_ring = [hc[:, 0], hc[:, 1], x3t[:], xn[:]]
        cv = Carve()
        WP = C + 2
        cv.at = scan_at
        xpad = cv(WP, WP)
        xrow = cv(C, C)
        coord = cv(2, T)
        coord_part = [cv(2, T, dt=BF16) for _ in range(3)]
        cv.at = 0
        crow = cv(CPER, T, dt=BF16, rows=96)
        xstat = cv(2, B, C)
        NU = 4
        LAG_MIX, LAG_POS, LAG_SUM = 2, 3, 3
        ahat = cv(NU, 2, HALF)
        nhat = cv(NU, 2, HALF)
        prod = cv(NU, HALF)
        sampled = cv(NBLK, B, C)
        yout = cv(NBLK, B, C)
        assert cv.at <= scan_at

        xn_rows = nc.dram_tensor("xn_rows", (P, C, C), F32, kind="Internal").ap()
        rpb_pad = nc.dram_tensor("rpb_pad", (NH, 13, C, C), F32, kind="Internal").ap()

        s_ld = {k: sem("ld_" + k) for k in
                ("x", "off", "def", "attn", "mamba", "conv", "pad", "rpb", "fill", "bias", "qk0", "qk1",
                 "sel", "parts0", "parts1", "parts2", "b4", "rows")}
        s_zero = sem("weights_zeroed")
        v_own, a_own, g_own = sem("vector_own"), sem("scalar_own"), sem("gpsimd_own")
        s = {}

        def S(name):
            if name not in s:
                s[name] = sem(name)
            return s[name]

        OFF_LOADS = 16 * 5
        FAR_LOADS = 16 * (G + G + 2 + 1 + B * G)
        ATTN_LOADS = 16 * (B * 4 + 1)
        QK_LOADS = 16 * 2 * PARTS * PARTS
        MAMBA_LOADS = 16 * (4 * 3 + 8 + B + 1)
        B4_LOADS = 16 * 3
        PART_LOADS = 16 * 3 * 2 * PAIRS
        NT = 2 * CGRP
        units = [(n, i) for n in range(NH) for i in range(NBLK)]
        NUNIT = len(units)
        LAG_TURN, LAG_COPY, LAG_PV = 2, 3, 4

        RING_ITEMS = ["x0", "x1", "z0", "z1", "conv4", "bc0", "step0", "step1", "conv5", "bc1", "step2", "step3",
                      "bc2", "step4", "step5"]
        U_ORDER = [0, 1, 4, 2, 3, 5]

        def ring_bank(what, n):
            return bank2(2 * (RING_ITEMS.index(f"{what}{n}") % 4))

        def u_count(t):
            return U_ORDER.index(t) + 1

        def pexp_buffer(t):
            i = units[t][1]
            return NSB if i == 0 else (NSB + 1 if i == NBLK - 1 else t % NSB)

        block = ctx.enter_context(nc.Block())

        @block.sync
        def _(eng):
            eng.dma_start(x0[:], d["x"]).then_inc(s_ld["x"], 16)
            eng.dma_start(ones_b[:], d["c_ones"]).then_inc(s_ld["x"], 16)
            eng.dma_start(ident[:], d["c_ident"]).then_inc(s_ld["x"], 16)
            eng.dma_start(w_off_raw, d["woff"].rearrange("c (k g) -> c k g", g=G)).then_inc(s_ld["off"], 16)
            eng.dma_start(b_off, d["boff_rows"]).then_inc(s_ld["off"], 16)
            eng.dma_start(b_chk, d["bchk"]).then_inc(s_ld["off"], 16)
            eng.dma_start(bmask[:], d["c_bmask"]).then_inc(s_ld["off"], 16)
            eng.dma_start(bsel[:], d["c_bsel"]).then_inc(s_ld["off"], 16)
            eng.wait_ge(s_zero, 1)
            for b in range(B):
                q = slice(C * b, C * b + C)
                eng.dma_start(w_def[q, :, q], d["wdef"]).then_inc(s_ld["def"], 16)
            eng.dma_start(rpb_pad.rearrange("n r j k -> (n r) (j k)"), d["c_far"]).then_inc(s_ld["pad"], 16)
            eng.wait_ge(s_ld["pad"], 16)
            lo, hi = WIN // 2, C - WIN // 2 - 1
            for n in range(NH):
                flat = rpb_pad[n].rearrange("r j k -> r (j k)")
                for j in list(range(lo)) + list(range(hi + 1, C)):
                    k0 = min(max(j - lo, 0), C - WIN)
                    eng.dma_start(rpb_pad[n, :, j, k0:k0 + WIN],
                                  d["rpb"][n, :, k0 - j + WIN - 1:k0 - j + 2 * WIN - 1]).then_inc(s_ld["rpb"], 16)
                dst = flat[:, lo * C:lo * C + (hi - lo + 1) * (C + 1)]
                dst = dst.rearrange("r (j k) -> r j k", k=C + 1)[:, :, 0:WIN]
                src = d["rpb"][n, :, WIN - 1 - lo:WIN - 1 - lo + WIN].unsqueeze(1).to_broadcast([13, hi - lo + 1, WIN])
                eng.dma_start(dst, src).then_inc(s_ld["rpb"], 16)
            for b in range(B):
                q = slice(C * b, C * b + C)
                h, j = divmod(b, B // QH)
                for m in range(2):
                    cols = w_attn[q, m].rearrange("c (h d b n) -> c h d b n", h=QH, d=HD, n=NH)[:, h, :, j]
                    eng.dma_start(cols, d["wqkv"][:, C * m:C * m + C].rearrange("c (d n) -> c d n", n=NH)).then_inc(s_ld["attn"], 16)
                eng.dma_start(w_attn[q, 2, q], d["wqkv"][:, 2 * C:]).then_inc(s_ld["attn"], 16)
                eng.dma_start(w_attn[q, 3, q], d["wproj"]).then_inc(s_ld["attn"], 16)
            eng.dma_start(b_attn[:], d["battn"]).then_inc(s_ld["attn"], 16)
            for p in range(PAIRS):
                for j in range(2):
                    b = 2 * p + j
                    q = slice(C * b, C * b + C)
                    r = slice(DI * j, DI * j + DI)
                    for part in range(2):
                        eng.dma_start(w_in[q, 2 * part + p, r], d["win"][:, DI * part:DI * part + DI]).then_inc(s_ld["mamba"], 16)
                    eng.dma_start(w_out[r, p, q], d["wout"]).then_inc(s_ld["mamba"], 16)
            for j in range(2):
                r = slice(DI * j, DI * j + DI)
                eng.dma_start(xp_raw[r], d["xproj"]).then_inc(s_ld["mamba"], 16)
                eng.dma_start(par[r], d["par"]).then_inc(s_ld["mamba"], 16)
                eng.dma_start(w_dt[RANK * j:RANK * j + RANK, :, r], d["dtw"]).then_inc(s_ld["mamba"], 16)
                eng.dma_start(w_low[RANK * j:RANK * j + RANK, :, r], d["xlow"]).then_inc(s_ld["mamba"], 16)
            for b in range(B):
                q = slice(C * b, C * b + C)
                eng.dma_start(b_conv[q], d["bconv"]).then_inc(s_ld["mamba"], 16)
            eng.dma_start(ycol[:], d["c_ycol"]).then_inc(s_ld["mamba"], 16)

            eng.wait_ge(s_ld["rpb"], 16 * NH * (2 * lo + 1))
            for n in range(NH):
                eng.dma_start(bias[n], d["c_far"][0:1, 0:BIASW].to_broadcast([P, BIASW])).then_inc(s_ld["fill"], 16)
            eng.wait_ge(s_ld["fill"], 16 * NH)
            for r in range(QROWS):
                q = slice(C * r, C * r + C)
                for off, first, d0 in ((0, 0, WIN - 1 - r), (EDGE, r + 1, WIN // 2), (EDGE + INNER, 1, WIN // 2 - r)):
                    for n in range(NH):
                        eng.dma_start(
                            bias[n][q, off + C * first:off + C * (first + WIN)].rearrange("j (r k) -> j r k", k=C),
                            rpb_pad[n, d0:d0 + WIN, :, :].rearrange("r j k -> j r k")).then_inc(s_ld["bias"], 16)

            eng.wait_ge(S("tap"), TAPS)
            eng.wait_ge(S("is_far"), 1)
            with eng.If(eng.value_load(is_far[:], min_val=0, max_val=1) >= 1):
                eng.dma_start(xn_rows, img[:, IMG_0, PAD:PAD + C, PAD:PAD + C]).then_inc(S("xn_rows"), 16)
                for g in range(G):
                    q = slice(C * g, C * g + C)
                    eng.dma_start(far_w[q].rearrange("p a k n -> p (a k n)"),
                                  d["wdef"][CG * g:CG * g + CG].rearrange("(z a) k n -> z (a k n)", z=1)
                                  .to_broadcast([C, CG * TAPS * C])).then_inc(S("far_loaded"), 16)
                    eng.dma_start(far_b[q], d["boff"][g:g + 1, :].to_broadcast([C, 2 * TAPS])).then_inc(S("far_loaded"), 16)
                for q in range(2):
                    eng.dma_start(far_grid[:, q, :], d["c_grid"][q:q + 1, :].to_broadcast([P, T])).then_inc(S("far_loaded"), 16)
                eng.dma_start(far_tap, d["c_tap"]).then_inc(S("far_loaded"), 16)
                eng.wait_ge(S("xn_rows"), 16)
                for b in range(B):
                    for g in range(G):
                        r = C * b + CG * g
                        eng.dma_start(far_img[C * g:C * g + C, b], xn_rows[r:r + CG].rearrange("a y x -> y a x")).then_inc(S("far_loaded"), 16)
                eng.wait_ge(S("far_loaded"), FAR_LOADS)

            for h in range(QH):
                for k in range(PARTS):
                    for m, rows_of in enumerate((q_rows, k_rows)):
                        if m == 0:
                            eng.wait_ge(S("q_part"), k + 1)
                        else:
                            eng.wait_ge(S(("k_hi", "k_mid", "k_lo")[k]), 1)
                        for j in range(PARTS):
                            r = HD * (PARTS * k + j if m == 0 else PARTS * j + k)
                            n = B * NH // QH
                            eng.dma_start(rows_of[r:r + HD, n * h:n * h + n], qk_part[P // QH * h:P // QH * (h + 1), m, k]).then_inc(s_ld[f"qk{h}"], 16)
            eng.wait_ge(S("x2t"), 1)
            eng.dma_start(sel.bitcast(U16), d["c_sel"].rearrange("p (n m) -> p n m", m=P)).then_inc(s_ld["sel"], 16)
            for q in range(2):
                eng.dma_start(grid[q], d["c_grid"][q:q + 1, :].to_broadcast([P, T])).then_inc(s_ld["b4"], 16)
            eng.dma_start(selc.bitcast(U16), d["c_selc"].rearrange("p (g q m) -> p g q m", g=CGRP, q=2)).then_inc(s_ld["b4"], 16)
            for dr in range(DIRS):
                for k in range(3):
                    eng.wait_ge(S(("part_hi", "part_mid", "part_lo")[k]), dr + 1)
                    for p in range(PAIRS):
                        for w, dst in enumerate((split_b, split_c)):
                            r = C * (2 * p + w)
                            eng.dma_start(dst[C * k:C * k + C, PAIRS * dr + p], parts[k][dr % 2][r:r + C]).then_inc(s_ld[f"parts{dr}"], 16)
            eng.wait_ge(S("conv_cleared"), 1)
            for b in range(B):
                q = slice(C * b, C * b + C)
                eng.dma_start(w_conv[q, :, :, q].rearrange("p t a n -> p (t a) n"),
                              d["wconv"].rearrange("c t a n -> c (t a) n")).then_inc(s_ld["conv"], 16)
            for odd in range(2):
                cols = slice(HALF * odd, HALF * odd + HALF)
                for k in range(3):
                    eng.wait_ge(S("coord_part"), 3 * odd + k + 1)
                    for q in range(2):
                        r = (q * 3 + k) * 16
                        eng.dma_start(crow[r:r + 16, :, cols], coord_part[k][:, q, cols]).then_inc(s_ld["rows"], 16)
            for h in range(2):
                eng.wait_ge(S("yout"), h + 1)
                for k in range(4 * h, 4 * h + 4):
                    eng.dma_start(out.rearrange("b h w c -> (h w) b c")[P * k:P * k + P], yout[:, k]).then_inc(S("stored"), 16)
            eng.wait_ge(S("stored"), 16 * NBLK)

        @block.tensor
        def _(pe):
            for name in LOOPED["tensor"].split():
                pe.sem_inc(S(name), LEAD)
            def mm(o, l, r, start=True, stop=True, **k):
                return pe.matmul(o, l, r, start=start, stop=stop, **k)

            def halves(dst, lhs, rhs, start=True, stop=True):
                for h in range(2):
                    last = mm(dst[:, HALF * h:HALF * h + HALF], lhs, rhs(h), start, stop)
                return last

            pe.wait_ge(s_ld["x"], 48)
            pe.wait_ge(S("sum1"), 1)
            mm(ps[:, 6, 0:C], ones_b[:], small[:, 0:C]).then_inc(S("mean1"), 1)
            pe.wait_ge(S("sum2"), 1)
            mm(ps[:, 7, 0:C], ones_b[:], small[:, C:2 * C]).then_inc(S("var1"), 1)

            def rows(kind, ky, kx, h):
                r0 = ky + 1 + 16 * h
                return img[:, kind, r0:r0 + 16, kx + 1:kx + 1 + C]

            pe.wait_ge(S("w_off"), B)
            pe.wait_ge(S("img"), 1)

            def offsets(k):
                if k:
                    pe.wait_ge(S("hats"), 4 * k)
                for q in range(2):
                    last = halves(bank2(2 * q), w_off[:, k, q].rearrange("p b g c -> p (b g c)"),
                                  lambda h: img[:, IMG_0, PAD + 16 * h:PAD + 16 * h + 16, PAD:PAD + C])
                last.then_inc(S("off"), 1)

            offsets(0)
            pe.wait_ge(s_ld["def"], 16 * B)
            for k in range(TAPS):
                if k + 1 < TAPS:
                    offsets(k + 1)
                m = k - 1
                if 0 <= m < NCHK:
                    if m:
                        pe.wait_ge(S("absd"), m)
                    w = w_off[:, :, :, :, :, 0].rearrange("p k q b g -> p (k q) (b g)")[:, KQ * m:KQ * m + KQ]
                    halves(bank2(6)[0:CHK], w,
                           lambda h: img[:, IMG_0, PAD + 16 * h:PAD + 16 * h + 16, PAD:PAD + C]).then_inc(S("chk"), 1)
                ky, kx = divmod(k, 3)
                o = bank2(4)
                halves(o, w_def[:, k], lambda h: rows(IMG_0, ky, kx, h), start=(k == 0), stop=False)
                for j, what in enumerate(("term_a", "term_m", "term_p")):
                    pe.wait_ge(S(what), k + 1)
                    last = halves(o, w_def[:, k], lambda h: term[:, k % 2, j, HALF * h:HALF * h + HALF],
                                  start=False, stop=(k == TAPS - 1 and j == 2))
                last.then_inc(S("tap"), 1)
                if k == 6:
                    pe.wait_ge(S("far"), 1)
                    pe.transpose(ps[0:1, 6, 0:CHK], far[0:CHK, 3:4], ident[0:CHK, 0:CHK]).then_inc(S("far_t"), 1)

            pe.wait_ge(S("is_far"), 1)
            with pe.If(pe.value_load(is_far[:], min_val=0, max_val=1) >= 1):
                pe.wait_ge(S("far_zeroed"), 1)
                for h in range(2):
                    mm(ps[:, 4 + h, :], far_wst.rearrange("p b n -> p (b n)"), x0[:, HALF * h:HALF * h + HALF],
                       start=True, stop=False, skip_group_check=True).then_inc(S("far_open"), 1)
                with pe.Fori(0, TAPS) as k:
                    with pe.Fori(0, B) as b:
                        pe.wait_ge(S("far_off"), above(k * (2 * B) + b * 2 + 2))
                        for q in range(2):
                            last = halves(bank2(2 * q), far_off[:, q].rearrange("p g y -> p (g y)"),
                                          lambda h: img[:, IMG_0, PAD + 16 * h:PAD + 16 * h + 16, PAD:PAD + C])
                        last.then_inc(S("far_d"), 1)
                        pe.wait_ge(S("far_hat"), above(k * (2 * B) + b * 2 + 2))
                        for a in range(CG):
                            pe.wait_ge(S("far_st"), above(k * (2 * B * CG) + b * (2 * CG) + (2 * a + 2)))
                            halves(bank2(6), far_xst.rearrange("p g x -> p (g x)"),
                                   lambda h: far_hat[:, 0, HALF * h:HALF * h + HALF]).then_inc(S("far_q"), 1)
                            pe.wait_ge(S("far_prod"), above(k * (B * CG) + b * CG + (a + 1)))
                            for h in range(2):
                                last = mm(ps[:, 4 + h, :], far_wst.rearrange("p b n -> p (b n)"),
                                          far_prod[:, HALF * h:HALF * h + HALF], start=False, stop=False, skip_group_check=True)
                            last.then_inc(S("far_out"), 1)
                pe.wait_ge(S("far_rezeroed"), 1)
                for h in range(2):
                    mm(ps[:, 4 + h, :], far_wst.rearrange("p b n -> p (b n)"), x0[:, HALF * h:HALF * h + HALF],
                       start=False, stop=True, skip_group_check=True)
            mm(ps[:, 6, 0:C], ones_b[:], ones_b[:, 0:C]).then_inc(S("deform"), 1)

            pe.wait_ge(s_ld["attn"], ATTN_LOADS)
            pe.wait_ge(S("xn2"), 1)
            for m in range(2):
                last = halves(bank2(2 * m), w_attn[:, m], lambda h: xn[:, HALF * h:HALF * h + HALF])
                last.then_inc(S("qk"), 1)
            for i in range(NBLK):
                last = mm(ps[:, 6 + i // 4, P * (i % 4):P * (i % 4) + P], xn[:, P * i:P * i + P], w_attn[:, 2])
                if i % 4 == 3:
                    last.then_inc(S("v"), 1)

            pe.wait_ge(S("v_copied"), 2)
            pe.wait_ge(s_ld["qk0"], QK_LOADS)

            def scores(b, t):
                n, i = units[t]
                pe.wait_ge(S("neg"), above(b * NUNIT + (t - 2 if t >= 3 else t - 1)))
                tiles, _, (lo, hi) = key_tiles(i)
                mm(ps[:, (0, 1, 6)[t % 3], lo:hi], q_rows[:, b * NH + n, P * i:P * i + P],
                   k_rows[:, b * NH + n, P * tiles[0] + lo:P * tiles[0] + hi]).then_inc(S("sc"), 1)

            def pt_done(b, t):
                pe.wait_ge(S("pt_a" if t % 2 else "pt_v"), above(b * (NUNIT // 2) + (t // 2 + 1)))

            def turn(b, t):
                pe.wait_ge(S("pexp"), above(b * NUNIT + (t + 1)))
                pt_done(b, t - 3 if t % NUNIT >= 3 else t - 2)
                for c, (_, end, q0, q1) in reversed(list(enumerate(seeing(units[t % NUNIT][1])))):
                    last = pe.transpose(ps[:, (2, 3, 7)[t % NUNIT % 3], end - q1:end],
                                        pexp[0:q1, pexp_buffer(t % NUNIT), P * c:P * c + P], ident[0:q1, 0:q1])
                last.then_inc(S("turned"), 1)

            def values(b, t):
                n, i = units[t % NUNIT]
                tiles, _, _ = key_tiles(i)
                if t == 0:
                    pe.wait_ge(S("vz"), above(b + 1))
                    pe.wait_ge(S("ot_b"), above(b))
                pt_done(b, t)
                for c, (at, end, q0, q1) in enumerate(seeing(i)):
                    o = P * (i % 4)
                    last = mm(ps[0:2 * C, 4 + i // 4, o + q0:o + q1], vz[:, tiles[c], n].rearrange("p a c -> p (a c)"),
                              pt[:, t % NSB, at:end], start=(n == 0 and i % 4 == 0 and c == 0),
                              stop=(n == NH - 1 and c == len(tiles) - 1), skip_group_check=True)
                last.then_inc(S("pv"), 1)

            def attend(b, first):
                for t in range(NUNIT):
                    scores(b, t)
                    if t >= LAG_TURN or not first:
                        turn(b, t - LAG_TURN)
                    if t >= LAG_PV or not first:
                        values(b, t - LAG_PV)

            attend(0, True)
            pe.wait_ge(s_ld["qk1"], QK_LOADS)
            with pe.Fori(1, B) as b:
                attend(b, False)
            for t in range(LAG_PV):
                if t < LAG_TURN:
                    turn(B, t - LAG_TURN)
                values(B, t - LAG_PV)

            pe.wait_ge(s_ld["mamba"], MAMBA_LOADS)
            for dr in range(DIRS):
                last = mm(ps[:, 7, P * dr:P * dr + P], w_low[:, dr], w_dt[:, dr])
            last.then_inc(S("w_step"), 1)
            pe.wait_ge(S("neg"), above(B * NUNIT))
            for b in range(B):
                pe.wait_ge(S("ot_b"), above(b + 1))
                for i in range(NBLK):
                    last = pe.transpose(ps[:, b, 2 * C * i:2 * C * i + 2 * C], ot_b[:, b, P * i:P * i + P], ident[0:2 * C, 0:2 * C])
                last.then_inc(S("sums_turned"), 1)
            pe.wait_ge(S("normalized"), B)
            for h in range(2):
                for i in range(4 * h, 4 * h + 4):
                    last = pe.transpose(ps[:, 4 + h, P * (i % 4):P * (i % 4) + P], ot_turned[:, i].rearrange("p b c -> p (b c)"), ident[:])
                last.then_inc(S("ot_back"), 1)
            for h in range(2):
                pe.wait_ge(S("attended"), h + 1)
                mm(ps[:, h, :], w_attn[:, 3], ot[:, HALF * h:HALF * h + HALF]).then_inc(S("proj"), 1)

            pe.wait_ge(S("w_step_copied"), 1)
            pe.wait_ge(S("xn3"), 1)
            for m in range(4):
                halves(bank2(2 * m), w_in[:, m], lambda h: xn[:, HALF * h:HALF * h + HALF]).then_inc(S("xz"), 1)
            pe.wait_ge(S("w_xp"), 4)
            def conv_banks(t):
                for k in range(KC):
                    last = halves(ring_bank("conv", t), w_diag[:, k],
                                  lambda h: xs_sliced[t % 2][:, k + HALF * h:k + HALF * h + HALF], start=(k == 0), stop=(k == KC - 1))
                last.then_inc(S("conv_pe"), 1)

            def bc_rows(dr):
                for p in range(PAIRS):
                    pe.wait_ge(S("u"), u_count(PAIRS * dr + p))
                    halves(ring_bank("bc", dr)[2 * C * p:2 * C * p + 2 * C], w_xp[:, dr].rearrange("p w j n -> p (w j n)"),
                           lambda h: u[:, dr, p, HALF * h:HALF * h + HALF]).then_inc(S("bc"), 1)

            def step_rows(t):
                dr, p = divmod(t, PAIRS)
                pe.wait_ge(S("u"), u_count(t))
                halves(ring_bank("step", t), w_step[:, dr],
                       lambda h: u[:, dr, p, HALF * h:HALF * h + HALF]).then_inc(S("dtf"), 1)

            pe.wait_ge(S("w_diag"), 1)
            pe.wait_ge(S("x_sliced"), 1)
            pe.wait_ge(S("x_copied"), 2)
            conv_banks(4)
            bc_rows(0)
            pe.wait_ge(S("zs"), 1)
            step_rows(0)
            pe.wait_ge(S("zs"), 2)
            step_rows(1)
            pe.wait_ge(S("u"), u_count(4))
            pe.wait_ge(S("x_sliced"), 2)
            conv_banks(5)
            pe.wait_ge(S("rest"), 1)
            bc_rows(1)
            pe.wait_ge(S("relu_dt"), 1)
            step_rows(2)
            pe.wait_ge(S("relu_dt"), 2)
            step_rows(3)
            pe.wait_ge(S("u"), u_count(5))
            bc_rows(2)
            pe.wait_ge(S("rest"), 2)
            step_rows(4)
            pe.wait_ge(S("relu_dt"), 3)
            step_rows(5)
            for dr in range(DIRS):
                pe.wait_ge(s_ld[f"parts{dr}"], PART_LOADS)
            pe.wait_ge(s_ld["sel"], 16)
            pe.wait_ge(S("relu_dt"), DP)
            pe.wait_ge(S("rest"), DIRS)

            def spread(t, n):
                pe.wait_ge(S("dbu"), above(t * NS + (n - 1)))
                for h in range(2):
                    last = mm(ps[:, 2 * (n % 2) + h, :], sel[:, n], split_b[:, t, HALF * h:HALF * h + HALF])
                last.then_inc(S("b_rep"), 1)
                pe.wait_ge(S("c_copied"), above(t * NS + n))
                for h in range(2):
                    last = mm(ps[:, 4 + h, :], sel[:, n], split_c[:, t, HALF * h:HALF * h + HALF])
                last.then_inc(S("c_rep"), 1)

            def collect(t, n):
                pe.wait_ge(S("hc"), above(t * NS + (n + 1)))
                if n == 0:
                    pe.wait_ge(S("y_turned"), above(t))
                for c in range(NBLK):
                    last = mm(ps[:, 6 + c // 4, P * (c % 4):P * (c % 4) + P], hc_ring[n % RING][:, P * c:P * c + P], ident[:],
                              start=(n == 0 and c % 4 == 0), stop=(n == NS - 1 and c % 4 == 3), is_transpose=True,
                              skip_group_check=True)
                last.then_inc(S("y_acc"), 1)

            def turn_y(t):
                bank = (0, 2, 4, 0, 2, 6)[t]
                if bank == 4:
                    pe.wait_ge(S("c_copied"), above(DP * NS))
                elif t < 3:
                    pe.wait_ge(S("dbu"), above(DP * NS))
                elif t < DP - 1:
                    pe.wait_ge(S("y_read"), t - 2)
                pe.wait_ge(S("y_turned"), above(t + 1))
                for c in range(NBLK):
                    last = pe.transpose(ps[:, bank + c // 4, P * (c % 4):P * (c % 4) + P], du[:, t, P * c:P * c + P], ident[:])
                last.then_inc(S("y_back"), 1)

            def states(t, last=False):
                for n in range(NS):
                    if n + AHEAD < NS:
                        spread(t, n + AHEAD)
                    elif not last:
                        spread(t + 1, n + AHEAD - NS)
                    if last and n == NS - 2:
                        for k in range(3):
                            turn_y(k)
                    collect(t, n)

            AHEAD = 4
            for n in range(AHEAD):
                spread(0, n)
            with pe.Fori(0, DP - 1) as t:
                states(t)
            states(DP - 1, last=True)
            for k in range(3, DP):
                turn_y(k)
            for p in range(PAIRS):
                pe.wait_ge(S("gated"), p + 1)
                for h in range(2):
                    last = mm(ps[:, h, :], w_out[:, p], u[:, 0, p, HALF * h:HALF * h + HALF],
                              start=(p == 0), stop=(p == PAIRS - 1))
            last.then_inc(S("mamba"), 1)

            pe.wait_ge(s_ld["conv"], 16 * B)
            pe.wait_ge(S("xn4"), 1)
            for par_ in range(2):
                for k in range(9):
                    ky, kx = divmod(k, 3)
                    for h in range(2):
                        last = mm(ps[:, 2 * par_ + h, :], w_conv[:, k, par_],
                                  xpad[:, ky + 16 * h:ky + 16 * h + 16, kx:kx + C], start=(k == 0), stop=(k == 8))
                last.then_inc(S("conv"), 1)
            pe.wait_ge(s_ld["rows"], 16 * 12)
            pe.wait_ge(s_ld["b4"], B4_LOADS)

            def spread4(j, t):
                g, h = divmod(t, 2)
                pe.wait_ge(S("abs"), above(j * NT + t - 1))
                for q in range(2):
                    last = mm(ps[:, 2 * (t % 2) + q, :], selc[:, g, q], crow[:, j, HALF * h:HALF * h + HALF])
                last.then_inc(S("crep"), 1)

            def sample(j, t):
                g, h = divmod(t % NT, 2)
                if h == 0:
                    pe.wait_ge(S("stat"), above((j if t >= 0 else j - 1) * CGRP + (g + 1)))
                pe.wait_ge(S("hat_y"), above(j * NT + (t + 1)))
                pe.wait_ge(S("prod"), above(j * NT + t - 1))
                mm(ps[:, 4 + t % 2, :], xstat[:, g % 2].rearrange("p b x -> p (b x)"),
                   nhat[:, t % NU, 0, :]).then_inc(S("rowmix"), 1)

            def turn4(j, t):
                pe.wait_ge(S("prod"), above(j * NT + (t + 1)))
                pe.wait_ge(S("summed"), above(j * NT + t - 1))
                for c in range(4):
                    last = pe.transpose(ps[:, 6 + t % 2, P * c:P * c + P], prod[:, t % NU, P * c:P * c + P], ident[:])
                last.then_inc(S("prod_turned"), 1)

            def map_channels(j, first):
                for t in range(NT):
                    spread4(j, t)
                    if t >= LAG_MIX or not first:
                        sample(j, t - LAG_MIX)
                    if t >= LAG_POS or not first:
                        turn4(j, t - LAG_POS)

            map_channels(0, True)
            with pe.Fori(1, CPER) as j:
                map_channels(j, False)
            for t in range(LAG_MIX):
                sample(CPER, t - LAG_MIX)
                turn4(CPER, t - LAG_POS)
            pe.wait_ge(S("abs"), above(CPER * NT))
            for c in range(NBLK):
                last = pe.transpose(ps[:, c // 4, P * (c % 4):P * (c % 4) + P], x3t[:, P * c:P * c + P], ident[:])
            last.then_inc(S("x3_turned"), 1)
            for t in range(LAG_MIX, LAG_POS):
                turn4(CPER, t - LAG_POS)

        @block.vector
        def _(ve):
            for name in LOOPED["vector"].split():
                ve.sem_inc(S(name), LEAD)
            own = Tally(ve, v_own)

            def tt(o, a, b, op):
                return ve.tensor_tensor(o, a, b, op)

            own(ve.memset(img[:, IMG_0], 0.0))
            x3 = x0[:].rearrange("p (h w) -> p h w", w=C)
            xc3 = xc.rearrange("p (h w) -> p h w", w=C)
            ve.wait_ge(s_ld["x"], 48)
            ve.tensor_reduce(small[:, 0:C], x3.rearrange("p h w -> p w h"), AX.X, ALU.add).then_inc(S("sum1"), 1)
            ve.wait_ge(S("mean1"), 1)
            own(tt(xc3, x3, ps[:, 6, 0:C].unsqueeze(1).to_broadcast([P, C, C]), ALU.subtract))
            own.sync()
            own(tt(sq, xc, xc, ALU.mult))
            own.sync()
            ve.tensor_reduce(small[:, C:2 * C], sq.rearrange("p (h w) -> p w h", w=C), AX.X, ALU.add).then_inc(S("sum2"), 1)
            ve.wait_ge(S("var1"), 1)
            ve.tensor_scalar(stat1[:, 0], ps[:, 7, 0:C], 1e-5, None, ALU.add).then_inc(S("var1e"), 1)
            ve.wait_ge(S("std1"), 1)
            own(ve.reciprocal(stat1[:, 2], stat1[:, 1]))
            own.sync()
            inner = slice(PAD, PAD + C)
            tt(img[:, IMG_0, inner, inner], xc3, stat1[:, 2].unsqueeze(1).to_broadcast([P, C, C]), ALU.mult).then_inc(S("img"), 1)
            ve.wait_ge(S("img"), 1)

            def shifted(kind, dy, dx, r0=1, r1=W1 - 1):
                return img[:, kind, r0 + dy:r1 + dy, 1 + dx:W1 - 1 + dx]

            for kind, dx in ((IMG_XM, -1), (IMG_XP, 1)):
                own(tt(shifted(kind, 0, 0, 0, W1), shifted(IMG_0, 0, dx, 0, W1), shifted(IMG_0, 0, 0, 0, W1), ALU.subtract))
            own.sync()
            for kind, of, dy in ((IMG_PM, IMG_XM, 1), (IMG_PP, IMG_XP, 1), (IMG_MM, IMG_XM, -1), (IMG_MP, IMG_XP, -1)):
                last = tt(shifted(kind, 0, 0), shifted(of, dy, 0), shifted(of, 0, 0), ALU.subtract)
            last.then_inc(S("diffs"), 1)
            ve.wait_ge(S("diffs"), 1)
            ve.wait_ge(S("y_diffs"), 2)

            for k in range(TAPS):
                ky, kx = divmod(k, 3)

                def im(kind):
                    return img[:, kind, ky + 1:ky + 1 + C, kx + 1:kx + 1 + C]

                def square(a):
                    return a.rearrange("p (h w) -> p h w", w=C)

                hat = [square(hats[:, k % 2, j]) for j in range(4)]
                ve.wait_ge(S("hats"), 4 * (k + 1))
                if k:
                    ve.wait_ge(S("term_p"), k)
                if k >= 2:
                    ve.wait_ge(S("tap"), k - 1)
                tt(square(tmp_m[:, k % 2]), hat[1], im(IMG_MP), ALU.mult).then_inc(S("mp"), 1)
                own(tt(square(tmp_v[:, 0]), hat[0], im(IMG_XM), ALU.mult))
                own(tt(square(tmp_v[:, 1]), hat[1], im(IMG_XP), ALU.mult))
                own(tt(square(tmp_v[:, 2]), hat[0], im(IMG_PM), ALU.mult))
                own(tt(square(tmp_v[:, 3]), hat[1], im(IMG_PP), ALU.mult))
                own.sync(own.n - 2)
                tt(term[:, k % 2, 0], tmp_v[:, 0], tmp_v[:, 1], ALU.add).then_inc(S("term_a"), 1)
                own.sync()
                own(tt(tmp_v[:, 2], tmp_v[:, 2], tmp_v[:, 3], ALU.add))
                own.sync()
                own(tt(square(tmp_v[:, 3]), square(tmp_v[:, 2]), im(IMG_YP), ALU.add))
                own.sync()
                tt(term[:, k % 2, 2], hats[:, k % 2, 3], tmp_v[:, 3], ALU.mult).then_inc(S("term_p"), 1)
                if k == 5:
                    ve.wait_ge(S("absd"), NCHK)
                    own(ve.tensor_reduce(far[0:CHK, 0:NCHK], absd, AX.X, ALU.max))
                    own.sync()
                    ve.tensor_reduce(far[0:CHK, 3:4], far[0:CHK, 0:NCHK], AX.X, ALU.max).then_inc(S("far"), 1)
                if k == 7:
                    ve.wait_ge(S("far_t"), 1)
                    own(ve.tensor_reduce(small[0:1, 60:61], ps[0:1, 6, 0:CHK], AX.X, ALU.max))
                    own.sync()
                    ve.tensor_scalar(is_far[:], small[0:1, 60:61], 1.0, None, ALU.is_gt).then_inc(S("is_far"), 1)
            ve.wait_ge(S("is_far"), 1)
            with ve.If(ve.value_load(is_far[:], min_val=0, max_val=1) >= 1):
                ve.wait_ge(S("tap"), TAPS)
                ve.wait_ge(S("far_loaded"), FAR_LOADS)
                ve.memset(far_wst, 0.0).then_inc(S("far_zeroed"), 1)
                ve.wait_ge(S("far_zeroed"), 1)
                raw = w_off_raw.rearrange("p (k q) g -> p k q g", q=2)
                with ve.Fori(0, TAPS) as k:
                    with ve.Fori(0, B) as b:
                        ve.wait_ge(S("far_out"), above(k * (B * CG) + b * CG))
                        ve.wait_ge(S("far_open"), 2)
                        for q in range(2):
                            tt(far_off[:, q], raw[:, bass.ds(k, 1), q].rearrange("p a g -> p g a").to_broadcast([P, G, C]),
                               bmask[:, bass.ds(b, 1)].unsqueeze(2).to_broadcast([P, G, C]), ALU.mult).then_inc(S("far_off"), 1)
                        ve.wait_ge(S("far_d"), above(k * B + b + 1))
                        ve.wait_ge(S("far_open"), 2)
                        for q in range(2):
                            ve.scalar_tensor_tensor(out=far_hat[:, q], in0=bank2(2 * q), scalar=far_b[:, bass.ds(k * 2 + q, 1)],
                                                    in1=far_grid[:, q], op0=ALU.add, op1=ALU.add).then_inc(S("far_pos"), 1)
                        for a in range(CG):
                            at = k * (B * CG) + b * CG + a
                            ve.wait_ge(S("far_out"), above(at))
                            ve.wait_ge(S("far_open"), 2)
                            tt(far_xst, far_img[:, bass.ds(b, 1), a].to_broadcast([P, G, C]),
                               bmask[:].unsqueeze(2).to_broadcast([P, G, C]), ALU.mult).then_inc(S("far_st"), 1)
                            tt(far_wst, far_w[:, a, bass.ds(k, 1), :].to_broadcast([P, B, C]),
                               bsel[:, bass.ds(b, 1), :].rearrange("p z b -> p b z").to_broadcast([P, B, C]), ALU.mult).then_inc(S("far_st"), 1)
                            ve.wait_ge(S("far_q"), above(at + 1))
                            ve.wait_ge(S("far_hat"), above(k * (2 * B) + b * 2 + 2))
                            tt(far_prod, bank2(6), far_hat[:, 1], ALU.mult).then_inc(S("far_prod"), 1)
                ve.wait_ge(S("far_out"), above(TAPS * B * CG))
                ve.memset(far_wst, 0.0).then_inc(S("far_rezeroed"), 1)
            ve.wait_ge(S("deform"), 1)
            own(ve.scalar_tensor_tensor(out=x1[:], in0=bank2(4), scalar=0.0, in1=x0[:], op0=ALU.max, op1=ALU.add))
            own.sync()
            ve.transpose(x1t[:].rearrange("p (c h) -> p h c", h=C), x1[:].rearrange("p (h w) -> p h w", w=C)).then_inc(S("x1t"), 1)
            ve.wait_ge(S("x1t"), 1)

            def normalize(x, name, into):
                for h in range(2):
                    own(ve.bn_stats(small[:, 8 + 6 * h:14 + 6 * h], x[:, HALF * h:HALF * h + HALF]))
                own.sync()
                own(ve.bn_aggr(small[:, 20:22], small[:, 8:20]))
                own.sync()
                ve.tensor_scalar(small[:, 22:23], small[:, 21:22], 1e-5, None, ALU.add).then_inc(S(name + "_var"), 1)
                ve.wait_ge(S(name + "_std"), 1)
                own(ve.reciprocal(small[:, 24:25], small[:, 23:24]))
                own.sync()
                x = x[:].rearrange("p (h w) -> p h w", w=C) if len(into.shape) == 3 else x[:]
                ve.tensor_scalar(into, x, small[:, 20:21], small[:, 24:25], ALU.subtract, ALU.mult).then_inc(S(name), 1)

            normalize(x1t, "xn2", xn[:])
            ve.wait_ge(s_ld["attn"], ATTN_LOADS)
            ve.wait_ge(S("qk"), 1)
            q = qk_full[:, 0]
            own(ve.tensor_scalar(q, bank2(0), b_attn[:, 0:1], -(float(HD) ** -0.5), ALU.add, ALU.mult))
            own.sync()
            for k in range(PARTS - 1):
                ve.tensor_copy(qk_part[:, 0, k], q).then_inc(S("q_part"), 1)
                ve.wait_ge(S("q_part"), k + 1)
                if k == 0:
                    own(tt(q, q, qk_part[:, 0, k], ALU.subtract))
                    own.sync()
            tt(qk_part[:, 0, PARTS - 1], q, qk_part[:, 0, PARTS - 2], ALU.subtract).then_inc(S("q_part"), 1)
            ve.wait_ge(S("k_mid"), 1)
            tt(qk_part[:, 1, 2], qk_full[:, 1], qk_part[:, 1, 1], ALU.subtract).then_inc(S("k_lo"), 1)
            ve.wait_ge(S("v"), 2)
            for h in range(2):
                ve.tensor_copy(vt[:, 4 * h:4 * h + 4].rearrange("p a n -> p (a n)"), ps[:, 6 + h, :]).then_inc(S("v_copied"), 1)
            ve.wait_ge(S("v_copied"), 2)
            ve.wait_ge(S("vz_cleared"), 1)

            def place_values(b):
                ve.wait_ge(S("pv"), above(b * NUNIT))
                ve.wait_ge(s_zero, 1)
                for n in range(NH):
                    last = ve.tensor_copy(vz[:, :, n, 0, HD * n:HD * n + HD], vt[:, :, bass.ds(b * C + HD * n, HD)])
                last.then_inc(S("vz"), 1)

            def copy_turned(b, t):
                w = seeing(units[t % NUNIT][1])[-1][1]
                ve.wait_ge(S("turned"), above(b * NUNIT + (t + 1)))
                ve.wait_ge(S("pv"), above(b * NUNIT + (t - NSB + 1)))
                ve.tensor_copy(pt[:, t % NSB, 0:w], ps[:, (2, 3, 7)[t % NUNIT % 3], 0:w]).then_inc(S("pt_v"), 1)

            def attend(b, first):
                for t in range(NUNIT):
                    n, i = units[t]
                    if t == LAG_PV and not first:
                        place_values(b)
                    ve.wait_ge(S("sc"), above(b * NUNIT + (t + 1)))
                    ve.wait_ge(S("pexp"), above(b * NUNIT + (t - NSB + 1)))
                    if (t - LAG_COPY) % 2 == 0 and (t >= LAG_COPY or not first):
                        copy_turned(b, t - LAG_COPY)
                    else:
                        ve.tensor_copy(small[:, 50 + t % 8:51 + t % 8], ident[:, 0:1])
                    tiles, off, (lo, hi) = key_tiles(i)
                    ve.tensor_tensor_reduce(sc[:, t % NSB, lo:hi], ps[:, (0, 1, 6)[t % 3], lo:hi], bias[n][:, off + lo:off + hi],
                                            1.0, 4 * BIG, ALU.add, ALU.min, nmax[:, t % NSB:t % NSB + 1]).then_inc(S("neg"), 1)

            place_values(0)
            ve.wait_ge(S("bias_negated"), NH)
            attend(0, True)
            with ve.Fori(1, B) as b:
                attend(b, False)
            for t in range(LAG_COPY):
                if (t - LAG_COPY) % 2 == 0:
                    copy_turned(B, t - LAG_COPY)
            for b in range(B):
                ve.wait_ge(S("sums_turned"), b + 1)
                v = ps[:, b, :].rearrange("p (i a n d) -> p i a n d", i=NBLK, a=2, n=NH)
                own(ve.reciprocal(rsum[:, b], v[:, :, 1, :, 0]))
                own.sync()
                tt(ot_turned[:, :, b].rearrange("p i (n d) -> p i n d", n=NH), v[:, :, 0],
                   rsum[:, b].unsqueeze(3).to_broadcast([P, NBLK, NH, HD]), ALU.mult).then_inc(S("normalized"), 1)
            for h in range(2):
                cols = slice(HALF * h, HALF * h + HALF)
                ve.wait_ge(S("proj"), h + 1)
                last = ve.scalar_tensor_tensor(out=x2t[:, cols], in0=ps[:, h, :], scalar=b_attn[:, 3:4], in1=x1t[:, cols],
                                               op0=ALU.add, op1=ALU.add)
            last.then_inc(S("x2t"), 1)
            ve.wait_ge(S("x2t"), 1)

            normalize(x2t, "xn3", xn[:])
            ve.wait_ge(s_ld["mamba"], MAMBA_LOADS)

            def convolve(t):
                dr, p = divmod(t, PAIRS)
                at = [2 * (KC - 1) - k if dr == 1 else k for k in range(KC)]
                a = acc_c[:, p]
                if t >= 2:
                    ve.wait_ge(S("u"), u_count(t - 2))
                ve.wait_ge(S("x_copied"), p + 1)
                own(ve.tensor_scalar(a, xs[:, p, at[0]:at[0] + T], par[:, dr, 0:1], par[:, dr, KC:KC + 1], ALU.mult, ALU.add))
                for k in range(1, KC):
                    own.sync()
                    last = ve.scalar_tensor_tensor(out=a, in0=xs[:, p, at[k]:at[k] + T], scalar=par[:, dr, k:k + 1], in1=a,
                                                   op0=ALU.mult, op1=ALU.add)
                    if k < KC - 1:
                        own(last)
                last.then_inc(S("conv1d"), 1)

            def take_rest(dr):
                ve.wait_ge(S("part_hi"), dr + 1)
                if dr == 2:
                    ve.wait_ge(S("part_lo"), 1)
                tt(rest[:, dr % 2], ring_bank("bc", dr), parts[0][dr % 2], ALU.subtract).then_inc(S("rest"), 1)

            def take_mid_lo(dr):
                if dr == 2:
                    ve.wait_ge(s_ld["parts0"], PART_LOADS)
                ve.wait_ge(S("rest"), dr + 1)
                ve.tensor_copy(parts[1][dr % 2], rest[:, dr % 2]).then_inc(S("part_mid"), 1)
                ve.wait_ge(S("part_mid"), dr + 1)
                tt(parts[2][dr % 2], rest[:, dr % 2], parts[1][dr % 2], ALU.subtract).then_inc(S("part_lo"), 1)

            ve.wait_ge(S("xs_cleared"), 1)
            def round_e(t):
                ve.wait_ge(S("e_dt"), t + 1)
                own(ve.tensor_scalar(one_e[t], du[:, t], 1.0, None, ALU.add))
                own.sync()
                ve.scalar_tensor_tensor(out=du[:, t], in0=one_e[t], scalar=-1.0, in1=du[:, t],
                                        op0=ALU.add, op1=ALU.subtract).then_inc(S("round_e"), 1)

            def times_u(t):
                dr, p = divmod(t, PAIRS)
                tt(du[:, t], delta[:, t], u[:, dr, p], ALU.mult).then_inc(S("du"), 1)

            for t in range(3):
                convolve(t)
            take_rest(0)
            take_mid_lo(0)
            convolve(3)
            take_rest(1)
            take_mid_lo(1)
            for t in range(4):
                round_e(t)
            take_rest(2)
            take_mid_lo(2)
            round_e(4)
            round_e(5)
            for t in range(DP):
                ve.wait_ge(S("ln"), t + 1)
                ve.wait_ge(S("relu_less"), t + 1)
                tt(delta[:, t], delta[:, t], one_e[t], ALU.add).then_inc(S("delta"), 1)
            ve.wait_ge(S("delta"), DP)
            times_u(0)
            ve.wait_ge(S("du"), 1)

            def inject(t, n):
                ve.wait_ge(S("b_rep"), above(t * NS + (n + 1)))
                ve.wait_ge(S("scan"), above(t * NS + (n - RING + 1)))
                ve.wait_ge(s_zero, 1)
                tt(dbu_ring[n % RING], du[:, t], bank2(2 * (n % 2)), ALU.mult).then_inc(S("dbu"), 1)

            def scan(t, n):
                ve.wait_ge(S("da"), above(t * NS + (n + 1)))
                ve.wait_ge(S("dbu"), above(t * NS + (n + 1)))
                ve.wait_ge(S("hc"), above(t * NS + (n - RING + 1)))
                ve.tensor_tensor_scan(hs_ring[n % RING], da[:, n % 2], dbu_ring[n % RING], 0.0, ALU.mult, ALU.add).then_inc(S("scan"), 1)

            def read_y(t):
                dr, p = divmod(t, PAIRS)
                ve.wait_ge(S("y_back"), t + 1)
                ve.scalar_tensor_tensor(out=u[:, dr, p], in0=u[:, dr, p], scalar=d_col[:, dr, p:p + 1],
                                        in1=bank2((0, 2, 4, 0, 2, 6)[t]), op0=ALU.mult, op1=ALU.add).then_inc(S("y_read"), 1)

            def states(t, first):
                inject(t, 0)
                for n in range(NS):
                    if n + 1 < NS:
                        inject(t, n + 1)
                    scan(t, n)
                    if first and n in (3, 6, 9, 12):
                        times_u(1 + n // 3)

            states(0, True)
            ve.wait_ge(S("du"), DP - 1)
            ve.wait_ge(S("du_pool"), 1)
            with ve.Fori(1, DP) as t:
                states(t, False)

            def join(p, dr):
                if dr == 1:
                    own(tt(u[:, 0, p], u[:, 0, p], u[:, 1, p, ::-1], ALU.add))
                else:
                    y0 = u[:, 0, p].rearrange("p (s m) -> p m s", s=SLICES)
                    own(tt(y0, y0, u[:, 2, p].rearrange("p (m s) -> p m s", s=SLICES), ALU.add))
                own.sync()

            for t in range(DP - 1):
                read_y(t)
            ve.wait_ge(S("y_read"), DP - 1)
            join(0, 1)
            join(0, 2)
            tt(u[:, 0, 0], u[:, 0, 0], zs[:, 0], ALU.mult).then_inc(S("gated"), 1)
            read_y(DP - 1)
            ve.wait_ge(S("y_read"), DP)
            ve.wait_ge(S("joined"), 1)
            join(1, 2)
            tt(u[:, 0, 1], u[:, 0, 1], zs[:, 1], ALU.mult).then_inc(S("gated"), 1)
            ve.wait_ge(S("mamba"), 1)
            tt(x3t[:], bank2(0), x2t[:], ALU.add).then_inc(S("x3t"), 1)
            ve.wait_ge(S("x3t"), 1)

            ve.wait_ge(S("xpad_cleared"), 1)
            inside = xpad[:, 1:1 + C, 1:1 + C]
            normalize(x3t, "xn4", inside)
            ve.wait_ge(S("xn4"), 1)
            ve.transpose(xrow, inside.rearrange("p r c -> p c r")).then_inc(S("xrow"), 1)
            ve.wait_ge(s_ld["b4"], B4_LOADS)
            for odd in range(2):
                cols = slice(HALF * odd, HALF * odd + HALF)
                ve.wait_ge(S("conv"), odd + 1)
                for q in range(2):
                    own(ve.scalar_tensor_tensor(out=coord[:, q, cols], in0=bank2(2 * odd)[:, q::2], scalar=b_conv[:, odd:odd + 1],
                                                in1=grid[q][:, cols], op0=ALU.add, op1=ALU.add))
                own.sync()
                v = coord[:, :, cols]
                own(ve.tensor_scalar(v, v, 0.0, float(C - 1), ALU.max, ALU.min))
                own.sync()
                hi, mid, lo = (x[:, :, cols] for x in coord_part)
                ve.tensor_copy(hi, v).then_inc(S("coord_part"), 1)
                ve.wait_ge(S("coord_part"), 3 * odd + 1)
                own(tt(v, v, hi, ALU.subtract))
                own.sync()
                ve.tensor_copy(mid, v).then_inc(S("coord_part"), 1)
                ve.wait_ge(S("coord_part"), 3 * odd + 2)
                tt(lo, v, mid, ALU.subtract).then_inc(S("coord_part"), 1)

            def hat4(j, t):
                ve.wait_ge(S("abs"), above(j * NT + (t + 1)))
                ve.wait_ge(S("prod"), above(j * NT + (t - NU + 1)))
                ve.tensor_scalar(nhat[:, t % NU, 1], ahat[:, t % NU, 1], 1.0, 1.0, ALU.min, ALU.subtract).then_inc(S("nhat"), 1)

            def product(j, t):
                ve.wait_ge(S("rowmix"), above(j * NT + (t + 1)))
                ve.wait_ge(S("nhat"), above(j * NT + (t + 1)))
                ve.wait_ge(S("prod_turned"), above(j * NT + (t - NU + 1)))
                tt(prod[:, t % NU], ps[:, 4 + t % 2, :], nhat[:, t % NU, 1], ALU.mult).then_inc(S("prod"), 1)

            def sum_columns(j, t):
                g, h = divmod(t % NT, 2)
                c = (j if t >= 0 else j - 1) + CPER * g
                ve.wait_ge(S("prod_turned"), above(j * NT + (t + 1)))
                ve.wait_ge(s_zero, 1)
                ve.tensor_reduce(sampled[:, 4 * h:4 * h + 4, :, bass.ds(c, 1)].rearrange("p k b a -> p k (b a)"),
                                 ps[:, 6 + t % 2, :].rearrange("p (k b x) -> p k b x", k=4, b=B), AX.X, ALU.add).then_inc(S("summed"), 1)

            def map_channels(j, first):
                for t in range(NT):
                    if t >= LAG_MIX or not first:
                        product(j, t - LAG_MIX)
                    hat4(j, t)
                    if t >= LAG_SUM or not first:
                        sum_columns(j, t - LAG_SUM)

            map_channels(0, True)
            with ve.Fori(1, CPER) as j:
                map_channels(j, False)
            for t in range(-LAG_SUM, 0):
                if t + LAG_SUM < LAG_MIX:
                    product(CPER, t + LAG_SUM - LAG_MIX)
                sum_columns(CPER, t)
            ve.wait_ge(S("x3_turned"), 1)
            ve.wait_ge(S("summed"), above(CPER * NT))
            for h in range(2):
                tt(yout[:, 4 * h:4 * h + 4].rearrange("p k b c -> p (k b c)"), ps[:, h, :],
                   sampled[:, 4 * h:4 * h + 4].rearrange("p k b c -> p (k b c)"), ALU.subtract).then_inc(S("yout"), 1)

        @block.scalar
        def _(ac):
            for name in LOOPED["scalar"].split():
                ac.sem_inc(S(name), LEAD)
            own = Tally(ac, a_own)
            ac.wait_ge(s_ld["off"], OFF_LOADS)
            wo = w_off.rearrange("p k q b g c -> p (k q) b g c")
            for b in range(B):
                ac.activation(wo[:, :, b], w_off_raw.unsqueeze(3).to_broadcast([P, 2 * TAPS, G, CG]), ACT.Copy,
                              scale=bmask[:, b:b + 1]).then_inc(S("w_off"), 1)
            ac.mul(b_off_neg, b_off, -1.0).then_inc(S("b_off_neg"), 1)
            ac.wait_ge(S("var1e"), 1)
            ac.activation(stat1[:, 1], stat1[:, 0], ACT.Sqrt).then_inc(S("std1"), 1)
            ac.wait_ge(S("b_off_neg"), 1)
            for k in range(TAPS):
                if k == TAPS - 2:
                    ac.wait_ge(s_ld["bias"], 16 * QROWS * 3 * NH)
                    for n in range(NH):
                        ac.mul(bias[n], bias[n], -1.0).then_inc(S("bias_negated"), 1)
                ac.wait_ge(S("off"), k + 1)
                if k >= 2:
                    ac.wait_ge(S("term_m"), k - 1)
                    ac.wait_ge(S("term_p"), k - 1)
                for j, (q, sign) in enumerate(((1, -1.0), (1, 1.0), (0, -1.0), (0, 1.0))):
                    col = (b_off if sign > 0 else b_off_neg)[:, 2 * k + q:2 * k + q + 1]
                    ac.activation(hats[:, k % 2, j], bank2(2 * q), ACT.Relu, bias=col, scale=sign).then_inc(S("hats"), 1)
                m = k - 2
                if 0 <= m < NCHK:
                    ac.wait_ge(S("chk"), m + 1)
                    ac.activation(absd[:, m], bank2(6)[0:CHK], ACT.Abs, bias=b_chk[:, m:m + 1]).then_inc(S("absd"), 1)

            ac.wait_ge(S("is_far"), 1)
            with ac.If(ac.value_load(is_far[:], min_val=0, max_val=1) >= 1):
                with ac.Fori(0, TAPS) as k:
                    with ac.Fori(0, B) as b:
                        for q in range(2):
                            ac.wait_ge(S("far_pos"), above(k * (2 * B) + b * 2 + (q + 1)))
                            ac.wait_ge(S("is_far"), 1)
                            ac.activation(far_hat[:, q], far_hat[:, q], ACT.Abs, bias=far_tap[:, bass.ds(k * 2 + q, 1)]).then_inc(S("far_abs"), 1)
                            ac.wait_ge(S("far_abs"), above(k * (2 * B) + b * 2 + (q + 1)))
                            ac.activation(far_hat[:, q], far_hat[:, q], ACT.Relu, bias=1.0, scale=-1.0).then_inc(S("far_hat"), 1)

            def root(name):
                own(ac.activation(small[:, 25:26], ident[:, 0:1], ACT.Sqrt))
                ac.wait_ge(S(name + "_var"), 1)
                ac.activation(small[:, 23:24], small[:, 22:23], ACT.Sqrt).then_inc(S(name + "_std"), 1)

            root("xn2")
            ac.wait_ge(s_ld["attn"], ATTN_LOADS)
            ac.wait_ge(S("qk"), 2)
            own(ac.activation(qk_full[:, 1], bank2(2), ACT.Identity, bias=b_attn[:, 1:2]))
            own.sync()
            ac.activation(qk_part[:, 1, 0], qk_full[:, 1], ACT.Copy).then_inc(S("k_hi"), 1)
            ac.wait_ge(S("k_rest"), 1)
            ac.activation(qk_part[:, 1, 1], qk_full[:, 1], ACT.Copy).then_inc(S("k_mid"), 1)

            def copy_turned(b, t):
                w = seeing(units[t % NUNIT][1])[-1][1]
                ac.wait_ge(S("turned"), above(b * NUNIT + (t + 1)))
                ac.wait_ge(S("pv"), above(b * NUNIT + (t - NSB + 1)))
                ac.activation(pt[:, t % NSB, 0:w], ps[:, (2, 3, 7)[t % NUNIT % 3], 0:w], ACT.Copy).then_inc(S("pt_a"), 1)

            def copy_sums(b):
                ac.wait_ge(S("pv"), above(b * NUNIT + NUNIT))
                ac.wait_ge(s_ld["attn"], ATTN_LOADS)
                ac.activation(ot_b[:, b, :], bank2(4)[0:2 * C], ACT.Copy).then_inc(S("ot_b"), 1)

            def attend(b, first):
                for t in range(NUNIT):
                    lo, hi = key_tiles(units[t][1])[2]
                    if t == LAG_PV and not first:
                        copy_sums(b - 1)
                    if (t - LAG_COPY) % 2 and (t >= LAG_COPY or not first):
                        copy_turned(b, t - LAG_COPY)
                    ac.wait_ge(S("neg"), above(b * NUNIT + (t + 1)))
                    ac.wait_ge(S("turned"), above(b * NUNIT + (t - NSB + 1)))
                    ac.activation(pexp[:, pexp_buffer(t), lo:hi], sc[:, t % NSB, lo:hi], ACT.Exp, bias=nmax[:, t % NSB:t % NSB + 1],
                                  scale=-1.0).then_inc(S("pexp"), 1)
            ac.wait_ge(S("pexp_cleared"), 1)
            attend(0, True)
            with ac.Fori(1, B) as b:
                attend(b, False)
            for t in range(LAG_COPY):
                if (t - LAG_COPY) % 2:
                    copy_turned(B, t - LAG_COPY)
            copy_sums(B - 1)
            for h in range(2):
                ac.wait_ge(S("ot_back"), h + 1)
                ac.activation(ot[:, HALF * h:HALF * h + HALF], ps[:, 4 + h, :], ACT.Identity, bias=b_attn[:, 2:3]).then_inc(S("attended"), 1)

            ac.wait_ge(S("w_step"), 1)
            ac.activation(w_step[:].rearrange("p d n -> p (d n)"), ps[:, 7, 0:DIRS * P], ACT.Copy).then_inc(S("w_step_copied"), 1)
            root("xn3")
            for p in range(PAIRS):
                ac.wait_ge(S("xz"), 1 + p)
                ac.activation(xs[:, p, KC - 1:KC - 1 + T], bank2(2 * p), ACT.Copy).then_inc(S("x_copied"), 1)
            for p in range(PAIRS):
                ac.wait_ge(S("xz"), 3 + p)
                ac.activation(zs[:, p], bank2(4 + 2 * p), ACT.Silu).then_inc(S("zs"), 1)
            def part_hi(dr):
                ac.wait_ge(S("bc"), PAIRS * (dr + 1))
                if dr == 2:
                    ac.wait_ge(s_ld["parts0"], PART_LOADS)
                ac.activation(parts[0][dr % 2], ring_bank("bc", dr), ACT.Copy).then_inc(S("part_hi"), 1)

            def step_size(t):
                dr = t // PAIRS
                x = ring_bank("step", t)
                ac.wait_ge(S("dtf"), t + 1)
                own(ac.activation(du[:, t], x, ACT.Abs, bias=par[:, dr, KC + 1:KC + 2]))
                ac.activation(delta[:, t], x, ACT.Relu, bias=par[:, dr, KC + 1:KC + 2]).then_inc(S("relu_dt"), 1)

            def activate(t):
                dr, p = divmod(t, PAIRS)
                if dr < 2:
                    ac.wait_ge(S("conv1d"), t + 1)
                    ac.activation(u[:, dr, p], acc_c[:, p, ::-1] if dr else acc_c[:, p], ACT.Silu).then_inc(S("u"), 1)
                else:
                    ac.wait_ge(S("conv_pe"), p + 1)
                    ac.activation(u[:, dr, p], ring_bank("conv", t), ACT.Silu, bias=par[:, dr, KC:KC + 1]).then_inc(S("u"), 1)

            def exponential(t):
                ac.wait_ge(S("relu_dt"), t + 1)
                ac.activation(du[:, t], du[:, t], ACT.Exp, scale=-1.0).then_inc(S("e_dt"), 1)

            activate(0)
            activate(1)
            activate(4)
            part_hi(0)
            step_size(0)
            step_size(1)
            activate(2)
            activate(3)
            activate(5)
            part_hi(1)
            a_all = a_col[:].rearrange("p d q n -> p (d q n)")
            ac.wait_ge(S("a_log"), PAIRS)
            own(ac.activation(a_all, a_all, ACT.Exp))
            own.sync()
            ac.mul(a_all, a_all, -1.0).then_inc(S("a_neg"), 1)
            exponential(0)
            exponential(1)
            for t in (2, 3):
                step_size(t)
                exponential(t)
            part_hi(2)
            for t in (4, 5):
                step_size(t)
                exponential(t)
            for t in range(DP):
                ac.wait_ge(S("round_e"), t + 1)
                ac.activation(one_e[t], one_e[t], ACT.Ln).then_inc(S("ln"), 1)
            own(ac.activation(small[:, 26:27], ident[:, 0:1], ACT.Exp))
            ac.wait_ge(S("delta"), DP)
            ac.wait_ge(S("a_neg"), 1)

            def copy_y(t):
                ac.wait_ge(S("y_acc"), above(t * NS + NS))
                ac.wait_ge(S("a_neg"), 1)
                ac.activation(du[:, t], bank2(6), ACT.Copy).then_inc(S("y_turned"), 1)

            def states(t, first):
                for n in range(NS):
                    ac.wait_ge(S("scan"), above(t * NS + (n - 1)))
                    ac.wait_ge(S("a_neg"), 1)
                    ac.activation(da[:, n % 2], delta[:, t], ACT.Exp, scale=a_all[:, bass.ds(t * NS + n, 1)]).then_inc(S("da"), 1)
                    ac.wait_ge(S("c_rep"), above(t * NS + (n + 1)))
                    ac.wait_ge(S("hc"), above(t * NS + (n - RING + 1)))
                    ac.activation(c_ring[n % RING], bank2(4), ACT.Copy).then_inc(S("c_copied"), 1)
                    if n == 3 and not first:
                        copy_y(t - 1)

            states(0, True)
            with ac.Fori(1, DP) as t:
                states(t, False)
            copy_y(DP - 1)

            root("xn4")
            ac.wait_ge(S("nycol"), 1)
            with ac.Fori(0, CPER) as j:
                for t in range(NT):
                    ac.wait_ge(S("crep"), above(j * NT + (t + 1)))
                    ac.wait_ge(S("nhat"), above(j * NT + (t - NU + 1)))
                    ac.wait_ge(S("hat_y"), above(j * NT + (t - NU + 1)))
                    ac.activation(ahat[:, t % NU].rearrange("p q n -> p (q n)"), bank2(2 * (t % 2)), ACT.Abs,
                                  bias=nycol[:, 0:1]).then_inc(S("abs"), 1)
                    ac.wait_ge(S("rowmix"), above(j * NT + (t - NU + 1)))
                    ac.wait_ge(S("abs"), above(j * NT + (t + 1)))
                    ac.activation(nhat[:, t % NU, 0], ahat[:, t % NU, 0], ACT.Relu, bias=1.0, scale=-1.0).then_inc(S("hat_y"), 1)

        @block.gpsimd
        def _(gp):
            for name in LOOPED["gpsimd"].split():
                gp.sem_inc(S(name), LEAD)
            own = Tally(gp, g_own)

            def mul(o, a, b):
                return gp.tensor_tensor(o, a, b, ALU.mult)

            def add(o, a, b):
                return gp.tensor_tensor(o, a, b, ALU.add)

            for w in (w_def, w_attn[:], w_in[:], w_out[:], w_dt[:], w_low[:]):
                last = gp.memset(w, 0.0)
            last.then_inc(s_zero, 1)
            own(gp.memset(w_xp[:], 0.0))
            gp.wait_ge(S("img"), 1)
            for kind, dy in ((IMG_YM, -1), (IMG_YP, 1)):
                gp.tensor_tensor(img[:, kind, 1:W1 - 1, 1:W1 - 1], img[:, IMG_0, 1 + dy:W1 - 1 + dy, 1:W1 - 1],
                                 img[:, IMG_0, 1:W1 - 1, 1:W1 - 1], ALU.subtract).then_inc(S("y_diffs"), 1)
            gp.wait_ge(S("y_diffs"), 2)
            gp.wait_ge(S("diffs"), 1)
            for k in range(TAPS):
                ky, kx = divmod(k, 3)

                def im(kind):
                    return img[:, kind, ky + 1:ky + 1 + C, kx + 1:kx + 1 + C]

                def square(a):
                    return a.rearrange("p (h w) -> p h w", w=C)

                gp.wait_ge(S("hats"), 4 * (k + 1))
                if k:
                    gp.wait_ge(S("term_m"), k)
                own(mul(square(tmp_p), square(hats[:, k % 2, 0]), im(IMG_MM)))
                own.sync()
                gp.wait_ge(S("mp"), k + 1)
                own(add(tmp_p, tmp_p, tmp_m[:, k % 2]))
                own.sync()
                own(add(square(tmp_p), square(tmp_p), im(IMG_YM)))
                own.sync()
                if k >= 2:
                    gp.wait_ge(S("tap"), k - 1)
                mul(term[:, k % 2, 1], hats[:, k % 2, 2], tmp_p).then_inc(S("term_m"), 1)

            gp.wait_ge(S("x1t"), 1)
            gp.memset(pexp, 0.0).then_inc(S("pexp_cleared"), 1)
            own(gp.memset(vz, 0.0))
            own.sync()
            for n in range(NH):
                last = gp.memset(vz[:, :, n, 1, HD * n:HD * n + HD], 1.0)
            last.then_inc(S("vz_cleared"), 1)

            gp.wait_ge(S("k_hi"), 1)
            gp.tensor_tensor(qk_full[:, 1], qk_full[:, 1], qk_part[:, 1, 0], ALU.subtract).then_inc(S("k_rest"), 1)

            gp.wait_ge(s_ld["mamba"], MAMBA_LOADS)
            own.sync()
            for j in range(2):
                r = slice(DI * j, DI * j + DI)
                for w in range(2):
                    gp.tensor_copy(w_xp[r, :, w, j, :], xp_raw[r, :, RANK + NS * w:RANK + NS * w + NS]).then_inc(S("w_xp"), 1)
                gp.wait_ge(S("w_xp"), 2 * (j + 1))
            for p in range(PAIRS):
                own(gp.tensor_copy(d_col[:, :, p:p + 1], par[:, :, KC + 2:KC + 3]))
                gp.tensor_copy(a_col[:, :, p, :], par[:, :, KC + 3:]).then_inc(S("a_log"), 1)
            gp.tensor_scalar(nycol[:], ycol[:], -1.0, None, ALU.mult).then_inc(S("nycol"), 1)
            gp.wait_ge(S("x2t"), 1)
            for v in (xs[:, :, 0:KC - 1], xs[:, :, KC - 1 + T:], xs_sliced[0][:, 0:KC - 1]):
                own(gp.memset(v, 0.0))
            gp.memset(xs_sliced[1][:, 0:KC - 1], 0.0).then_inc(S("xs_cleared"), 1)
            for k in range(KC):
                last = gp.tensor_scalar(w_diag[:, k], ident[:], par[:, 2, k:k + 1], None, ALU.mult)
            last.then_inc(S("w_diag"), 1)
            for p in range(PAIRS):
                gp.wait_ge(S("x_copied"), p + 1)
                gp.tensor_copy(xs_sliced[p][:, KC - 1:].rearrange("p (m s) -> p m s", s=SLICES),
                               xs[:, p, KC - 1:KC - 1 + T].rearrange("p (s m) -> p m s", s=SLICES)).then_inc(S("x_sliced"), 1)
            for t in range(DP):
                gp.wait_ge(S("round_e"), t + 1)
                gp.tensor_tensor(delta[:, t], delta[:, t], du[:, t], ALU.subtract).then_inc(S("relu_less"), 1)
            gp.wait_ge(S("relu_less"), DP)
            gp.wait_ge(S("delta"), 2)
            mul(du[:, 1], delta[:, 1], u[:, 0, 1]).then_inc(S("du_pool"), 1)
            gp.wait_ge(S("relu_less"), DP)
            with gp.Fori(0, DP) as t:
                for n in range(NS):
                    gp.wait_ge(S("scan"), above(t * NS + (n + 1)))
                    gp.wait_ge(S("c_copied"), above(t * NS + (n + 1)))
                    gp.wait_ge(S("y_acc"), above(t * NS + (n - RING + 1)))
                    gp.wait_ge(S("relu_less"), DP)
                    mul(hc_ring[n % RING], hs_ring[n % RING], c_ring[n % RING]).then_inc(S("hc"), 1)

            gp.wait_ge(S("scan"), above(DP * NS))
            gp.memset(w_conv[:], 0.0).then_inc(S("conv_cleared"), 1)
            gp.wait_ge(S("y_acc"), above(DP * NS))
            gp.memset(xpad, 0.0).then_inc(S("xpad_cleared"), 1)
            gp.wait_ge(S("y_read"), 4)
            gp.tensor_tensor(u[:, 0, 1], u[:, 0, 1], u[:, 1, 1, ::-1], ALU.add).then_inc(S("joined"), 1)
            gp.wait_ge(S("xrow"), 1)
            gp.wait_ge(s_ld["b4"], B4_LOADS)
            with gp.Fori(0, CPER) as j:
                for g in range(CGRP):
                    gp.wait_ge(S("rowmix"), above(j * NT + 2 * (g - 1)))
                    gp.wait_ge(S("xrow"), 1)
                    gp.tensor_tensor(xstat[:, g % 2],
                                     xrow[:, :, bass.ds(j + CPER * g, 1)].rearrange("p x a -> p a x").to_broadcast([P, B, C]),
                                     bmask[:].unsqueeze(2).to_broadcast([P, B, C]), ALU.mult).then_inc(S("stat"), 1)
    return nc


def constants():
    import numpy as np

    p = np.arange(P)
    quad, low = p // C, p % C
    same = quad[:, None] == quad[None, :]
    c = {
        "c_ident": np.eye(P, dtype=np.float32),
        "c_ones": (same / float(T)).astype(np.float32),
        "c_far": np.full((NH * 13, T), -BIG, np.float32),
        "c_ycol": low[:, None].astype(np.float32),
        "c_bmask": (quad[:, None] == np.arange(B)[None, :]).astype(np.float32),
        "c_grid": np.stack([np.arange(T) // C, np.arange(T) % C]).astype(np.float32),
    }
    sel_b = np.broadcast_to(np.eye(B, dtype=np.float32), (P, B, B))
    c["c_bsel"] = sel_b.astype(np.float32)
    tap = np.stack([np.arange(TAPS) // 3 - 1, np.arange(TAPS) % 3 - 1], 1).reshape(-1)
    c["c_tap"] = (tap[None, :] - low[:, None]).astype(np.float32)
    r = np.arange(96)
    batch, state = (r % 32) // NS, r % NS
    sel = (state[:, None, None] == np.arange(NS)[None, :, None]) & (batch[:, None, None] == (p // DI)[None, None, :])
    one = np.uint16(0x3F80)
    c["c_sel"] = sel.reshape(96, NS * P) * one
    q, rb, rg = r // 48, (r % 16) // CGRP, r % CGRP
    selc = ((rg[:, None, None, None] == np.arange(CGRP)[None, :, None, None])
            & (q[:, None, None, None] == np.arange(2)[None, None, :, None])
            & (rb[:, None, None, None] == quad[None, None, None, :]))
    c["c_selc"] = selc.reshape(96, CGRP * 2 * P) * one
    return c


def laid_out(i):
    import numpy as np

    a = {k: np.asarray(v) for k, v in i.items()}
    sfx = ("", "_b", "_s")
    cols = [np.stack([a["L2_conv_conv_w" + x] for x in sfx], 1)]
    for name in ("conv_b", "dt_proj_b", "D"):
        cols.append(np.stack([a["L2_conv_" + name + x] for x in sfx], 1)[:, :, None])
    cols.append(np.stack([a["L2_conv_A_log" + x] for x in sfx], 1))
    w, bias = a["L1_conv_w_qkv"], a["L1_conv_b_qkv"]
    turn = lambda v: np.swapaxes(v.reshape(v.shape[:-1] + (NH, HD)), -1, -2)
    w_attn = [turn(w[:, C * k:C * k + C]).reshape(C, C) for k in range(2)] + [w[:, 2 * C:]]
    b_attn = [np.broadcast_to(turn(bias[C * k:C * k + C])[None, :, None], (QH, HD, B // QH, NH)).reshape(P) for k in range(2)]
    b_attn += [np.tile(bias[2 * C:], B), np.tile(a["L1_conv_b_proj"], B)]
    m = {
        "x": a["x"].reshape(P, T),
        "woff": np.tile(a["L0_conv_w_off"].reshape(G, TAPS * 2, C).transpose(2, 1, 0).reshape(C, TAPS * 2 * G), (B, 1)),
        "boff_rows": np.tile(np.repeat(a["L0_conv_b_off"].reshape(G, TAPS * 2), CG, 0), (B, 1)),
        "boff": a["L0_conv_b_off"].reshape(G, TAPS * 2),
        "bchk": np.broadcast_to(a["L0_conv_b_off"].reshape(1, G, 3, 6).transpose(3, 0, 1, 2), (6, B, G, 3)).reshape(6 * B * G, 3),
        "wdef": a["L0_conv_w_def"].reshape(C, C, TAPS).transpose(1, 2, 0),
        "wqkv": np.concatenate(w_attn, 1), "battn": np.stack(b_attn, 1), "rpb": a["L1_conv_rpb"],
        "wproj": a["L1_conv_w_proj"],
        "win": a["L2_conv_in_proj_w"].T,
        "par": np.concatenate(cols, 2),
        "xproj": np.stack([a["L2_conv_x_proj_w" + x].T for x in sfx], 1),
        "xlow": np.stack([a["L2_conv_x_proj_w" + x][0:RANK] for x in sfx], 1),
        "dtw": np.stack([a["L2_conv_dt_proj_w" + x].T for x in sfx], 1),
        "wout": a["L2_conv_out_proj_w"].T,
        "wconv": a["L3_conv_W"].reshape(9, C, C, 2).transpose(1, 0, 3, 2),
        "bconv": a["L3_conv_b"].reshape(C, 2),
    }
    m.update(constants())
    return {k: np.ascontiguousarray(v) for k, v in m.items()}


def kernel(**inputs):
    import numpy as _np
    import concourse.bacc as _bacc
    from concourse import mybir as _mybir
    from concourse.bass_utils import run_bass_kernel_spmd as _run

    nc = _bacc.Bacc("TRN2", target_bir_lowering=False, num_devices=1)
    arrays, d = {}, {}
    for name, a in laid_out(inputs).items():
        arrays[f"in_{name}"] = a
        d[name] = nc.dram_tensor(f"in_{name}", a.shape, _mybir.dt.from_np(a.dtype), kind="ExternalInput").ap()
    out = nc.dram_tensor("out_0", (B, C, C, C), _mybir.dt.float32, kind="ExternalOutput").ap()
    build(nc, d, out)
    return _run(nc, [arrays], core_ids=[0]).results[0]["out_0"]
```
